# Optimizing a Trainium2 kernel written in Bass

```python
import numpy as np
import jax
import jax.numpy as jnp

def _softmax(x, axis=-1):
    return jax.nn.softmax(x, axis=axis)

def _gelu(x):
    return jax.nn.gelu(x, approximate=True)

def _silu(x):
    return jax.nn.silu(x)

def _sigmoid(x):
    return jax.nn.sigmoid(x)

def _layernorm(x, axis=-1, eps=1e-05):
    m = jnp.mean(x, axis=axis, keepdims=True)
    v = jnp.var(x, axis=axis, keepdims=True)
    return (x - m) / jnp.sqrt(v + eps)

def _scatter_add(tgt, idx, src, axis=0):
    return tgt.at[idx].add(src)

def _segment_sum(src, seg, n):
    return jax.ops.segment_sum(src, seg, n)
kernel_name = 'mk_xattn_ffn_d2_seqx_r4_552c55'

def setup_inputs(seed: int=0):
    np.random.seed(seed)
    _w = jnp.asarray

    def _rec_inputs():
        import jax
        import jax.numpy as jnp
        _rk = jax.random.key(seed)
        x = -0.0003929 + 0.9999 * jax.random.normal(jax.random.fold_in(_rk, 1), (4, 512, 256), jnp.float32)
        _lenS = 512 - jax.random.randint(jax.random.fold_in(_rk, 7), (4,), 0, max(1, 512 // 4) + 1, jnp.int32)
        _lenS2 = 1601 - jax.random.randint(jax.random.fold_in(_rk, 8), (4,), 0, max(1, 1601 // 4) + 1, jnp.int32)
        _ctx_1024P = jax.random.normal(jax.random.fold_in(_rk, 11), (4, 16, 256), jnp.float32)
        _ctx_1024c = jax.random.dirichlet(jax.random.fold_in(_rk, 511), 0.3 * jnp.ones((16,), jnp.float32), (4, 1601))
        _ctx_1024t = jnp.einsum('bsk,bkd->bsd', _ctx_1024c, _ctx_1024P)
        _ctx_1024t = _ctx_1024t * jax.lax.rsqrt(jnp.mean(jnp.square(_ctx_1024t)) + 1e-12) * 0.953939
        ctx_1024 = 2.81802e-05 + 1.00001 * (_ctx_1024t + 0.3 * jax.random.normal(jax.random.fold_in(_rk, 611), (4, 1601, 256), jnp.float32))
        _validS = jnp.arange(512)[None, :] < _lenS[:, None]
        _validS2 = jnp.arange(1601)[None, :] < _lenS2[:, None]
        _causal = jnp.tril(jnp.ones((512, 512), dtype=bool))
        mask_BxSxS2_bk1 = jnp.broadcast_to(_validS2[:, None, :], (4, 512, 1601))
        return (x, ctx_1024, mask_BxSxS2_bk1)
    x, ctx_1024, mask_BxSxS2_bk1 = _rec_inputs()

    def _L0_xattn_setup():
        import jax, jax.numpy as jnp
        import numpy as np
        B, S, H = (8, 512, 256)
        key = jax.random.key(seed)
        ks = jax.random.split(key, 12)
        s = 1.0 / np.sqrt(H)
        return {'_q': jax.random.normal(ks[0], (B, S, H), jnp.float32), '_kv': jax.random.normal(ks[1], (B, S, H), jnp.float32), 'W_kv': jax.random.normal(ks[2], (H, 2 * H), jnp.float32) * s, 'b_kv': jnp.zeros((2 * H,), jnp.float32), 'W_q': jax.random.normal(ks[3], (H, H), jnp.float32) * s, 'b_q': jnp.zeros((H,), jnp.float32), 'W1': jax.random.normal(ks[4], (H, 4 * H), jnp.float32) * s, 'b1': jnp.zeros((4 * H,), jnp.float32), 'W2': jax.random.normal(ks[5], (4 * H, H), jnp.float32) * (1.0 / np.sqrt(4 * H)), 'b2': jnp.zeros((H,), jnp.float32)}
    _L0_xattn_all = _L0_xattn_setup()
    _L0_xattn_in = {k: v for k, v in _L0_xattn_all.items() if k in ('W_kv', 'b_kv', 'W_q', 'b_q', 'W1', 'b1', 'W2', 'b2')}
    del _L0_xattn_all

    def _L0_ffn_setup():
        import jax, jax.numpy as jnp
        import numpy as np
        B, S, D = (2, 256, 256)
        E, K, I = (8, 2, 256)
        LIMIT = 7.0
        ALPHA = 1.702

        def _swiglu(t, limit):
            glu = jnp.minimum(t[..., ::2], limit)
            lin = jnp.clip(t[..., 1::2], -limit, limit)
            return glu * jax.nn.sigmoid(ALPHA * glu) * (lin + 1.0)
        key = jax.random.key(seed)
        k0, k1, k2, k3 = jax.random.split(key, 4)
        return {'x': jax.random.normal(k0, (B, S, D), jnp.float32), 'norm_w': jnp.ones((D,), jnp.float32), 'gate_w': jax.random.normal(k1, (E, D), jnp.float32) / np.sqrt(D).astype(np.float32), 'gate_b': jnp.zeros((E,), jnp.float32), 'mlp1_w': jax.random.normal(k2, (E, 2 * I, D), jnp.float32) / np.sqrt(D).astype(np.float32), 'mlp1_b': jnp.zeros((E, 2 * I), jnp.float32), 'mlp2_w': jax.random.normal(k3, (E, D, I), jnp.float32) / np.sqrt(I).astype(np.float32), 'mlp2_b': jnp.zeros((E, D), jnp.float32)}
    _L0_ffn_all = _L0_ffn_setup()
    _L0_ffn_in = {k: v for k, v in _L0_ffn_all.items() if k in ('norm_w', 'gate_w', 'gate_b', 'mlp1_w', 'mlp1_b', 'mlp2_w', 'mlp2_b')}
    del _L0_ffn_all

    def _L1_xattn_setup():
        import jax, jax.numpy as jnp
        import numpy as np
        DIM = 256
        HEADS = 16
        DIM_HEAD = 64
        INNER = HEADS * DIM_HEAD
        B, N = (2, 512)
        key = jax.random.key(seed)
        ks = jax.random.split(key, 8)
        q = jax.random.normal(ks[0], (B, N, DIM), dtype=jnp.float32)
        k = jax.random.normal(ks[1], (B, N, DIM), dtype=jnp.float32)
        v = jax.random.normal(ks[2], (B, N, DIM), dtype=jnp.float32)
        causal = jnp.triu(jnp.ones((N, N), dtype=jnp.bool_), k=1)
        mask = jnp.broadcast_to(causal, (B, N, N))
        s = 0.02
        Wq = jax.random.normal(ks[3], (DIM, INNER), dtype=jnp.float32) * s
        Wk = jax.random.normal(ks[4], (DIM, INNER), dtype=jnp.float32) * s
        Wv = jax.random.normal(ks[5], (DIM, INNER), dtype=jnp.float32) * s
        Wo = jax.random.normal(ks[6], (INNER, DIM), dtype=jnp.float32) * s
        bo = jnp.zeros((DIM,), dtype=jnp.float32)
        return {'q': q, 'k': k, 'v': v, 'mask': mask, 'Wq': Wq, 'Wk': Wk, 'Wv': Wv, 'Wo': Wo, 'bo': bo}
    _L1_xattn_all = _L1_xattn_setup()
    _L1_xattn_in = {k: v for k, v in _L1_xattn_all.items() if k in ('Wq', 'Wk', 'Wv', 'Wo', 'bo')}
    del _L1_xattn_all

    def _L1_ffn_setup():
        import jax, jax.numpy as jnp
        import numpy as np
        B, S, D = (4, 128, 256)
        E, K, H = (64, 8, 64)
        ES, HS = (2, 512)
        key = jax.random.key(seed)
        ks = jax.random.split(key, 8)
        scale = 0.02
        rn = lambda k, shape, s: jax.random.normal(k, shape, jnp.float32) * s
        return {'x': rn(ks[0], (B, S, D), 1.0), 'router_w': rn(ks[1], (D, E), scale), 'router_b': jnp.zeros((E,), jnp.float32), 'w1': rn(ks[2], (E, D, H), scale), 'b1': jnp.zeros((E, H), jnp.float32), 'w2': rn(ks[3], (E, H, D), scale), 'b2': jnp.zeros((E, D), jnp.float32), 'sw1': rn(ks[4], (ES, D, HS), scale), 'sb1': jnp.zeros((ES, HS), jnp.float32), 'sw2': rn(ks[5], (ES, HS, D), scale), 'sb2': jnp.zeros((ES, D), jnp.float32)}
    _L1_ffn_all = _L1_ffn_setup()
    _L1_ffn_in = {k: v for k, v in _L1_ffn_all.items() if k in ('router_w', 'router_b', 'w1', 'b1', 'w2', 'b2', 'sw1', 'sb1', 'sw2', 'sb2')}
    del _L1_ffn_all
    return {'x': x, 'ctx_1024': ctx_1024, 'mask_BxSxS2_bk1': mask_BxSxS2_bk1, 'L0_xattn_W_kv': _L0_xattn_in['W_kv'], 'L0_xattn_b_kv': _L0_xattn_in['b_kv'], 'L0_xattn_W_q': _L0_xattn_in['W_q'], 'L0_xattn_b_q': _L0_xattn_in['b_q'], 'L0_xattn_W1': _L0_xattn_in['W1'], 'L0_xattn_b1': _L0_xattn_in['b1'], 'L0_xattn_W2': _L0_xattn_in['W2'], 'L0_xattn_b2': _L0_xattn_in['b2'], 'L0_ffn_norm_w': _L0_ffn_in['norm_w'], 'L0_ffn_gate_w': _L0_ffn_in['gate_w'], 'L0_ffn_gate_b': _L0_ffn_in['gate_b'], 'L0_ffn_mlp1_w': _L0_ffn_in['mlp1_w'], 'L0_ffn_mlp1_b': _L0_ffn_in['mlp1_b'], 'L0_ffn_mlp2_w': _L0_ffn_in['mlp2_w'], 'L0_ffn_mlp2_b': _L0_ffn_in['mlp2_b'], 'L1_xattn_Wq': _L1_xattn_in['Wq'], 'L1_xattn_Wk': _L1_xattn_in['Wk'], 'L1_xattn_Wv': _L1_xattn_in['Wv'], 'L1_xattn_Wo': _L1_xattn_in['Wo'], 'L1_xattn_bo': _L1_xattn_in['bo'], 'L1_ffn_router_w': _L1_ffn_in['router_w'], 'L1_ffn_router_b': _L1_ffn_in['router_b'], 'L1_ffn_w1': _L1_ffn_in['w1'], 'L1_ffn_b1': _L1_ffn_in['b1'], 'L1_ffn_w2': _L1_ffn_in['w2'], 'L1_ffn_b2': _L1_ffn_in['b2'], 'L1_ffn_sw1': _L1_ffn_in['sw1'], 'L1_ffn_sb1': _L1_ffn_in['sb1'], 'L1_ffn_sw2': _L1_ffn_in['sw2'], 'L1_ffn_sb2': _L1_ffn_in['sb2']}

def reference(x, ctx_1024, mask_BxSxS2_bk1, L0_xattn_W_kv, L0_xattn_b_kv, L0_xattn_W_q, L0_xattn_b_q, L0_xattn_W1, L0_xattn_b1, L0_xattn_W2, L0_xattn_b2, L0_ffn_norm_w, L0_ffn_gate_w, L0_ffn_gate_b, L0_ffn_mlp1_w, L0_ffn_mlp1_b, L0_ffn_mlp2_w, L0_ffn_mlp2_b, L1_xattn_Wq, L1_xattn_Wk, L1_xattn_Wv, L1_xattn_Wo, L1_xattn_bo, L1_ffn_router_w, L1_ffn_router_b, L1_ffn_w1, L1_ffn_b1, L1_ffn_w2, L1_ffn_b2, L1_ffn_sw1, L1_ffn_sb1, L1_ffn_sw2, L1_ffn_sb2):
    import jax
    import jax.numpy as jnp

    def _L0_xattn_ref(_q, _kv, W_kv, b_kv, W_q, b_q, W1, b1, W2, b2):
        import jax, jax.numpy as jnp
        import numpy as np
        B, S, H = (8, 512, 256)
        kv = _kv @ W_kv + b_kv
        k, v = jnp.split(kv, 2, axis=-1)
        q = _q @ W_q + b_q
        scores = jnp.einsum('bqh,bkh->bqk', q, k)
        attn = jax.nn.softmax(scores, axis=-1)
        out = jnp.einsum('bqk,bkh->bqh', attn, v)
        hidden = jax.nn.gelu(out @ W1 + b1, approximate=False)
        return hidden @ W2 + b2

    def _L0_ffn_ref(x, norm_w, gate_w, gate_b, mlp1_w, mlp1_b, mlp2_w, mlp2_b):
        import jax, jax.numpy as jnp
        import numpy as np
        B, S, D = (2, 256, 256)
        E, K, I = (8, 2, 256)
        LIMIT = 7.0
        ALPHA = 1.702

        def _swiglu(t, limit):
            glu = jnp.minimum(t[..., ::2], limit)
            lin = jnp.clip(t[..., 1::2], -limit, limit)
            return glu * jax.nn.sigmoid(ALPHA * glu) * (lin + 1.0)
        eps = jnp.finfo(x.dtype).eps
        h = x * jax.lax.rsqrt(jnp.mean(x * x, axis=-1, keepdims=True) + eps) * norm_w
        flat = h.reshape(-1, D)
        logits = flat @ gate_w.T + gate_b
        vals, idx = jax.lax.top_k(logits, K)
        wts = jax.nn.softmax(vals, axis=-1)
        t1 = jnp.einsum('td,efd->tef', flat, mlp1_w) + mlp1_b
        act = _swiglu(t1, LIMIT)
        y = jnp.einsum('tei,edi->ted', act, mlp2_w) + mlp2_b
        sel = jnp.take_along_axis(y, idx[:, :, None], axis=1)
        out = jnp.sum(sel * wts[:, :, None], axis=1).reshape(x.shape)
        return x + out

    def _L1_xattn_ref(q, k, v, mask, Wq, Wk, Wv, Wo, bo):
        import jax, jax.numpy as jnp
        import numpy as np
        DIM = 256
        HEADS = 16
        DIM_HEAD = 64
        INNER = HEADS * DIM_HEAD
        B, N = (2, 512)
        h, d = (HEADS, DIM_HEAD)
        scale = d ** (-0.5)
        b, n, _ = q.shape

        def heads_split(x):
            return x.reshape(b, -1, h, d).transpose(0, 2, 1, 3)
        qh = heads_split(q @ Wq)
        kh = heads_split(k @ Wk)
        vh = heads_split(v @ Wv)
        dots = jnp.einsum('bhid,bhjd->bhij', qh, kh) * scale
        mask_value = -jnp.finfo(dots.dtype).max
        dots = jnp.where(mask[:, None, :, :], mask_value, dots)
        attn = jax.nn.softmax(dots, axis=-1)
        out = jnp.einsum('bhij,bhjd->bhid', attn, vh)
        out = out.transpose(0, 2, 1, 3).reshape(b, n, h * d)
        out = out @ Wo + bo
        return out

    def _L1_ffn_ref(x, router_w, router_b, w1, b1, w2, b2, sw1, sb1, sw2, sb2):
        import jax, jax.numpy as jnp
        import numpy as np
        B, S, D = (4, 128, 256)
        E, K, H = (64, 8, 64)
        ES, HS = (2, 512)
        b_, s_, d_ = x.shape
        xf = x.reshape(-1, d_)
        probs = jax.nn.softmax(xf @ router_w + router_b, axis=-1)
        tw, ti = jax.lax.top_k(probs, K)
        tw = tw / jnp.sum(tw, axis=-1, keepdims=True)

        def body(acc, p):
            W1, B1, W2, B2, e = p
            h = jax.nn.silu(xf @ W1 + B1) @ W2 + B2
            cw = jnp.sum(jnp.where(ti == e, tw, 0.0), axis=-1)
            return (acc + cw[:, None] * h, None)
        routed, _ = jax.lax.scan(body, jnp.zeros_like(xf), (w1, b1, w2, b2, jnp.arange(w1.shape[0])))

        def shared_mlp(W1, B1, W2, B2):
            return jax.nn.silu(xf @ W1 + B1) @ W2 + B2
        shared = jnp.sum(jax.vmap(shared_mlp)(sw1, sb1, sw2, sb2), axis=0)
        return (routed + shared).reshape(b_, s_, d_)
    x = x + _L0_xattn_ref(_layernorm(x, axis=-1), ctx_1024, L0_xattn_W_kv, L0_xattn_b_kv, L0_xattn_W_q, L0_xattn_b_q, L0_xattn_W1, L0_xattn_b1, L0_xattn_W2, L0_xattn_b2)
    x = x + _L0_ffn_ref(_layernorm(x, axis=-1), L0_ffn_norm_w, L0_ffn_gate_w, L0_ffn_gate_b, L0_ffn_mlp1_w, L0_ffn_mlp1_b, L0_ffn_mlp2_w, L0_ffn_mlp2_b)
    x = x + _L1_xattn_ref(_layernorm(x, axis=-1), ctx_1024, ctx_1024, mask_BxSxS2_bk1, L1_xattn_Wq, L1_xattn_Wk, L1_xattn_Wv, L1_xattn_Wo, L1_xattn_bo)
    x = x + _L1_ffn_ref(_layernorm(x, axis=-1), L1_ffn_router_w, L1_ffn_router_b, L1_ffn_w1, L1_ffn_b1, L1_ffn_w2, L1_ffn_b2, L1_ffn_sw1, L1_ffn_sb1, L1_ffn_sw2, L1_ffn_sb2)
    return x

_drawn_inputs = setup_inputs


def setup_inputs(seed=0):
    import zlib

    import numpy as np

    out = dict(_drawn_inputs(seed))
    spreads = {'L0_xattn_b_kv': (0.0, 0.1),
     'L0_xattn_b_q': (0.0, 0.1),
     'L0_xattn_b1': (0.0, 0.1),
     'L0_xattn_b2': (0.0, 0.1),
     'L0_ffn_norm_w': (1.0, 0.2),
     'L0_ffn_gate_b': (0.0, 0.1),
     'L0_ffn_mlp1_b': (0.0, 0.1),
     'L0_ffn_mlp2_b': (0.0, 0.1),
     'L1_xattn_bo': (0.0, 0.1),
     'L1_ffn_router_b': (0.0, 0.8),
     'L1_ffn_b1': (0.0, 0.8),
     'L1_ffn_b2': (0.0, 0.554),
     'L1_ffn_sb1': (0.0, 0.602),
     'L1_ffn_sb2': (0.0, 0.1)}
    factors = {'L1_xattn_Wq': 8.0,
     'L1_xattn_Wk': 8.0,
     'L1_ffn_router_w': 4.165,
     'L1_ffn_w1': 8.0,
     'L1_ffn_w2': 8.0}
    for name, (base, spread) in spreads.items():
        noise = np.random.default_rng([zlib.crc32(name.encode()), seed]).standard_normal(out[name].shape)
        drawn = base * np.exp(spread * noise) if base else spread * noise
        out[name] = jnp.asarray(drawn.astype(out[name].dtype))
    for name, factor in factors.items():
        out[name] = (out[name] * factor).astype(out[name].dtype)
    return out
```

```python
from contextlib import ExitStack

import concourse.bass as bass
from concourse import mybir

F32 = mybir.dt.float32
F32R = mybir.dt.float32r
U8 = mybir.dt.uint8
I32 = mybir.dt.int32
ACT = mybir.ActivationFunctionType
ALU = mybir.AluOpType
AX = mybir.AxisListType

P = 128
B, S, D = 4, 512, 256
S2 = 1601
KD = D // P
QT = S // P
NT = B * QT
S2P = S2 + 1
KT = -(-S2 // P)
KLAST = S2 - (KT - 1) * P
E0, I0 = 8, 256
E1, H1 = 64, 64
ES, HS = 2, 512
TOP1 = 8
G1 = E1 * H1 // 512
GS = ES * HS // 512
HEADS, DH = 16, 64
PAIRS = HEADS // 2
WIN = S2 // 4
W0 = S2 - WIN
LN_EPS = 1e-5
RMS_EPS = 1.1920928955078125e-07
BIG = 3.4028234663852886e38
LIMIT, ALPHA = 7.0, 1.702

COLS = {}
ROWS = {}


def _place(table, parts):
    at = 0
    for name, n in parts:
        table[name] = (at, n)
        at += n
    return at


NCOLS = _place(COLS, [("bq", KD), ("bk", KD), ("bv", KD), ("b1", 8), ("mlp1_b", 4 * E0), ("l1_b1", 4 * (G1 + GS)),
                      ("gate_b", 1), ("router_b", 1)])
NROWS = _place(ROWS, [("b2", D), ("norm_w", D), ("bo", D)])


def split_matmul(pe, out, w, x, first=True, last=True):
    pe.matmul(out, w[0], x[0], start=first, stop=False)
    pe.matmul(out, w[0], x[1], start=False, stop=False)
    return pe.matmul(out, w[1], x[0], start=False, stop=last)


def build_program(nc, x, ctxT, ctx, mask, cols, rows, l0_wq, l0_wkT, l0_wv, l0_w1, l0_w2, gate_wT,
                  mlp1, mlp2, mlp2_b, l1_wp, router_w, l1_w1, l1_w2, l1_b2, out):
    with ExitStack() as ctx_all:
        def sem(name):
            return ctx_all.enter_context(nc.semaphore(name))

        def keep(name, shape, dt=F32):
            return ctx_all.enter_context(nc.sbuf_tensor(name, shape, dt))

        def arena():
            stack = ExitStack()

            def sb(name, shape, dt=F32):
                return stack.enter_context(nc.sbuf_tensor(name, shape, dt))
            return stack, sb

        X = keep("X", [P, NT, D])
        ident = keep("ident", [P, P])
        halfneg = keep("halfneg", [P, QT])
        C = keep("C", [P, NCOLS])
        R = keep("R", [P, NROWS])
        ZT = [keep(f"ZT{h}", [P, KD, B * S], F32R) for h in range(2)]
        Z = keep("Z", [P, QT, D])
        HZ = keep("HZ", [P, QT, D])
        zz = keep("zz", [P, D])
        st = keep("st", [P, QT, 6])
        mv = keep("mv", [P, QT, 2])
        ve = keep("ve", [P, QT])
        rs = keep("rs", [P, QT])
        ms = keep("ms", [P, QT])
        ve2 = keep("ve2", [P, QT])
        rs2 = keep("rs2", [P, QT])
        flag = keep("flag", [P, 1], I32)
        fl_m = keep("fl_m", [P, QT, S2], U8)
        fl_a = keep("fl_a", [P, NT])
        fl_b = keep("fl_b", [P, NT])
        fl_s = keep("fl_s", [P, 2])
        PS = ctx_all.enter_context(nc.psum_tensor("PS", [P, 8, 512], F32))
        wscratch = nc.dram_tensor("wscratch", [(G1 + GS) * 8, B * S], F32).ap()

        def col(name, j):
            return C[:, COLS[name][0] + j:COLS[name][0] + j + 1]

        def row(name):
            return R[:, ROWS[name][0]:ROWS[name][0] + ROWS[name][1]]

        stA, sb = arena()
        a_raw = sb("a_raw", [P, 3, KD, D])
        a_w = [sb(f"a_w{h}", [P, 3, KD, D], F32R) for h in range(2)]
        a_bk = sb("a_bk", [P, KD, 2], F32R)
        a_cT = sb("a_cT", [P, KD, S2])
        a_c = [sb(f"a_c{h}", [P, KD, S2P], F32R) for h in range(2)]
        a_nat = sb("a_nat", [P, KT, D])
        a_q = [sb(f"a_q{h}", [P, KD, S], F32R) for h in range(2)]
        a_qp = [sb(f"a_qp{h}", [P, KD, S], F32R) for h in range(2)]
        a_p = [sb(f"a_p{i}", [P, S2]) for i in range(2)]
        a_pt = sb("a_pt", [P, KT, S])
        a_cs = sb("a_cs", [P, QT])
        a_mx = sb("a_mx", [P, QT])
        a_nm = sb("a_nm", [P, QT])
        a_nb = sb("a_nb", [P, QT])
        a_l = sb("a_l", [P, QT])
        a_rl = sb("a_rl", [P, QT])
        stA.close()
        a_u = a_q

        def ffn_memory(tag, KTH):
            return dict(
                w1r=sb(tag + "_w1r", [P, KD, 512]), w2r=sb(tag + "_w2r", [P, KTH, D]),
                w1=[[sb(f"{tag}_w1{h}{i}", [P, KD, 512], F32R) for h in range(2)] for i in range(2)],
                w2=[[sb(f"{tag}_w2{h}{i}", [P, KTH, D], F32R) for h in range(2)] for i in range(2)],
                hf=sb(tag + "_hf", [P, 4, 512]),
                h=[[sb(f"{tag}_h{h}{i}", [P, KTH, 512], F32R) for h in range(2)] for i in range(2)],
            )

        stM, sb = arena()
        memM = ffn_memory("m", 4)
        stM.close()
        stB, sb = arena()
        memB = ffn_memory("b", 2)
        b_gs = sb("b_gs", [P, 2, 512])
        b_c1 = sb("b_c1", [P, 4 * E0])
        b_gate_raw = sb("b_gate_raw", [P, KD, E0])
        b_gate = [sb(f"b_gate{h}", [P, KD, E0], F32R) for h in range(2)]
        b_lt = sb("b_lt", [E0, 512])
        b_lg = sb("b_lg", [P, QT, 16])
        b_mr = sb("b_mr", [P, QT, 16])
        b_top = sb("b_top", [P, QT, 8])
        b_in = sb("b_in", [P, QT, 8])
        b_d = sb("b_d", [P, QT, 2])
        b_w = sb("b_w", [P, QT, 2])
        b_s1 = sb("b_s1", [P, QT, E0])
        b_s2 = sb("b_s2", [P, QT, E0])
        b_wt = sb("b_wt", [P, NT, E0])
        b_wT = sb("b_wT", [E0, 512])
        b_b2 = sb("b_b2", [E0, D])
        stB.close()
        stD, sb = arena()
        memD = ffn_memory("d", 4)
        d_wb = [sb(f"d_wb{i}", [P, 4, 512]) for i in range(2)]
        d_rw_raw = sb("d_rw_raw", [P, KD, E1])
        d_rw = [sb(f"d_rw{h}", [P, KD, E1], F32R) for h in range(2)]
        d_lt = sb("d_lt", [E1, 512])
        d_lg = sb("d_lg", [P, QT, E1])
        d_pr = sb("d_pr", [P, QT, E1])
        d_mr = sb("d_mr", [P, QT, E1])
        d_top = sb("d_top", [P, QT, TOP1])
        d_nm = sb("d_nm", [P, QT])
        d_sm = sb("d_sm", [P, QT])
        d_rsm = sb("d_rsm", [P, QT])
        d_ts = sb("d_ts", [P, QT])
        d_rts = sb("d_rts", [P, QT])
        d_w = sb("d_w", [P, QT, E1])
        d_wT = sb("d_wT", [E1 + ES, 512])
        d_one = sb("d_one", [GS * 8, B * S])
        d_b2 = sb("d_b2", [E1 + ES, D])
        stD.close()

        def attn_memory(tag, nk, kt, sbufs):
            nkp = nk + nk % 2
            m = dict(nk=nk, nkp=nkp, kt=kt, sbufs=sbufs,
                     tag=tag, wr=sb(tag + "wr", [P, 3 * KD + 2, P]),
                     w=[sb(f"{tag}w{h}", [P, 3 * KD + 2, P], F32R) for h in range(2)],
                     q=[sb(f"{tag}q{h}", [P, S], F32R) for h in range(2)],
                     k=[sb(f"{tag}k{h}", [P, nkp], F32R) for h in range(2)],
                     v=sb(tag + "v", [P, len(kt), P]),
                     sm=[sb(f"{tag}sm{i}", [P, nk]) for i in range(2)],
                     pr=[sb(f"{tag}pr{i}", [P, nk]) for i in range(2 * sbufs)],
                     pt=sb(tag + "pt", [P, 2 if sbufs == 2 else 1, len(kt), S]),
                     u=[sb(f"{tag}u{h}", [P, S], F32R) for h in range(2)],
                     mn=sb(tag + "mn", [P, 8]), l=sb(tag + "l", [P, 8]), rl=sb(tag + "rl", [P, 8]))
            return m

        stC, sb = arena()
        c_mw = sb("c_mw", [P, NT, WIN])
        c_mu = sb("c_mu", [P, NT, WIN], U8)
        c_cr = sb("c_cr", [P, KD, WIN])
        c_c = [sb(f"c_c{h}", [P, B, KD, WIN], F32R) for h in range(2)]
        memF = attn_memory("f_", WIN, [(WIN // 4 * j, WIN // 4) for j in range(4)], 2)
        stC.close()
        stG, sb = arena()
        g_cr = sb("g_cr", [P, KD, S2])
        g_c = [sb(f"g_c{h}", [P, KD, S2P], F32R) for h in range(2)]
        g_mu = sb("g_mu", [P, QT, S2], U8)
        memG = attn_memory("g_", S2, [(P * j, min(P, S2 - P * j)) for j in range(KT)], 1)
        stG.close()
        const_in = sem("const_in")
        x_in = sem("x_in")
        ones_ready = sem("ones_ready")
        ident_ready = sem("ident_ready")
        x_done = [sem(f"x_done{i}") for i in range(5)]
        LN = {k: sem("ln_" + k) for k in ("stats", "moments", "ve", "rstd", "z", "turned", "hi", "lo", "ms", "ve2",
                                          "rstd2", "h", "zadd")}
        flag_in = sem("flag_in")
        flag_red = sem("flag_red")
        flag_sum = sem("flag_sum")
        flag_ready = sem("flag_ready")

        def wait_past(eng, s, value):
            if isinstance(value, int) and value <= 0:
                return
            eng.wait_ge(s, value)

        def each(eng, n, steps, peel=True):
            if peel:
                steps(0)
            with eng.Fori(1 if peel else 0, n) as i:
                steps(i)

        def settle(eng):
            eng.nop(nofuse=True)

        def ln_dve(dve, s, rms=False):
            L = LN
            def batch(b):
                for i in range(QT):
                    dve.bn_stats(st[:, i, :], X[:, b * QT + i, :]).then_inc(L["stats"], 1)
                dve.wait_ge(L["stats"], (s * B + b) * QT + QT)
                settle(dve)
                for i in range(QT):
                    dve.bn_aggr(mv[:, i, :], st[:, i, :]).then_inc(L["moments"], 1)
                dve.wait_ge(L["moments"], (s * B + b) * QT + QT)
                dve.tensor_scalar(ve[:, :], mv[:, :, 1], LN_EPS, None, ALU.add).then_inc(L["ve"], 1)
                dve.wait_ge(L["rstd"], (s * B + b) + 1)
                for i in range(QT):
                    if rms:
                        wait_past(dve, L["zadd"], b * QT)
                    else:
                        wait_past(dve, L["turned"], (s * B + b) * QT)
                    dve.tensor_scalar(Z[:, i, :], X[:, b * QT + i, :], mv[:, i, 0:1], rs[:, i:i + 1],
                                      ALU.subtract, ALU.mult).then_inc(L["z"], 1)
                if rms:
                    for i in range(QT):
                        dve.wait_ge(L["z"], (s * B + b) * QT + i + 1)
                        dve.tensor_tensor_reduce(zz[:, :], Z[:, i, :], Z[:, i, :], 1.0, 0.0, ALU.mult, ALU.add,
                                                 ms[:, i:i + 1]).then_inc(L["ms"], 1)
                        dve.wait_ge(L["ms"], b * QT + i + 1)
                    dve.tensor_scalar(ve2[:, :], ms[:, :], 1.0 / D, RMS_EPS, ALU.mult, ALU.add).then_inc(L["ve2"], 1)
                    dve.wait_ge(L["rstd2"], b + 1)
                    dve.wait_ge(L["turned"], (s * B + b) * QT)
                    for i in range(QT):
                        dve.scalar_tensor_tensor(HZ[:, i, :], Z[:, i, :], rs2[:, i:i + 1], row("norm_w"),
                                                 ALU.mult, ALU.mult).then_inc(L["h"], 1)
                for i in range(QT):
                    dve.wait_ge(L["hi"], (s * B + b) * QT + i + 1)
                    dve.tensor_tensor(ZT[1][:, :, bass.ds(b * S + i * P, P)],
                                      PS[:, 6 + i % 2, 0:KD * P].rearrange("p (k t) -> p k t", k=KD),
                                      ZT[0][:, :, bass.ds(b * S + i * P, P)].bitcast(F32),
                                      ALU.subtract).then_inc(L["lo"], 1)
            each(dve, B, batch)

        def ln_pool(pool, s, rms=False):
            L = LN
            def batch(b):
                pool.wait_ge(L["ve"], (s * B + b) + 1)
                pool.tensor_tensor(rs[:, :], ve[:, :], halfneg[:, :], ALU.pow).then_inc(L["rstd"], 1)
                if rms:
                    pool.wait_ge(L["ve2"], b + 1)
                    pool.tensor_tensor(rs2[:, :], ve2[:, :], halfneg[:, :], ALU.pow).then_inc(L["rstd2"], 1)
                    pool.wait_ge(L["h"], b * QT + QT)
                    for i in range(QT):
                        pool.tensor_tensor(X[:, b * QT + i, :], X[:, b * QT + i, :], Z[:, i, :],
                                           ALU.add).then_inc(L["zadd"], 1)
            each(pool, B, batch)

        def ln_pe(pe, s, rms=False):
            L = LN
            src = HZ if rms else Z
            def batch(b):
                for i in range(QT):
                    pe.wait_ge(L["h"] if rms else L["z"], (b if rms else s * B + b) * QT + i + 1)
                    if i >= 2:
                        pe.wait_ge(L["lo"], (s * B + b) * QT + i - 1)
                    else:
                        wait_past(pe, L["lo"], (s * B + b) * QT)
                    for k in range(KD):
                        last = pe.transpose(PS[:, 6 + i % 2, k * P:(k + 1) * P], src[:, i, k * P:(k + 1) * P],
                                            ident[:, :])
                    last.then_inc(L["turned"], 1)
            each(pe, B, batch)

        def ln_act(act, s):
            L = LN
            def batch(b):
                for i in range(QT):
                    act.wait_ge(L["turned"], (s * B + b) * QT + i + 1)
                    settle(act)
                    act.activation(ZT[0][:, :, bass.ds(b * S + i * P, P)],
                                   PS[:, 6 + i % 2, 0:KD * P].rearrange("p (k t) -> p k t", k=KD),
                                   ACT.Copy).then_inc(L["hi"], 1)
            each(act, B, batch)

        def wait_blocks(eng, s):
            eng.wait_ge(LN["lo"], NT * (s + 1))

        A = {k: sem("a_" + k) for k in (
            "w_in", "w_hi", "w_lo", "pad", "ctxT_in", "nat_in", "ctx_hi", "ctx_lo", "q", "q_hi", "q_lo", "qp", "qp_hi",
            "qp_lo", "csum", "s", "own", "nb", "exp", "rl", "norm", "t", "t_out_act", "t_out_dve", "u",
            "u_hi", "u_lo", "o", "o_hi", "o_lo")}
        TG = [(0, 4), (4, 4), (8, 4), (12, 1)]

        def a_sync(sp):
            for j, w in enumerate((l0_wq, l0_wkT, l0_wv)):
                sp.dma_start(a_raw[:, j, :, :], w.rearrange("(k p) n -> p k n", p=P)).then_inc(A["w_in"], 16)
            def batch(b):
                wait_past(sp, A["ctx_lo"], b)
                sp.dma_start(a_cT[:, :, :], ctxT[b].rearrange("(k p) s -> p k s", p=P)).then_inc(A["ctxT_in"], 16)
                wait_past(sp, flag_red, b * 2)
                settle(sp)
                sp.dma_start(fl_m[:, :, :], mask[b].rearrange("(i p) s -> p i s", p=P)).then_inc(flag_in, 16)
                wait_past(sp, A["u"], b * KD)
                sp.dma_start(a_nat[:, 0:KT - 1, :],
                             ctx[b, 0:(KT - 1) * P].rearrange("(t p) d -> p t d", p=P)).then_inc(A["nat_in"], 16)
                sp.dma_start(a_nat[0:KLAST, KT - 1, :], ctx[b, (KT - 1) * P:S2]).then_inc(A["nat_in"], 16)
            each(sp, B, batch)

        def a_pe(pe):
            wait_blocks(pe, 0)
            pe.wait_ge(A["w_lo"], 2)
            sflat = PS[:, 0:4, :].rearrange("p a c -> p (a c)")
            def batch(b):
                zb = [z[:, :, bass.ds(b * S, S)] for z in ZT]
                wait_past(pe, A["exp"], b * QT)
                for m in range(KD):
                    for k in range(KD):
                        last = split_matmul(pe, PS[:, m, :], [w[:, 0, k, m * P:(m + 1) * P] for w in a_w],
                                            [z[:, k, :] for z in zb], k == 0, k == KD - 1)
                    last.then_inc(A["q"], 1)
                pe.wait_ge(A["q_lo"], b * KD + KD)
                for m in range(KD):
                    for k in range(KD):
                        last = split_matmul(pe, PS[:, m, :], [w[:, 1, k, m * P:(m + 1) * P] for w in a_w],
                                            [q[:, k, :] for q in a_q], k == 0, k == KD - 1)
                    last.then_inc(A["qp"], 1)
                for i in range(QT):
                    for n, (k, h) in enumerate([(k, h) for k in range(KD) for h in range(2)]):
                        last = pe.matmul(PS[:, 2, 2 * i:2 * i + 2], a_q[h][:, k, i * P:(i + 1) * P], a_bk[:, k, :],
                                         start=n == 0, stop=n == 2 * KD - 1)
                last.then_inc(A["qp"], 1)
                pe.wait_ge(A["qp_lo"], b * KD + KD)
                pe.wait_ge(A["csum"], b + 1)
                pe.wait_ge(A["ctx_lo"], b + 1)

                def turn(i):
                    pe.wait_ge(A["norm"], b * QT + i + 1)
                    for g, (t0, nt) in enumerate(TG):
                        n = b * QT + i
                        if g >= 2:
                            pe.wait_ge(A["t_out_dve" if g % 2 == 0 else "t_out_act"], n * 2 + 1)
                        else:
                            wait_past(pe, A["t_out_dve" if g % 2 == 0 else "t_out_act"], n * 2)
                        for t in range(t0, t0 + nt):
                            w = P if t < KT - 1 else KLAST
                            last = pe.transpose(PS[0:w, 4 + g % 2, (t - t0) * P:(t - t0 + 1) * P],
                                                a_p[i % 2][:, t * P:t * P + w], ident[:, :])
                        last.then_inc(A["t"], 1)

                for i in range(QT):
                    if i:
                        pe.wait_ge(A["exp"], b * QT + i)
                    for c in range(4):
                        w = min(512, S2P - 512 * c)
                        for k in range(KD):
                            last = split_matmul(pe, sflat[:, 512 * c:512 * c + w],
                                                [q[:, k, i * P:(i + 1) * P] for q in a_qp],
                                                [a[:, k, 512 * c:512 * c + w] for a in a_c], k == 0, k == KD - 1)
                    last.then_inc(A["s"], 1)
                    if i:
                        turn(i - 1)
                turn(QT - 1)
                pe.wait_ge(A["t_out_dve"], b * QT * 2 + QT * 2)
                pe.wait_ge(A["t_out_act"], b * QT * 2 + QT * 2)
                pe.wait_ge(A["nat_in"], b * 32 + 32)
                wait_past(pe, A["o_lo"], b * KD)
                for m in range(KD):
                    for t in range(KT):
                        w = P if t < KT - 1 else KLAST
                        last = pe.matmul(PS[:, 6 + m, :], a_nat[0:w, t, m * P:(m + 1) * P], a_pt[0:w, t, :],
                                         start=t == 0, stop=t == KT - 1)
                    last.then_inc(A["u"], 1)
                pe.wait_ge(A["u_lo"], b * KD + KD)
                for m in range(KD):
                    for k in range(KD):
                        last = split_matmul(pe, PS[:, 6 + m, :], [w[:, 2, k, m * P:(m + 1) * P] for w in a_w],
                                            [u[:, k, :] for u in a_u], k == 0, k == KD - 1)
                    last.then_inc(A["o"], 1)
            each(pe, B, batch)


        def a_act(act):
            act.wait_ge(A["w_in"], 48)
            act.wait_ge(const_in, 32)
            act.activation(a_w[0][:, :, :, :], a_raw[:, :, :, :], ACT.Copy).then_inc(A["w_hi"], 1)
            act.activation(a_bk[:, :, 0], C[:, COLS["bk"][0]:COLS["bk"][0] + KD], ACT.Copy).then_inc(A["w_hi"], 1)
            def batch(b):
                act.wait_ge(A["ctxT_in"], b * 16 + 16)
                wait_past(act, A["s"], b * QT)
                act.activation(a_c[0][:, :, 0:S2], a_cT[:, :, :], ACT.Copy).then_inc(A["ctx_hi"], 1)
                for m in range(KD):
                    act.wait_ge(A["q"], b * KD + m + 1)
                    wait_past(act, A["o"], b * KD)
                    act.activation(a_q[0][:, m, :], PS[:, m, :], ACT.Identity, bias=col("bq", m)).then_inc(A["q_hi"], 1)
                for m in range(KD):
                    act.wait_ge(A["qp"], b * (KD + 1) + m + 1)
                    act.activation(a_qp[0][:, m, :], PS[:, m, :], ACT.Copy).then_inc(A["qp_hi"], 1)

                def turned(i):
                    for g in (1, 3):
                        t0, nt = TG[g]
                        w = P if t0 + nt < KT else KLAST
                        act.wait_ge(A["t"], (b * QT + i) * 4 + g + 1)
                        wait_past(act, A["u"], b * KD)
                        act.activation(a_pt[0:w, t0:t0 + nt, i * P:(i + 1) * P],
                                       PS[0:w, 5, 0:nt * P].rearrange("p (t q) -> p t q", t=nt),
                                       ACT.Copy).then_inc(A["t_out_act"], 1)

                for i in range(QT):
                    act.wait_ge(A["nb"], b * QT + i + 1)
                    if i >= 2:
                        act.wait_ge(A["t"], (b * QT + i - 1) * 4)
                    else:
                        wait_past(act, A["t"], b * QT * 4)
                    act.activation(a_p[i % 2][:, :], PS[:, 0:4, :].rearrange("p a c -> p (a c)")[:, 0:S2], ACT.Exp,
                                   bias=a_nb[:, i:i + 1], accum_out=a_l[:, i:i + 1]).then_inc(A["exp"], 1)
                    if i:
                        turned(i - 1)
                turned(QT - 1)
                for m in range(KD):
                    act.wait_ge(A["u"], b * KD + m + 1)
                    act.activation(a_u[0][:, m, :], PS[:, 6 + m, :], ACT.Copy).then_inc(A["u_hi"], 1)
                for m in range(KD):
                    act.wait_ge(A["o"], b * KD + m + 1)
                    settle(act)
                    act.activation(ZT[0][:, m, bass.ds(b * S, S)], PS[:, 6 + m, :], ACT.Identity,
                                   bias=col("bv", m)).then_inc(A["o_hi"], 1)
            each(act, B, batch)

        def a_pool(pool):
            pool.memset(a_c[0][:, :, S2:S2P].bitcast(F32), 0.0).then_inc(A["pad"], 1)
            pool.memset(a_c[1][:, :, S2:S2P].bitcast(F32), 0.0).then_inc(A["pad"], 1)
            def batch(b):
                for i in range(QT):
                    pool.wait_ge(A["rl"], b * QT + i + 1)
                    settle(pool)
                    pool.tensor_scalar(a_p[i % 2][:, :], a_p[i % 2][:, :], a_rl[:, i:i + 1], None,
                                       ALU.mult).then_inc(A["norm"], 1)
            each(pool, B, batch)

        def a_dve(dve):
            dve.wait_ge(A["pad"], 2)
            dve.wait_ge(A["w_hi"], 2)
            dve.tensor_tensor(a_w[1][:, :, :, :].rearrange("p a k n -> p (a k n)"),
                              a_raw[:, :, :, :].rearrange("p a k n -> p (a k n)"),
                              a_w[0][:, :, :, :].rearrange("p a k n -> p (a k n)").bitcast(F32),
                              ALU.subtract).then_inc(A["w_lo"], 1)
            dve.tensor_tensor(a_bk[:, :, 1], C[:, COLS["bk"][0]:COLS["bk"][0] + KD], a_bk[:, :, 0].bitcast(F32),
                              ALU.subtract).then_inc(A["w_lo"], 1)
            def batch(b):
                dve.wait_ge(A["ctx_hi"], b + 1)
                dve.tensor_tensor(a_c[1][:, :, 0:S2], a_cT[:, :, :], a_c[0][:, :, 0:S2].bitcast(F32),
                                  ALU.subtract).then_inc(A["ctx_lo"], 1)
                for m in range(KD):
                    dve.wait_ge(A["q_hi"], b * KD + m + 1)
                    dve.scalar_tensor_tensor(a_q[1][:, m, :], PS[:, m, :], col("bq", m), a_q[0][:, m, :].bitcast(F32),
                                             ALU.add, ALU.subtract).then_inc(A["q_lo"], 1)
                for m in range(KD):
                    dve.wait_ge(A["qp_hi"], b * KD + m + 1)
                    dve.tensor_tensor(a_qp[1][:, m, :], PS[:, m, :], a_qp[0][:, m, :].bitcast(F32),
                                      ALU.subtract).then_inc(A["qp_lo"], 1)
                dve.wait_ge(A["qp"], b * (KD + 1) + KD + 1)
                dve.tensor_reduce(a_cs[:, :], PS[:, 2, 0:2 * QT].rearrange("p (i h) -> p i h", h=2), AX.X,
                                  ALU.add).then_inc(A["csum"], 1)

                def turned(i):
                    for g in (0, 2):
                        t0, nt = TG[g]
                        dve.wait_ge(A["t"], (b * QT + i) * 4 + g + 1)
                        wait_past(dve, A["u"], b * KD)
                        dve.tensor_copy(a_pt[:, t0:t0 + nt, i * P:(i + 1) * P],
                                        PS[:, 4, 0:nt * P].rearrange("p (t q) -> p t q", t=nt)).then_inc(A["t_out_dve"], 1)

                for i in range(QT):
                    n = b * QT + i + 1
                    dve.wait_ge(A["s"], n)
                    dve.wait_ge(A["csum"], b + 1)
                    dve.tensor_reduce(a_mx[:, i:i + 1], PS[:, 0:4, :].rearrange("p a c -> p (a c)")[:, 0:S2], AX.X,
                                      ALU.max).then_inc(A["own"], 1)
                    dve.wait_ge(A["own"], 2 * n - 1)
                    dve.tensor_scalar(a_nm[:, i:i + 1], a_mx[:, i:i + 1], a_cs[:, i:i + 1], -1.0, ALU.add,
                                      ALU.mult).then_inc(A["own"], 1)
                    dve.wait_ge(A["own"], 2 * n)
                    dve.tensor_tensor(a_nb[:, i:i + 1], a_nm[:, i:i + 1], a_cs[:, i:i + 1], ALU.add).then_inc(A["nb"], 1)
                    if i:
                        turned(i - 1)
                    dve.wait_ge(A["exp"], n)
                    dve.reciprocal(a_rl[:, i:i + 1], a_l[:, i:i + 1]).then_inc(A["rl"], 1)
                turned(QT - 1)
                for m in range(KD):
                    dve.wait_ge(A["u_hi"], b * KD + m + 1)
                    dve.tensor_tensor(a_u[1][:, m, :], PS[:, 6 + m, :], a_u[0][:, m, :].bitcast(F32),
                                      ALU.subtract).then_inc(A["u_lo"], 1)
                for m in range(KD):
                    dve.wait_ge(A["o_hi"], b * KD + m + 1)
                    dve.scalar_tensor_tensor(ZT[1][:, m, bass.ds(b * S, S)], PS[:, 6 + m, :], col("bv", m),
                                             ZT[0][:, m, bass.ds(b * S, S)].bitcast(F32), ALU.add,
                                             ALU.subtract).then_inc(A["o_lo"], 1)
                dve.wait_ge(flag_in, b * 16 + 16)
                dve.tensor_reduce(fl_a[:, bass.ds(b * QT, QT)], fl_m[:, :, 0:W0], AX.X, ALU.min).then_inc(flag_red, 1)
                dve.tensor_reduce(fl_b[:, bass.ds(b * QT, QT)], fl_m[:, :, W0:S2], AX.X, ALU.min).then_inc(flag_red, 1)
            each(dve, B, batch)


        def ffn_sems(tag, *own):
            return {k: sem(tag + "_" + k) for k in ("w_in", "w1_hi", "w2_hi", "w_lo", "h", "h_hi", "h_lo", "y", *own)}

        def sweep(eng, G, unit, split):
            def groups(g0, last):
                for n in range(2 * B):
                    g = g0 + n // B
                    unit(g, n % B, g * B + n % B)
                    if n % B == SPLIT_AT and split and not (last and n // B == 1):
                        split(g + 1, (n // B + 1) % 2)
            if split:
                split(0, 0)
            groups(0, G == 2)
            if G > 4:
                with eng.Fori(1, G // 2 - 1) as j:
                    groups(j * 2, False)
            if G > 2:
                groups(G - 2, True)
        SPLIT_AT = 1

        def ffn_sync(sp, F, mem, G, w1, w2, wb=None):
            def unit(g, b, u):
                if b == 0:
                    wait_past(sp, F["w_lo"], g * 2)
                    sp.dma_start(mem["w1r"][:, :, :], w1[g].rearrange("(k p) n -> p k n", p=P)).then_inc(F["w_in"], 16)
                    sp.dma_start(mem["w2r"][:, :, :], w2[g].rearrange("(k p) n -> p k n", p=P)).then_inc(F["w_in"], 16)
                if wb:
                    wb(g, b, u)
            sweep(sp, G, unit, None)

        def ffn_pe(pe, F, mem, G, KTH, x_sem, x_incs, h_read):
            def hidden(g, b, u, wpar):
                if b == 0:
                    pe.wait_ge(F["w_lo"], g * 2 + 2)
                for m in range(4):
                    h_read(u, m)
                    for k in range(KD):
                        last = split_matmul(pe, PS[:, m, :], [w[:, k, m * P:(m + 1) * P] for w in mem["w1"][wpar]],
                                            [z[:, k, b * S:(b + 1) * S] for z in ZT], k == 0, k == KD - 1)
                    last.then_inc(F["h"], 1)

            def second(g, b, u, wpar):
                pe.wait_ge(F["h_lo"], u * KTH + KTH)
                wait_past(pe, x_sem, (u - 1) * x_incs)
                for i in range(QT):
                    for k in range(KTH):
                        last = split_matmul(pe, PS[:, 4 + 2 * (b % 2) + i // 2, (i % 2) * D:(i % 2 + 1) * D],
                                            [h[:, k, i * P:(i + 1) * P] for h in mem["h"][b % 2]],
                                            [w[:, k, :] for w in mem["w2"][wpar]], k == 0, k == KTH - 1)
                last.then_inc(F["y"], 1)

            def groups(g0, last):
                for n in range(2 * B):
                    if n + 1 < 2 * B or not last:
                        g, b = g0 + (n + 1) // B, (n + 1) % B
                        hidden(g, b, g * B + b, ((n + 1) // B) % 2)
                    g, b = g0 + n // B, n % B
                    second(g, b, g * B + b, n // B)
            hidden(0, 0, 0, 0)
            groups(0, G == 2)
            if G > 4:
                with pe.Fori(1, G // 2 - 1) as j:
                    groups(j * 2, False)
            if G > 2:
                groups(G - 2, True)

        def split_act(act, F, mem):
            def split(g, wpar):
                act.wait_ge(F["w_in"], g * 32 + 32)
                wait_past(act, F["y"], (g - 1) * B)
                act.activation(mem["w1"][wpar][0][:, :, :], mem["w1r"][:, :, :], ACT.Copy).then_inc(F["w1_hi"], 1)
            return split

        def split_pool(pool, F, mem):
            def split(g, wpar):
                pool.wait_ge(F["w_in"], g * 32 + 32)
                wait_past(pool, F["y"], (g - 1) * B)
                settle(pool)
                pool.tensor_copy(mem["w2"][wpar][0][:, :, :], mem["w2r"][:, :, :]).then_inc(F["w2_hi"], 1)
            return split

        def split_dve(dve, F, mem):
            def split(g, wpar):
                dve.wait_ge(F["w1_hi"], g + 1)
                dve.tensor_tensor(mem["w1"][wpar][1][:, :, :], mem["w1r"][:, :, :],
                                  mem["w1"][wpar][0][:, :, :].bitcast(F32), ALU.subtract).then_inc(F["w_lo"], 1)
                dve.wait_ge(F["w2_hi"], g + 1)
                dve.tensor_tensor(mem["w2"][wpar][1][:, :, :], mem["w2r"][:, :, :],
                                  mem["w2"][wpar][0][:, :, :].bitcast(F32), ALU.subtract).then_inc(F["w_lo"], 1)
            return split

        def high_hidden(eng, F, mem, u, b, m, KTH, ready):
            eng.wait_ge(ready, u * KTH + m + 1)
            wait_past(eng, F["y"], u - 1)
            settle(eng)
            if eng is nc.scalar:
                i = eng.activation(mem["h"][b % 2][0][:, m, :], mem["hf"][:, m, :], ACT.Copy)
            else:
                i = eng.tensor_copy(mem["h"][b % 2][0][:, m, :], mem["hf"][:, m, :])
            i.then_inc(F["h_hi"], 1)

        def low_hidden(dve, F, mem, u, b, m, KTH):
            dve.wait_ge(F["h_hi"], u * KTH + m + 1)
            dve.tensor_tensor(mem["h"][b % 2][1][:, m, :], mem["hf"][:, m, :],
                              mem["h"][b % 2][0][:, m, :].bitcast(F32), ALU.subtract).then_inc(F["h_lo"], 1)

        def accumulate(dve, F, u, b, x_sem):
            dve.wait_ge(F["y"], u + 1)
            for h in range(2):
                xs = X[:, b * QT + 2 * h:b * QT + 2 * h + 2, :]
                dve.tensor_tensor(xs, PS[:, 4 + 2 * (b % 2) + h, :].rearrange("p (t d) -> p t d", t=2), xs,
                                  ALU.add).then_inc(x_sem, 1)

        M = ffn_sems("m", "act")
        bias_added = sem("m_bias_added")

        def m_act(act):
            def unit(g, b, u):
                for m in range(4):
                    act.wait_ge(M["h"], u * 4 + m + 1)
                    wait_past(act, M["h_lo"], (u - 1) * 4 + m + 1)
                    act.activation(memM["hf"][:, m, :], PS[:, m, :], ACT.Gelu, bias=col("b1", g * 4 + m)
                                   ).then_inc(M["act"], 1)
            sweep(act, 2, unit, split_act(act, M, memM))

        def m_pool(pool):
            pool.wait_ge(LN["z"], NT)
            for b in range(B):
                pool.tensor_tensor(X[:, b * QT:(b + 1) * QT, :], X[:, b * QT:(b + 1) * QT, :],
                                   row("b2").unsqueeze(1).to_broadcast([P, QT, D]), ALU.add).then_inc(bias_added, 1)

            def unit(g, b, u):
                for m in range(4):
                    high_hidden(pool, M, memM, u, b, m, 4, M["act"])
            sweep(pool, 2, unit, split_pool(pool, M, memM))

        def m_dve(dve):
            dve.wait_ge(bias_added, B)

            def unit(g, b, u):
                for m in range(4):
                    low_hidden(dve, M, memM, u, b, m, 4)
                if u > 0:
                    accumulate(dve, M, u - 1, (b - 1) % B, x_done[0])
            sweep(dve, 2, unit, split_dve(dve, M, memM))
            accumulate(dve, M, 2 * B - 1, B - 1, x_done[0])

        BM = ffn_sems("b", "glu", "lin", "sig", "gated", "mul")
        BR = {k: sem("br_" + k) for k in ("w_in", "w_hi", "w_lo", "set", "lt", "lt_out", "lg", "own", "neg",
                                           "sig", "w", "keep", "wt", "wt_out", "yb", "x")}

        def b_sync(sp):
            sp.dma_start(b_gate_raw[:, :, :], gate_wT.rearrange("(k p) e -> p k e", p=P)).then_inc(BR["w_in"], 16)
            sp.dma_start(b_b2[:, :], mlp2_b).then_inc(BR["w_in"], 16)
            ffn_sync(sp, BM, memB, E0, mlp1, mlp2)

        def b_route_pe(pe):
            wait_blocks(pe, 1)
            pe.wait_ge(BR["w_lo"], 1)
            pe.wait_ge(BR["w_in"], 32)
            def batch(b):
                for k in range(KD):
                    last = split_matmul(pe, PS[0:E0, 0, :], [w[:, k, :] for w in b_gate],
                                        [z[:, k, bass.ds(b * S, S)] for z in ZT], k == 0, k == KD - 1)
                last.then_inc(BR["lt"], 1)
                pe.wait_ge(BR["lt_out"], b + 1)
                settle(pe)
                for i in range(QT):
                    last = pe.transpose(PS[:, 1, i * E0:(i + 1) * E0], b_lt[:, i * P:(i + 1) * P], ident[0:E0, 0:E0])
                last.then_inc(BR["lg"], 1)
                pe.wait_ge(BR["w"], b + 1)
                for i in range(QT):
                    last = pe.transpose(PS[0:E0, 2, i * P:(i + 1) * P], b_s2[:, i, :], ident[:, :])
                last.then_inc(BR["wt"], 1)
                pe.wait_ge(BR["wt_out"], b + 1)
                wait_past(pe, BR["x"], b * 2)
                for i in range(QT):
                    last = pe.matmul(PS[:, 3 + i // 2, (i % 2) * D:(i % 2 + 1) * D], b_wT[:, i * P:(i + 1) * P],
                                     b_b2[:, :], start=True, stop=True)
                last.then_inc(BR["yb"], 1)
            each(pe, B, batch)
            pe.wait_ge(BR["x"], B * 2)

        def b_route_act(act):
            act.wait_ge(BR["w_in"], 32)
            act.activation(b_gate[0][:, :, :], b_gate_raw[:, :, :], ACT.Copy).then_inc(BR["w_hi"], 1)
            def batch(b):
                act.wait_ge(BR["lt"], b + 1)
                wait_past(act, BR["lg"], b)
                act.activation(b_lt[:, :], PS[0:E0, 0, :], ACT.Identity,
                               bias=col("gate_b", 0)[0:E0]).then_inc(BR["lt_out"], 1)
                act.wait_ge(BR["neg"], b + 1)
                wait_past(act, BR["w"], b)
                for i in range(QT):
                    act.activation(b_s1[:, i, :], b_lg[:, i, 0:E0], ACT.Sigmoid, bias=b_d[:, i, 0:1],
                                   scale=2.0).then_inc(BR["sig"], 1)
            each(act, B, batch)

        def b_route_pool(pool):
            pool.memset(b_lg[:, :, :], -BIG).then_inc(BR["set"], 1)
            pool.memset(b_in[:, :, :], -BIG).then_inc(BR["set"], 1)

        def b_route_dve(dve):
            dve.wait_ge(BR["w_hi"], 1)
            dve.tensor_tensor(b_gate[1][:, :, :], b_gate_raw[:, :, :], b_gate[0][:, :, :].bitcast(F32),
                              ALU.subtract).then_inc(BR["w_lo"], 1)
            dve.tensor_scalar(b_c1[:, :], C[:, COLS["mlp1_b"][0]:COLS["mlp1_b"][0] + 4 * E0], 1.0, None,
                              ALU.add).then_inc(BR["keep"], 1)
            dve.wait_ge(BR["set"], 2)
            def batch(b):
                dve.wait_ge(BR["lg"], b + 1)
                wait_past(dve, BR["sig"], b * QT)
                dve.tensor_copy(b_lg[:, :, 0:E0],
                                PS[:, 1, 0:QT * E0].rearrange("p (i e) -> p i e", e=E0)).then_inc(BR["own"], 1)
                dve.wait_ge(BR["own"], b * 10 + 1)
                settle(dve)
                for i in range(QT):
                    dve.max(b_top[:, i, :], b_lg[:, i, 0:E0]).then_inc(BR["own"], 1)
                dve.wait_ge(BR["own"], b * 10 + 5)
                dve.tensor_copy(b_in[:, :, 0:2], b_top[:, :, 0:2]).then_inc(BR["own"], 1)
                dve.scalar_tensor_tensor(b_d[:, :, 0], b_top[:, :, 0], -1.0, b_top[:, :, 1], ALU.mult,
                                         ALU.subtract).then_inc(BR["neg"], 1)
                dve.wait_ge(BR["own"], b * 10 + 6)
                settle(dve)
                for i in range(QT):
                    dve.match_replace(b_mr[:, i, :], b_in[:, i, :], b_lg[:, i, :], BIG).then_inc(BR["own"], 1)
                dve.wait_ge(BR["own"], b * 10 + 10)
                dve.wait_ge(BR["sig"], b * QT + QT)
                wait_past(dve, BR["wt"], b)
                dve.scalar_tensor_tensor(b_s2[:, :, :], b_mr[:, :, 0:E0], BIG, b_s1[:, :, :], ALU.is_equal,
                                         ALU.mult).then_inc(BR["w"], 1)
                dve.wait_ge(BR["w"], b + 1)
                dve.tensor_copy(b_wt[:, bass.ds(b * QT, QT), :], b_s2[:, :, :]).then_inc(BR["keep"], 1)
                dve.wait_ge(BR["wt"], b + 1)
                wait_past(dve, BR["yb"], b)
                dve.tensor_copy(b_wT[:, :], PS[0:E0, 2, :]).then_inc(BR["wt_out"], 1)
                dve.wait_ge(BR["yb"], b + 1)
                dve.wait_ge(LN["zadd"], NT)
                for h in range(2):
                    xs = X[:, bass.ds(b * QT + 2 * h, 2), :]
                    dve.tensor_tensor(xs, PS[:, 3 + h, :].rearrange("p (t d) -> p t d", t=2), xs,
                                      ALU.add).then_inc(BR["x"], 1)
            each(dve, B, batch)

        def b_act(act):
            def unit(g, b, u):
                for j in range(2):
                    act.wait_ge(BM["glu"], u * 2 + j + 1)
                    wait_past(act, BM["mul"], (u - 1) * 2 + j + 1)
                    act.activation(b_gs[:, j, :], memB["hf"][:, j, :], ACT.Sigmoid, scale=ALPHA).then_inc(BM["sig"], 1)
                for j in range(2):
                    high_hidden(act, BM, memB, u, b, j, 2, BM["mul"])
            sweep(act, E0, unit, split_act(act, BM, memB))

        def b_pool(pool):
            def unit(g, b, u):
                for j in range(2):
                    pool.wait_ge(BM["sig"], u * 2 + j + 1)
                    pool.tensor_tensor(b_gs[:, j, :], b_gs[:, j, :], memB["hf"][:, j, :], ALU.mult).then_inc(BM["gated"], 1)
            sweep(pool, E0, unit, split_pool(pool, BM, memB))

        def b_accumulate(dve, g, u, b):
            dve.wait_ge(BM["y"], u + 1)
            for i in range(QT):
                t = b * QT + i
                dve.scalar_tensor_tensor(X[:, t, :], PS[:, 4 + 2 * (b % 2) + i // 2, (i % 2) * D:(i % 2 + 1) * D],
                                         b_wt[:, t, bass.ds(g, 1)], X[:, t, :], ALU.mult, ALU.add
                                         ).then_inc(x_done[1], 1)

        def b_dve(dve):
            dve.wait_ge(BR["x"], B * 2)
            dve.wait_ge(BR["keep"], B + 1)
            b1 = COLS["mlp1_b"][0]

            def unit(g, b, u):
                for j in range(2):
                    dve.wait_ge(BM["h"], u * 4 + j + 1)
                    wait_past(dve, BM["h_lo"], (u - 1) * 2 + j + 1)
                    dve.tensor_scalar(memB["hf"][:, j, :], PS[:, j, :], C[:, bass.ds(b1 + g * 4 + j, 1)], LIMIT,
                                      ALU.add, ALU.min).then_inc(BM["glu"], 1)
                for j in range(2):
                    dve.wait_ge(BM["h"], u * 4 + 2 + j + 1)
                    dve.tensor_scalar(memB["hf"][:, 2 + j, :], PS[:, 2 + j, :], b_c1[:, bass.ds(g * 4 + 2 + j, 1)],
                                      LIMIT + 1.0, ALU.add, ALU.min).then_inc(BM["lin"], 1)
                for j in range(2):
                    dve.wait_ge(BM["lin"], u * 2 + j + 1)
                    dve.wait_ge(BM["gated"], u * 2 + j + 1)
                    dve.scalar_tensor_tensor(memB["hf"][:, j, :], memB["hf"][:, 2 + j, :], 1.0 - LIMIT, b_gs[:, j, :],
                                             ALU.max, ALU.mult).then_inc(BM["mul"], 1)
                for j in range(2):
                    low_hidden(dve, BM, memB, u, b, j, 2)
                if not (isinstance(u, int) and u == 0):
                    b_accumulate(dve, (g - 1) if b == 0 else g, u - 1, (b - 1) % B)
            sweep(dve, E0, unit, split_dve(dve, BM, memB))
            b_accumulate(dve, E0 - 1, E0 * B - 1, B - 1)

        DM = ffn_sems("d", "act", "mul", "wb_in0", "wb_in1")
        DR = {k: BR[k] for k in ("w_in", "w_hi", "w_lo", "lt", "lt_out", "lg", "wt", "wt_out", "yb", "x")}
        DR |= {k: sem("dr_" + k) for k in ("one", "max", "exp", "own", "sel", "w", "stored", "one_stored")}
        NE = (G1 + GS) * 8

        def d_sync(sp):
            sp.dma_start(d_rw_raw[:, :, :], router_w.rearrange("(k p) e -> p k e", p=P)).then_inc(DR["w_in"], 16)
            sp.dma_start(d_b2[:, :], l1_b2).then_inc(DR["w_in"], 16)
            sp.wait_ge(DR["one"], 2)
            sp.dma_start(wscratch[E1:NE, :], d_one[:, :]).then_inc(DR["one_stored"], 16)
            def batch(b):
                sp.wait_ge(DR["wt_out"], (B + b) + 1)
                sp.dma_start(wscratch[0:E1, bass.ds(b * S, S)], d_wT[0:E1, :]).then_inc(DR["stored"], 16)
            each(sp, B, batch)
            sp.wait_ge(DR["one_stored"], 16)
            sp.wait_ge(DR["stored"], 16 * B)

            def wb(g, b, u):
                wait_past(sp, DM["mul"], (u - 1) * 4)
                for s in range(2):
                    src = wscratch[bass.ds(g * 8, 8), b * S:(b + 1) * S].rearrange("(m s) t -> s m t", s=2)[s]
                    sp.dma_start(d_wb[b % 2][s * H1:(s + 1) * H1, :, :],
                                 src.unsqueeze(0).to_broadcast([H1, 4, S])).then_inc(DM[f"wb_in{b % 2}"], 16)
            ffn_sync(sp, DM, memD, G1 + GS, l1_w1, l1_w2, wb)

        def d_route_pe(pe):
            wait_blocks(pe, 3)
            pe.wait_ge(DR["w_lo"], 2)
            pe.wait_ge(DR["w_in"], 64)
            pe.wait_ge(DR["one"], 2)
            def batch(b):
                for k in range(KD):
                    last = split_matmul(pe, PS[0:E1, 0, :], [w[:, k, :] for w in d_rw],
                                        [z[:, k, bass.ds(b * S, S)] for z in ZT], k == 0, k == KD - 1)
                last.then_inc(DR["lt"], 1)
                pe.wait_ge(DR["lt_out"], (B + b) + 1)
                settle(pe)
                for i in range(QT):
                    last = pe.transpose(PS[:, 1, i * E1:(i + 1) * E1], d_lt[:, i * P:(i + 1) * P], ident[0:E1, 0:E1])
                last.then_inc(DR["lg"], 1)
                pe.wait_ge(DR["w"], b * QT + QT)
                settle(pe)
                for i in range(QT):
                    last = pe.transpose(PS[0:E1, 2, i * P:(i + 1) * P], d_w[:, i, :], ident[:, :])
                last.then_inc(DR["wt"], 1)
                pe.wait_ge(DR["wt_out"], (B + b) + 1)
                pe.wait_ge(DR["x"], (B + b) * 2)
                for i in range(QT):
                    last = pe.matmul(PS[:, 3 + i // 2, (i % 2) * D:(i % 2 + 1) * D], d_wT[:, i * P:(i + 1) * P],
                                     d_b2[:, :], start=True, stop=True)
                last.then_inc(DR["yb"], 1)
            each(pe, B, batch)
            pe.wait_ge(DR["x"], B * 4)

        def d_route_act(act):
            act.wait_ge(DR["w_in"], 64)
            act.activation(d_rw[0][:, :, :], d_rw_raw[:, :, :], ACT.Copy).then_inc(DR["w_hi"], 1)
            def batch(b):
                act.wait_ge(DR["lt"], (B + b) + 1)
                act.wait_ge(DR["lg"], (B + b))
                act.activation(d_lt[:, :], PS[0:E1, 0, :], ACT.Identity,
                               bias=col("router_b", 0)[0:E1]).then_inc(DR["lt_out"], 1)
                act.wait_ge(DR["max"], b + 1)
                for i in range(QT):
                    wait_past(act, DR["sel"], b)
                    act.activation(d_pr[:, i, :], PS[:, 1, i * E1:(i + 1) * E1], ACT.Exp, bias=d_nm[:, i:i + 1],
                                   accum_out=d_sm[:, i:i + 1]).then_inc(DR["exp"], 1)
            each(act, B, batch)

        def d_route_pool(pool):
            pool.memset(d_one[:, :], 1.0).then_inc(DR["one"], 1)
            pool.memset(d_wT[E1:E1 + ES, :], 1.0).then_inc(DR["one"], 1)
            pool.wait_ge(DR["one"], 2)

        def d_route_dve(dve):
            dve.wait_ge(DR["w_hi"], 2)
            dve.tensor_tensor(d_rw[1][:, :, :], d_rw_raw[:, :, :], d_rw[0][:, :, :].bitcast(F32),
                              ALU.subtract).then_inc(DR["w_lo"], 1)
            def batch(b):
                dve.wait_ge(DR["lg"], (B + b) + 1)
                dve.tensor_reduce(d_nm[:, :], PS[:, 1, 0:QT * E1].rearrange("p (i e) -> p i e", e=E1), AX.X, ALU.max,
                                  negate=True).then_inc(DR["max"], 1)
                dve.wait_ge(DR["exp"], b * QT + QT)
                dve.reciprocal(d_rsm[:, :], d_sm[:, :]).then_inc(DR["own"], 1)
                dve.wait_ge(DR["own"], b * 15 + 1)
                for i in range(QT):
                    dve.tensor_scalar(d_pr[:, i, :], d_pr[:, i, :], d_rsm[:, i:i + 1], None,
                                      ALU.mult).then_inc(DR["own"], 1)
                dve.wait_ge(DR["own"], b * 15 + 5)
                settle(dve)
                for i in range(QT):
                    dve.max(d_top[:, i, :], d_pr[:, i, :]).then_inc(DR["own"], 1)
                dve.wait_ge(DR["own"], b * 15 + 9)
                dve.tensor_reduce(d_ts[:, :], d_top[:, :, :], AX.X, ALU.add).then_inc(DR["own"], 1)
                for i in range(QT):
                    dve.match_replace(d_mr[:, i, :], d_top[:, i, :], d_pr[:, i, :], -1.0).then_inc(DR["own"], 1)
                dve.wait_ge(DR["own"], b * 15 + 10)
                dve.reciprocal(d_rts[:, :], d_ts[:, :]).then_inc(DR["own"], 1)
                dve.wait_ge(DR["own"], b * 15 + 14)
                dve.wait_ge(DR["wt"], (B + b))
                dve.scalar_tensor_tensor(d_w[:, :, :], d_mr[:, :, :], -1.0, d_pr[:, :, :], ALU.is_equal,
                                         ALU.mult).then_inc(DR["sel"], 1)
                dve.wait_ge(DR["sel"], b + 1)
                dve.wait_ge(DR["own"], b * 15 + 15)
                for i in range(QT):
                    dve.tensor_scalar(d_w[:, i, :], d_w[:, i, :], d_rts[:, i:i + 1], None, ALU.mult).then_inc(DR["w"], 1)
                dve.wait_ge(DR["wt"], (B + b) + 1)
                dve.wait_ge(DR["yb"], (B + b))
                wait_past(dve, DR["stored"], b * 16)
                dve.tensor_copy(d_wT[0:E1, :], PS[0:E1, 2, :]).then_inc(DR["wt_out"], 1)
                dve.wait_ge(DR["yb"], (B + b) + 1)
                for h in range(2):
                    xs = X[:, bass.ds(b * QT + 2 * h, 2), :]
                    dve.tensor_tensor(xs, PS[:, 3 + h, :].rearrange("p (t d) -> p t d", t=2), xs,
                                      ALU.add).then_inc(DR["x"], 1)
            each(dve, B, batch)

        def d_act(act):
            b1 = COLS["l1_b1"][0]

            def unit(g, b, u):
                for m in range(4):
                    act.wait_ge(DM["h"], u * 4 + m + 1)
                    wait_past(act, DM["h_lo"], (u - 1) * 4 + m + 1)
                    settle(act)
                    act.activation(memD["hf"][:, m, :], PS[:, m, :], ACT.Silu, bias=C[:, bass.ds(b1 + g * 4 + m, 1)]
                                   ).then_inc(DM["act"], 1)
            sweep(act, G1 + GS, unit, split_act(act, DM, memD))

        def d_pool(pool):
            def unit(g, b, u):
                for m in range(4):
                    high_hidden(pool, DM, memD, u, b, m, 4, DM["mul"])
            sweep(pool, G1 + GS, unit, split_pool(pool, DM, memD))

        def d_dve(dve):
            dve.wait_ge(DR["x"], B * 4)

            def unit(g, b, u):
                dve.wait_ge(DM[f"wb_in{b % 2}"], (u // 2) * 32 + 32 if isinstance(u, int) else (g * 2 + b // 2) * 32 + 32)
                for m in range(4):
                    dve.wait_ge(DM["act"], u * 4 + m + 1)
                    dve.tensor_tensor(memD["hf"][:, m, :], memD["hf"][:, m, :], d_wb[b % 2][:, m, :],
                                      ALU.mult).then_inc(DM["mul"], 1)
                for m in range(4):
                    low_hidden(dve, DM, memD, u, b, m, 4)
                if not (isinstance(u, int) and u == 0):
                    accumulate(dve, DM, u - 1, (b - 1) % B, x_done[3])
            sweep(dve, G1 + GS, unit, split_dve(dve, DM, memD))
            accumulate(dve, DM, (G1 + GS) * B - 1, B - 1, x_done[3])

        def attn_sems(tag):
            return {k: sem("c" + tag + k) for k in (
                "w_in", "w_hi", "w_lo", "q", "q_hi", "q_lo", "k", "k_hi", "k_lo", "v", "v_out", "s", "min", "exp", "rl",
                "norm", "t", "t_out_act", "t_out_dve", "u", "u_hi", "u_lo", "y", "x", "ctx_in", "ctx_hi", "ctx_lo",
                "mask_in", "mask", "pad")}

        CF = CG = attn_sems("_")
        bo_added = sem("c_bo_added")
        attn_done = sem("attn_done")
        WQ, WK, WV, WO = 0, KD, 2 * KD, 3 * KD

        def chunks(m):
            return [(c, min(512, m["nkp"] - c)) for c in range(0, m["nkp"], 512)]

        def tile_groups(m):
            n = len(m["kt"])
            return [(t, min(4, n - t)) for t in range(0, n, 4)]

        def v_groups(m):
            return tile_groups(m)

        def c_sync(sp, m, F, fast=False):
            if fast:
                for b in range(B):
                    sp.dma_start(c_mu[:, b * QT:(b + 1) * QT, :],
                                 mask[b, :, W0:S2].rearrange("(i p) s -> p i s", p=P)).then_inc(F["mask_in"], 16)
                for b in range(B):
                    wait_past(sp, F["ctx_lo"], b)
                    sp.dma_start(c_cr[:, :, :], ctxT[b, :, W0:S2].rearrange("(k p) s -> p k s", p=P)
                                 ).then_inc(F["ctx_in"], 16)
            def head_pair(pair):
                wait_past(sp, F["w_lo"], pair)
                sp.dma_start(m["wr"][:, :, :], l1_wp[pair]).then_inc(F["w_in"], 16)
                if not fast:
                    def batch(b):
                        it = pair * B + b
                        wait_past(sp, F["ctx_lo"], it)
                        settle(sp)
                        wait_past(sp, F["min"], it * 8)
                        sp.dma_start(g_cr[:, :, :], ctxT[b].rearrange("(k p) s -> p k s", p=P)).then_inc(F["ctx_in"], 16)
                        sp.dma_start(g_mu[:, :, :], mask[b].rearrange("(i p) s -> p i s", p=P)).then_inc(F["mask_in"], 16)
                    each(sp, B, batch, isinstance(pair, int))
            each(sp, PAIRS, head_pair)

        def over_units(eng, fast, start, unit):
            def head_pair(pair):
                start(pair)
                if fast:
                    for b in range(B):
                        unit(pair * B + b, b)
                else:
                    def batch(b):
                        unit(pair * B + b, b)
                    each(eng, B, batch, isinstance(pair, int))
            each(eng, PAIRS, head_pair)

        def c_pe(pe, m, F, fast=False):
            nb = m["sbufs"]
            TB = 2 if fast else 6
            tg, ngr = tile_groups(m), len(tile_groups(m))
            sall = PS[:, 0:4, :].rearrange("p a c -> p (a c)")
            wait_blocks(pe, 2)

            def start(pair):
                pe.wait_ge(F["w_lo"], pair + 1)
                settle(pe)
                if fast:
                    pe.wait_ge(F["ctx_lo"], B)

            def unit(it, b):
                zb = [z[:, :, bass.ds(b * S, S)] for z in ZT]
                cc = [c[:, b, :, :] for c in c_c] if fast else g_c
                if not fast:
                    pe.wait_ge(F["ctx_lo"], it + 1)
                wait_past(pe, F["x"], it * 2)
                for k in range(KD):
                    last = split_matmul(pe, PS[:, 4, :], [w[:, WQ + k, :] for w in m["w"]], [z[:, k, :] for z in zb],
                                        k == 0, k == KD - 1)
                last.then_inc(F["q"], 1)
                nch = len(chunks(m))
                for n, (c0, cw) in enumerate(chunks(m)):
                    if n:
                        pe.wait_ge(F["k_lo"], it * nch + n)
                    for k in range(KD):
                        last = split_matmul(pe, PS[:, 5, 0:cw], [w[:, WK + k, :] for w in m["w"]],
                                            [c[:, k, c0:c0 + cw] for c in cc], k == 0, k == KD - 1)
                    last.then_inc(F["k"], 1)
                if not fast:
                    wait_past(pe, F["t_out_dve"], it * 8 * ngr)
                for n, (t0, nt) in enumerate(v_groups(m)):
                    if n:
                        pe.wait_ge(F["v_out"], it * len(v_groups(m)) + n)
                    for t in range(t0, t0 + nt):
                        k0, kw = m["kt"][t]
                        for k in range(KD):
                            last = split_matmul(pe, PS[0:kw, 6, (t - t0) * P:(t - t0 + 1) * P],
                                                [c[:, k, k0:k0 + kw] for c in cc], [w[:, WV + k, :] for w in m["w"]],
                                                k == 0, k == KD - 1)
                    last.then_inc(F["v"], 1)

                def scores(n):
                    h, i = n // QT, n % QT
                    if fast:
                        pe.wait_ge(F["min"], it * 8 + n - 1) if n >= 2 else pe.wait_ge(F["min"], it * 8)
                    else:
                        wait_past(pe, F["min"], it * 8 + n)
                    if n == 0:
                        pe.wait_ge(F["q_lo"], it + 1)
                        pe.wait_ge(F["k_lo"], it * nch + nch)
                    for c0, cw in chunks(m):
                        o = PS[:, n % 2, 0:cw] if fast else sall[:, c0:c0 + cw]
                        last = split_matmul(pe, o, [q[h * DH:(h + 1) * DH, i * P:(i + 1) * P] for q in m["q"]],
                                            [k[h * DH:(h + 1) * DH, c0:c0 + cw] for k in m["k"]])
                    last.then_inc(F["s"], 1)

                def turn(n):
                    pe.wait_ge(F["norm"], it * 8 + n + 1)
                    for g, (t0, nt) in enumerate(tg):
                        if fast:
                            wait_past(pe, F["t_out_dve" if n % 2 == 0 else "t_out_act"], it * 4 + n // 2)
                        else:
                            wait_past(pe, F["t_out_dve"], (it * 8 + n) * ngr + g)
                            if n == 0 and g == 0:
                                pe.wait_ge(F["v_out"], it * ngr + ngr)
                        for t in range(t0, t0 + nt):
                            k0, kw = m["kt"][t]
                            last = pe.transpose(PS[0:kw, TB + (n % 2 if fast else 0), (t - t0) * P:(t - t0 + 1) * P],
                                                m["pr"][n % len(m["pr"])][:, k0:k0 + kw], ident[:, :])
                        last.then_inc(F["t"], 1)

                def attend(heads):
                    if fast:
                        pe.wait_ge(F["t_out_dve"], it * 4 + 4)
                        pe.wait_ge(F["t_out_act"], it * 4 + 4)
                    else:
                        pe.wait_ge(F["t_out_dve"], (it * 8 + 4 * heads[0] + 4) * ngr)
                    pe.wait_ge(F["v_out"], it * ngr + ngr)
                    wait_past(pe, F["u_lo"], it)
                    for t, (k0, kw) in enumerate(m["kt"]):
                        for h in heads:
                            last = pe.matmul(PS[h * DH:(h + 1) * DH, 7, :], m["v"][0:kw, t, h * DH:(h + 1) * DH],
                                             m["pt"][0:kw, h if fast else 0, t, :], start=t == 0,
                                             stop=t == len(m["kt"]) - 1, skip_group_check=True)
                    last.then_inc(F["u"], 1)

                if fast:
                    scores(0)
                    scores(1)
                    for n in range(8):
                        if n + 2 < 8:
                            scores(n + 2)
                        turn(n)
                    attend([0, 1])
                    pe.wait_ge(F["u_lo"], it + 1)
                else:
                    for h in range(2):
                        for n in range(4 * h, 4 * h + 4):
                            scores(n)
                            turn(n)
                        attend([h])
                    pe.wait_ge(F["u_lo"], it + 1)
                for i in range(QT):
                    wo = [w[:, WO:WO + 2, :].rearrange("p a n -> p (a n)") for w in m["w"]]
                    last = split_matmul(pe, PS[:, 4 + i // 2, (i % 2) * D:(i % 2 + 1) * D],
                                        [u[:, i * P:(i + 1) * P] for u in m["u"]], wo)
                last.then_inc(F["y"], 1)
            over_units(pe, fast, start, unit)

        def c_act(act, m, F, fast=False):
            if fast:
                for b in range(B):
                    act.wait_ge(F["ctx_in"], 16 * b + 16)
                    act.activation(c_c[0][:, b, :, :], c_cr[:, :, :], ACT.Copy).then_inc(F["ctx_hi"], 1)

            def start(pair):
                act.wait_ge(F["w_in"], pair * 16 + 16)
                wait_past(act, F["y"], pair * B)
                act.activation(m["w"][0][:, :, :], m["wr"][:, :, :], ACT.Copy).then_inc(F["w_hi"], 1)

            def unit(it, b):
                nch = len(chunks(m))
                if not fast:
                    act.wait_ge(F["ctx_in"], it * 16 + 16)
                    wait_past(act, F["y"], it)
                    act.activation(g_c[0][:, :, 0:S2], g_cr[:, :, :], ACT.Copy).then_inc(F["ctx_hi"], 1)
                act.wait_ge(F["q"], it + 1)
                wait_past(act, F["s"], it * 8)
                act.activation(m["q"][0][:, :], PS[:, 4, :], ACT.Copy, scale=-DH ** -0.5).then_inc(F["q_hi"], 1)
                for n, (c0, cw) in enumerate(chunks(m)):
                    act.wait_ge(F["k"], it * nch + n + 1)
                    act.activation(m["k"][0][:, c0:c0 + cw], PS[:, 5, 0:cw], ACT.Copy).then_inc(F["k_hi"], 1)

                def turned(n):
                    act.wait_ge(F["t"], it * 8 + n + 1)
                    wait_past(act, F["u"], it)
                    kw = m["kt"][0][1]
                    act.activation(m["pt"][0:kw, n // QT, :, (n % QT) * P:(n % QT + 1) * P],
                                   PS[0:kw, 3, :].rearrange("p (t q) -> p t q", q=P), ACT.Copy
                                   ).then_inc(F["t_out_act"], 1)

                def attended(h, count):
                    hs = slice(0, P) if fast else slice(h * DH, (h + 1) * DH)
                    act.wait_ge(F["u"], count)
                    wait_past(act, F["y"], it)
                    act.activation(m["u"][0][hs, :], PS[hs, 7, :], ACT.Copy).then_inc(F["u_hi"], 1)

                ngr = len(tile_groups(m))
                for n in range(8):
                    act.wait_ge(F["min"], it * 8 + n + 1)
                    np_ = len(m["pr"])
                    if n >= np_:
                        act.wait_ge(F["t"], (it * 8 + n - np_ + 1) * ngr)
                    else:
                        wait_past(act, F["t"], it * 8 * ngr)
                    act.activation(m["pr"][n % np_][:, :], m["sm"][n % 2][:, :], ACT.Exp, bias=m["mn"][:, n:n + 1],
                                   scale=-1.0, accum_out=m["l"][:, n:n + 1]).then_inc(F["exp"], 1)
                    if fast and n >= 2 and n % 2 == 0:
                        turned(n - 1)
                    if not fast and n % QT == QT - 1:
                        attended(n // QT, it * 2 + n // QT + 1)
                if fast:
                    turned(7)
                    attended(0, it + 1)
            over_units(act, fast, start, unit)

        def c_pool(pool, m, F, fast=False):
            if not fast:
                pool.memset(g_c[0][:, :, S2:S2P].bitcast(F32), 0.0).then_inc(F["pad"], 1)
                pool.memset(g_c[1][:, :, S2:S2P].bitcast(F32), 0.0).then_inc(F["pad"], 1)
            else:
                for b in range(B):
                    pool.wait_ge(F["mask_in"], B * 16)
                    pool.tensor_scalar(c_mw[:, b * QT:(b + 1) * QT, :], c_mu[:, b * QT:(b + 1) * QT, :], BIG, None,
                                       ALU.mult).then_inc(F["mask"], 1)

            def unit(it, b):
                for n in range(8):
                    pool.wait_ge(F["rl"], it * 8 + n + 1)
                    settle(pool)
                    p = m["pr"][n % len(m["pr"])]
                    pool.tensor_scalar(p[:, :], p[:, :], m["rl"][:, n:n + 1], None, ALU.mult).then_inc(F["norm"], 1)
            over_units(pool, fast, lambda pair: None, unit)

        def c_dve(dve, m, F, fast=False):
            if fast:
                for b in range(B):
                    dve.wait_ge(F["ctx_hi"], b + 1)
                    dve.tensor_tensor(c_c[1][:, b, :, :], c_cr[:, :, :], c_c[0][:, b, :, :].bitcast(F32),
                                      ALU.subtract).then_inc(F["ctx_lo"], 1)
                dve.wait_ge(F["mask"], B)
            dve.wait_ge(bo_added, B)

            def start(pair):
                dve.wait_ge(F["w_hi"], pair + 1)
                dve.tensor_tensor(m["w"][1][:, :, :], m["wr"][:, :, :], m["w"][0][:, :, :].bitcast(F32),
                                  ALU.subtract).then_inc(F["w_lo"], 1)

            def unit(it, b):
                nch, ngr = len(chunks(m)), len(tile_groups(m))
                if not fast:
                    dve.wait_ge(F["pad"], 2)
                    dve.wait_ge(F["ctx_hi"], it + 1)
                    dve.tensor_tensor(g_c[1][:, :, 0:S2], g_cr[:, :, :], g_c[0][:, :, 0:S2].bitcast(F32),
                                      ALU.subtract).then_inc(F["ctx_lo"], 1)
                dve.wait_ge(F["q_hi"], it + 1)
                dve.scalar_tensor_tensor(m["q"][1][:, :], PS[:, 4, :], -DH ** -0.5, m["q"][0][:, :].bitcast(F32),
                                         ALU.mult, ALU.subtract).then_inc(F["q_lo"], 1)
                for n, (c0, cw) in enumerate(chunks(m)):
                    dve.wait_ge(F["k_hi"], it * nch + n + 1)
                    dve.tensor_tensor(m["k"][1][:, c0:c0 + cw], PS[:, 5, 0:cw], m["k"][0][:, c0:c0 + cw].bitcast(F32),
                                      ALU.subtract).then_inc(F["k_lo"], 1)
                for n, (t0, nt) in enumerate(v_groups(m)):
                    kw = m["kt"][t0 + nt - 1][1]
                    dve.wait_ge(F["v"], it * ngr + n + 1)
                    if n == 0:
                        wait_past(dve, F["u"], it if fast else it * 2)
                    dve.tensor_copy(m["v"][0:kw, t0:t0 + nt, :],
                                    PS[0:kw, 6, 0:nt * P].rearrange("p (t n) -> p t n", t=nt)).then_inc(F["v_out"], 1)

                def masked(n):
                    i = n % QT
                    dve.wait_ge(F["s"], it * 8 + n + 1)
                    wait_past(dve, F["exp"], it * 8 + n - 1 if n >= 2 else it * 8)
                    if fast:
                        sc, mw = PS[:, n % 2, 0:m["nk"]], c_mw[:, b * QT + i, :]
                    else:
                        sc = PS[:, 0:4, :].rearrange("p a c -> p (a c)")[:, 0:m["nk"]]
                        dve.wait_ge(F["mask_in"], it * 16 + 16)
                        dve.tensor_scalar(m["sm"][n % 2][:, :], g_mu[:, i, :], BIG, None, ALU.mult).then_inc(F["mask"], 1)
                        dve.wait_ge(F["mask"], it * 8 + n + 1)
                        mw = m["sm"][n % 2][:, :]
                    settle(dve)
                    dve.tensor_tensor_reduce(m["sm"][n % 2][:, :], sc, mw, 1.0, BIG, ALU.add, ALU.min,
                                             m["mn"][:, n:n + 1]).then_inc(F["min"], 1)

                def recip(n):
                    dve.wait_ge(F["exp"], it * 8 + n + 1)
                    dve.reciprocal(m["rl"][:, n:n + 1], m["l"][:, n:n + 1]).then_inc(F["rl"], 1)

                def turned(n):
                    for g, (t0, nt) in enumerate(tile_groups(m)):
                        kw = m["kt"][t0 + nt - 1][1]
                        dve.wait_ge(F["t"], (it * 8 + n) * ngr + g + 1)
                        wait_past(dve, F["u"], it if fast else it * 2 + n // QT)
                        dve.tensor_copy(m["pt"][0:kw, n // QT if fast else 0, t0:t0 + nt, (n % QT) * P:(n % QT + 1) * P],
                                        PS[0:kw, 2 if fast else 6, 0:nt * P].rearrange("p (t q) -> p t q", q=P)
                                        ).then_inc(F["t_out_dve"], 1)

                if fast:
                    masked(0)
                    for n in range(8):
                        if n + 1 < 8:
                            masked(n + 1)
                        recip(n)
                        if n % 2 == 1:
                            turned(n - 1)
                else:
                    for n in range(8):
                        masked(n)
                        recip(n)
                        turned(n)
                        if n % QT == QT - 1:
                            h = n // QT
                            dve.wait_ge(F["u_hi"], it * 2 + h + 1)
                            hs = slice(h * DH, (h + 1) * DH)
                            u_lo = dve.tensor_tensor(m["u"][1][hs, :], PS[hs, 7, :], m["u"][0][hs, :].bitcast(F32),
                                                     ALU.subtract)
                            if h == 1:
                                u_lo.then_inc(F["u_lo"], 1)
                if fast:
                    dve.wait_ge(F["u_hi"], it + 1)
                    dve.tensor_tensor(m["u"][1][:, :], PS[:, 7, :], m["u"][0][:, :].bitcast(F32),
                                      ALU.subtract).then_inc(F["u_lo"], 1)
                dve.wait_ge(F["y"], it + 1)
                for h in range(2):
                    xs = X[:, b * QT + 2 * h:b * QT + 2 * h + 2, :] if fast else X[:, bass.ds(b * QT + 2 * h, 2), :]
                    dve.tensor_tensor(xs, PS[:, 4 + h, :].rearrange("p (t d) -> p t d", t=2), xs,
                                      ALU.add).then_inc(F["x"], 1)
            over_units(dve, fast, start, unit)
            dve.tensor_copy(flag[1:2, 0:1], flag[0:1, 0:1]) if False else None
            dve.wait_ge(F["x"], PAIRS * B * 2)
            dve.memset(fl_s[:, 0:1], 0.0).then_inc(attn_done, 1)

        NS = 2 * QT
        UNITS = PAIRS * B
        AHEAD = 3

        def window_units(eng, steps, before):
            def head_pair(pair, final):
                for b in range(B):
                    steps(pair, b, pair if b < B - 1 else pair + 1, (b + 1) % B, final and b == B - 1)
            before()
            head_pair(0, False)
            with eng.Fori(1, PAIRS - 1) as pair:
                head_pair(pair, False)
            head_pair(PAIRS - 1, True)

        def w_sync(sp, m, F):
            for b in range(B):
                sp.dma_start(c_mu[:, b * QT:(b + 1) * QT, :],
                             mask[b, :, W0:S2].rearrange("(i p) s -> p i s", p=P)).then_inc(F["mask_in"], 16)
            sp.dma_start(m["wr"][:, :, :], l1_wp[0]).then_inc(F["w_in"], 16)
            for b in range(B):
                wait_past(sp, F["ctx_lo"], b)
                sp.dma_start(c_cr[:, :, :], ctxT[b, :, W0:S2].rearrange("(k p) s -> p k s", p=P)
                             ).then_inc(F["ctx_in"], 16)
            with sp.Fori(1, PAIRS) as pair:
                sp.wait_ge(F["w_lo"], pair * 2)
                sp.dma_start(m["wr"][:, :, :], l1_wp[pair]).then_inc(F["w_in"], 16)

        def w_pe(pe, m, F):
            def queries_and_keys(pair, b):
                u = pair * B + b
                if b == 0:
                    pe.wait_ge(F["w_lo"], pair * 2 + 1)
                if isinstance(u, int) and u < B:
                    pe.wait_ge(F["ctx_lo"], u + 1)
                wait_past(pe, F["x"], (u - 1) * 2)
                for k in range(KD):
                    last = split_matmul(pe, PS[:, 4, :], [w[:, WQ + k, :] for w in m["w"]],
                                        [z[:, k, b * S:(b + 1) * S] for z in ZT], k == 0, k == KD - 1)
                last.then_inc(F["q"], 1)
                for k in range(KD):
                    last = split_matmul(pe, PS[:, 5, 0:WIN], [w[:, WK + k, :] for w in m["w"]],
                                        [c[:, b, k, :] for c in c_c], k == 0, k == KD - 1)
                last.then_inc(F["k"], 1)

            def values(pair, b):
                u = pair * B + b
                wait_past(pe, F["v_out"], u)
                for t, (k0, kw) in enumerate(m["kt"]):
                    for k in range(KD):
                        last = split_matmul(pe, PS[0:kw, 6, t * P:(t + 1) * P], [c[:, b, k, k0:k0 + kw] for c in c_c],
                                            [w[:, WV + k, :] for w in m["w"]], k == 0, k == KD - 1)
                last.then_inc(F["v"], 1)

            def scores(u, n):
                h, i = n // QT, n % QT
                wait_past(pe, F["min"], u * NS + n - 1)
                if n == 0:
                    pe.wait_ge(F["q_lo"], u + 1)
                    pe.wait_ge(F["k_lo"], u + 1)
                split_matmul(pe, PS[:, n % 2, 0:WIN], [q[h * DH:(h + 1) * DH, i * P:(i + 1) * P] for q in m["q"]],
                             [k[h * DH:(h + 1) * DH, :] for k in m["k"]]).then_inc(F["s"], 1)

            def turn(u, n):
                pe.wait_ge(F["norm"], u * NS + n + 1)
                wait_past(pe, F["t_out_act"], u * NS + n - 1)
                for t, (k0, kw) in enumerate(m["kt"]):
                    last = pe.transpose(PS[0:kw, 2 + n % 2, t * P:(t + 1) * P], m["pr"][n % 4][:, k0:k0 + kw], ident[:, :])
                last.then_inc(F["t"], 1)

            def attend(u):
                pe.wait_ge(F["t_out_act"], u * NS + NS)
                pe.wait_ge(F["v_out"], u + 1)
                wait_past(pe, F["u_lo"], u)
                for t, (k0, kw) in enumerate(m["kt"]):
                    for h in range(2):
                        last = pe.matmul(PS[h * DH:(h + 1) * DH, 7, :], m["v"][0:kw, t, h * DH:(h + 1) * DH],
                                         m["pt"][0:kw, h, t, :], start=t == 0, stop=t == len(m["kt"]) - 1,
                                         skip_group_check=True)
                last.then_inc(F["u"], 1)

            def project(u):
                pe.wait_ge(F["u_lo"], u + 1)
                wo = [w[:, WO:WO + 2, :].rearrange("p a n -> p (a n)") for w in m["w"]]
                for i in range(QT):
                    last = split_matmul(pe, PS[:, 4 + i // 2, (i % 2) * D:(i % 2 + 1) * D],
                                        [a[:, i * P:(i + 1) * P] for a in m["u"]], wo)
                last.then_inc(F["y"], 1)

            def before():
                wait_blocks(pe, 2)
                queries_and_keys(0, 0)
                values(0, 0)
                for n in range(AHEAD):
                    scores(0, n)

            def steps(pair, b, pair2, b2, final):
                u = pair * B + b
                for n in range(NS):
                    if n + AHEAD < NS:
                        scores(u, n + AHEAD)
                    turn(u, n)
                    if n + AHEAD == NS - 1 and not final:
                        queries_and_keys(pair2, b2)
                if not final:
                    for n in range(AHEAD):
                        scores(u + 1, n)
                attend(u)
                if not final:
                    values(pair2, b2)
                if b == 0:
                    pe.wait_ge(F["w_lo"], pair * 2 + 2)
                project(u)
            window_units(pe, steps, before)

        def w_act(act, m, F):
            def high_weights(pair):
                act.wait_ge(F["w_in"], pair * 16 + 16)
                wait_past(act, F["v"], pair * B)
                act.activation(m["w"][0][:, 0:WO, :], m["wr"][:, 0:WO, :], ACT.Copy).then_inc(F["w_hi"], 1)

            def high_output(pair):
                wait_past(act, F["y"], pair * B)
                act.activation(m["w"][0][:, WO:, :], m["wr"][:, WO:, :], ACT.Copy).then_inc(F["w_hi"], 1)

            def high_queries_and_keys(u):
                act.wait_ge(F["q"], u + 1)
                wait_past(act, F["s"], u * NS)
                act.activation(m["q"][0][:, :], PS[:, 4, :], ACT.Copy, scale=-DH ** -0.5).then_inc(F["q_hi"], 1)
                act.wait_ge(F["k"], u + 1)
                act.activation(m["k"][0][:, :], PS[:, 5, 0:WIN], ACT.Copy).then_inc(F["k_hi"], 1)

            def exponentials(u, n):
                act.wait_ge(F["min"], u * NS + n + 1)
                wait_past(act, F["t"], u * NS + n - 3)
                act.activation(m["pr"][n % 4][:, :], m["sm"][n % 2][:, :], ACT.Exp, bias=m["mn"][:, n:n + 1],
                               scale=-1.0, accum_out=m["l"][:, n:n + 1]).then_inc(F["exp"], 1)

            def turned(u, n):
                act.wait_ge(F["t"], u * NS + n + 1)
                if n == 0:
                    wait_past(act, F["u"], u)
                act.activation(m["pt"][0:WIN // 4, n // QT, :, (n % QT) * P:(n % QT + 1) * P],
                               PS[0:WIN // 4, 2 + n % 2, :].rearrange("p (t q) -> p t q", q=P), ACT.Copy
                               ).then_inc(F["t_out_act"], 1)

            def before():
                high_weights(0)
                high_output(0)
                for b in range(B):
                    act.wait_ge(F["ctx_in"], 16 * b + 16)
                    act.activation(c_c[0][:, b, :, :], c_cr[:, :, :], ACT.Copy).then_inc(F["ctx_hi"], 1)
                    if b == 0:
                        high_queries_and_keys(0)
                for n in range(AHEAD):
                    exponentials(0, n)

            def steps(pair, b, pair2, b2, final):
                u = pair * B + b
                if b == 0 and not (isinstance(pair, int) and pair == 0):
                    high_output(pair)
                for n in range(AHEAD, NS):
                    exponentials(u, n)
                    turned(u, n - AHEAD)
                    if n == NS - 2 and b == B - 1 and not final:
                        high_weights(pair2)
                if not final:
                    high_queries_and_keys(u + 1)
                for n in range(NS - AHEAD, NS):
                    turned(u, n)
                if not final:
                    for n in range(AHEAD):
                        exponentials(u + 1, n)
                act.wait_ge(F["u"], u + 1)
                wait_past(act, F["y"], u)
                act.activation(m["u"][0][:, :], PS[:, 7, :], ACT.Copy).then_inc(F["u_hi"], 1)
            window_units(act, steps, before)

        def w_pool(pool, m, F):
            for b in range(B):
                pool.wait_ge(F["mask_in"], B * 16)
                pool.tensor_scalar(c_mw[:, b * QT:(b + 1) * QT, :], c_mu[:, b * QT:(b + 1) * QT, :], BIG, None,
                                   ALU.mult).then_inc(F["mask"], 1)

        def w_dve(dve, m, F):
            def low_weights(pair):
                dve.wait_ge(F["w_hi"], pair * 2 + 1)
                dve.tensor_tensor(m["w"][1][:, 0:WO, :], m["wr"][:, 0:WO, :], m["w"][0][:, 0:WO, :].bitcast(F32),
                                  ALU.subtract).then_inc(F["w_lo"], 1)

            def low_output(pair):
                dve.wait_ge(F["w_hi"], pair * 2 + 2)
                dve.tensor_tensor(m["w"][1][:, WO:, :], m["wr"][:, WO:, :], m["w"][0][:, WO:, :].bitcast(F32),
                                  ALU.subtract).then_inc(F["w_lo"], 1)

            def low_queries_and_keys(u):
                dve.wait_ge(F["q_hi"], u + 1)
                dve.scalar_tensor_tensor(m["q"][1][:, :], PS[:, 4, :], -DH ** -0.5, m["q"][0][:, :].bitcast(F32),
                                         ALU.mult, ALU.subtract).then_inc(F["q_lo"], 1)
                dve.wait_ge(F["k_hi"], u + 1)
                dve.tensor_tensor(m["k"][1][:, :], PS[:, 5, 0:WIN], m["k"][0][:, :].bitcast(F32),
                                  ALU.subtract).then_inc(F["k_lo"], 1)

            def values_out(u):
                dve.wait_ge(F["v"], u + 1)
                wait_past(dve, F["u"], u)
                dve.tensor_copy(m["v"][0:WIN // 4, :, :],
                                PS[0:WIN // 4, 6, :].rearrange("p (t n) -> p t n", n=P)).then_inc(F["v_out"], 1)

            def masked(u, b, n):
                dve.wait_ge(F["s"], u * NS + n + 1)
                wait_past(dve, F["exp"], u * NS + n - 1)
                settle(dve)
                dve.tensor_tensor_reduce(m["sm"][n % 2][:, :], PS[:, n % 2, 0:WIN], c_mw[:, b * QT + n % QT, :], 1.0,
                                         BIG, ALU.add, ALU.min, m["mn"][:, n:n + 1]).then_inc(F["min"], 1)

            def normalised(u, n):
                dve.wait_ge(F["exp"], u * NS + n + 1)
                dve.reciprocal(m["rl"][:, n:n + 1], m["l"][:, n:n + 1]).then_inc(F["rl"], 1)
                dve.wait_ge(F["rl"], u * NS + n + 1)
                p = m["pr"][n % 4]
                dve.tensor_scalar(p[:, :], p[:, :], m["rl"][:, n:n + 1], None, ALU.mult).then_inc(F["norm"], 1)

            def first_probabilities(u, b):
                masked(u, b, 0)
                for n in range(AHEAD):
                    if n + 1 < AHEAD:
                        masked(u, b, n + 1)
                    normalised(u, n)

            def before():
                low_weights(0)
                low_output(0)
                for b in range(B):
                    dve.wait_ge(F["ctx_hi"], b + 1)
                    dve.tensor_tensor(c_c[1][:, b, :, :], c_cr[:, :, :], c_c[0][:, b, :, :].bitcast(F32),
                                      ALU.subtract).then_inc(F["ctx_lo"], 1)
                    if b == 0:
                        low_queries_and_keys(0)
                values_out(0)
                dve.wait_ge(F["mask"], B)
                dve.wait_ge(bo_added, B)
                first_probabilities(0, 0)

            def steps(pair, b, pair2, b2, final):
                u = pair * B + b
                if b == 0 and not (isinstance(pair, int) and pair == 0):
                    low_output(pair)
                masked(u, b, AHEAD)
                for n in range(AHEAD, NS):
                    if n + 1 < NS:
                        masked(u, b, n + 1)
                    normalised(u, n)
                    if n == NS - 1 and b == B - 1 and not final:
                        low_weights(pair2)
                if not final:
                    low_queries_and_keys(u + 1)
                    first_probabilities(u + 1, b2)
                dve.wait_ge(F["u_hi"], u + 1)
                dve.tensor_tensor(m["u"][1][:, :], PS[:, 7, :], m["u"][0][:, :].bitcast(F32),
                                  ALU.subtract).then_inc(F["u_lo"], 1)
                if not final:
                    values_out(u + 1)
                dve.wait_ge(F["y"], u + 1)
                for h in range(2):
                    xs = X[:, b * QT + 2 * h:b * QT + 2 * h + 2, :]
                    dve.tensor_tensor(xs, PS[:, 4 + h, :].rearrange("p (t d) -> p t d", t=2), xs,
                                      ALU.add).then_inc(F["x"], 1)
            window_units(dve, steps, before)
            dve.wait_ge(F["x"], UNITS * 2)
            dve.memset(fl_s[:, 0:1], 0.0).then_inc(attn_done, 1)

        def both_paths(eng, window, general):
            eng.wait_ge(flag_ready, 1)
            path = eng.value_load(flag[0:1, 0:1], min_val=0, max_val=1)
            with eng.If(path == 0):
                window(eng, memF, CF)
            with eng.Else():
                general(eng, memG, CG)

        block = ctx_all.enter_context(nc.Block())

        @block.sync
        def _(sp):
            for b in range(B):
                sp.dma_start(X[:, b * QT:(b + 1) * QT, :], x[b].rearrange("(i p) d -> p i d", p=P)).then_inc(x_in, 16)
            sp.dma_start(C[:, :], cols).then_inc(const_in, 16)
            sp.dma_start(R[:, :], rows.partition_broadcast(P)).then_inc(const_in, 16)
            a_sync(sp)
            sp.wait_ge(A["o_lo"], B * KD)
            ffn_sync(sp, M, memM, 2, l0_w1, l0_w2)
            sp.wait_ge(x_done[0], 2 * B * 2)
            b_sync(sp)
            sp.wait_ge(x_done[1], E0 * B * QT)
            both_paths(sp, w_sync, c_sync)
            sp.wait_ge(attn_done, 1)
            d_sync(sp)
            sp.wait_ge(x_done[3], (G1 + GS) * B * 2)
            for b in range(B):
                sp.dma_start(out[b].rearrange("(i p) d -> p i d", p=P), X[:, b * QT:(b + 1) * QT, :]).then_inc(x_in, 16)
            sp.wait_ge(x_in, 2 * B * 16)

        @block.gpsimd
        def _(pool):
            pool.memset(halfneg[:, :], -0.5).then_inc(ident_ready, 1)
            pool.memset(ident[:, :], 0.0).then_inc(ident_ready, 1)
            pool.wait_ge(ident_ready, 2)
            pool.affine_select(out=ident[:, :], in_=ident[:, :], compare_op=ALU.not_equal, fill=1.0, base=0,
                               pattern=[[-1, P]], channel_multiplier=1).then_inc(ident_ready, 1)
            ln_pool(pool, 0)
            a_pool(pool)
            pool.wait_ge(A["o_lo"], B * KD)
            pool.wait_ge(const_in, 32)
            m_pool(pool)
            pool.wait_ge(x_done[0], 2 * B * 2)
            b_route_pool(pool)
            ln_pool(pool, 1, rms=True)
            b_pool(pool)
            pool.wait_ge(x_done[1], E0 * B * QT)
            ln_pool(pool, 2)
            pool.wait_ge(LN["z"], NT * 3)
            for b in range(B):
                pool.tensor_tensor(X[:, b * QT:(b + 1) * QT, :], X[:, b * QT:(b + 1) * QT, :],
                                   row("bo").unsqueeze(1).to_broadcast([P, QT, D]), ALU.add).then_inc(bo_added, 1)
            both_paths(pool, w_pool, c_pool)
            pool.wait_ge(attn_done, 1)
            d_route_pool(pool)
            ln_pool(pool, 3)
            d_pool(pool)

        @block.scalar
        def _(act):
            ln_act(act, 0)
            a_act(act)
            act.wait_ge(A["o_lo"], B * KD)
            m_act(act)
            act.wait_ge(x_done[0], 2 * B * 2)
            ln_act(act, 1)
            b_route_act(act)
            b_act(act)
            act.wait_ge(x_done[1], E0 * B * QT)
            ln_act(act, 2)
            both_paths(act, w_act, c_act)
            act.wait_ge(attn_done, 1)
            ln_act(act, 3)
            d_route_act(act)
            d_act(act)

        @block.vector
        def _(dve):
            dve.wait_ge(x_in, B * 16)
            ln_dve(dve, 0)
            a_dve(dve)
            dve.wait_ge(flag_red, 2 * B)
            dve.tensor_reduce(fl_s[:, 0:1], fl_a[:, :], AX.X, ALU.min).then_inc(flag_sum, 1)
            dve.tensor_reduce(fl_s[:, 1:2], fl_b[:, :], AX.X, ALU.max).then_inc(flag_sum, 1)
            dve.wait_ge(flag_sum, 2)
            dve.tensor_tensor(fl_a[:, 0:1], fl_s[:, 1:2], fl_s[:, 0:1], ALU.subtract).then_inc(flag_sum, 1)
            dve.wait_ge(flag_sum, 3)
            dve.tensor_scalar(fl_b[:, 0:1], fl_a[:, 0:1], 1.0, None, ALU.add).then_inc(flag_sum, 1)
            dve.memset(fl_b[:, 1:2], 1.0).then_inc(flag_sum, 1)
            dve.wait_ge(flag_sum, 6)
            dve.tensor_scalar(flag[0:1, :], PS[0:1, 3, 0:1], 1.0, None, ALU.min).then_inc(flag_ready, 1)
            m_dve(dve)
            dve.wait_ge(x_done[0], 2 * B * 2)
            ln_dve(dve, 1, rms=True)
            b_route_dve(dve)
            b_dve(dve)
            dve.wait_ge(x_done[1], E0 * B * QT)
            ln_dve(dve, 2)
            both_paths(dve, w_dve, c_dve)
            ln_dve(dve, 3)
            d_route_dve(dve)
            d_dve(dve)

        @block.tensor
        def _(pe):
            pe.wait_ge(ident_ready, 3)
            ln_pe(pe, 0)
            a_pe(pe)
            pe.wait_ge(flag_sum, 5)
            pe.matmul(PS[0:1, 3, 0:1], fl_b[:, 0:1], fl_b[:, 1:2], start=True, stop=True).then_inc(flag_sum, 1)
            pe.wait_ge(flag_ready, 1)
            pe.wait_ge(A["o_lo"], B * KD)
            ffn_pe(pe, M, memM, 2, 4, x_done[0], 2,
                   lambda u, m: wait_past(pe, M["act"], (u - 1) * 4 + m + 1))
            pe.wait_ge(x_done[0], 2 * B * 2)
            ln_pe(pe, 1, rms=True)
            b_route_pe(pe)
            ffn_pe(pe, BM, memB, E0, 2, x_done[1], QT,
                   lambda u, m: wait_past(pe, BM["glu" if m < 2 else "lin"], (u - 1) * 2 + m % 2 + 1))
            pe.wait_ge(x_done[1], E0 * B * QT)
            ln_pe(pe, 2)
            both_paths(pe, w_pe, c_pe)
            pe.wait_ge(attn_done, 1)
            ln_pe(pe, 3)
            d_route_pe(pe)
            ffn_pe(pe, DM, memD, G1 + GS, 4, x_done[3], 2,
                   lambda u, m: wait_past(pe, DM["act"], (u - 1) * 4 + m + 1))


def kernel(**inp):
    import numpy as np
    import concourse.bacc as bacc
    from concourse.bass_utils import run_bass_kernel_spmd as run

    a = {k: np.asarray(v) for k, v in inp.items()}

    def tall(v):
        return v.reshape(-1, P).T

    def one_column(v):
        c = np.zeros((P, 1), v.dtype)
        c[:len(v), 0] = v
        return c

    wkv, bkv = a["L0_xattn_W_kv"], a["L0_xattn_b_kv"]
    mlp1 = np.concatenate([a["L0_ffn_mlp1_w"][:, 0::2], a["L0_ffn_mlp1_w"][:, 1::2]], axis=1).transpose(0, 2, 1)
    mlp1_b = np.concatenate([a["L0_ffn_mlp1_b"][:, 0::2], a["L0_ffn_mlp1_b"][:, 1::2]], axis=1)
    l1_b1 = np.concatenate([a["L1_ffn_b1"].reshape(-1), a["L1_ffn_sb1"].reshape(-1)])
    cols = np.concatenate([tall(a["L0_xattn_b_q"]), tall(bkv[:D]), tall(bkv[D:]), tall(a["L0_xattn_b1"]),
                           tall(mlp1_b.reshape(-1)), tall(l1_b1), one_column(a["L0_ffn_gate_b"]),
                           one_column(a["L1_ffn_router_b"])], axis=1)
    rows = np.concatenate([a["L0_xattn_b2"], a["L0_ffn_norm_w"], a["L1_xattn_bo"]])

    def pair_cols(w):
        return w.reshape(KD, P, PAIRS, P).transpose(2, 1, 0, 3)

    l1_wp = np.concatenate([pair_cols(a["L1_xattn_Wq"]), pair_cols(a["L1_xattn_Wk"]), pair_cols(a["L1_xattn_Wv"]),
                            a["L1_xattn_Wo"].reshape(PAIRS, P, 2, P)], axis=2)
    l1_w1 = np.concatenate([a["L1_ffn_w1"].reshape(G1, 8, D, H1).transpose(0, 2, 1, 3).reshape(G1, D, 512),
                            a["L1_ffn_sw1"]], axis=0)
    l1_w2 = np.concatenate([a["L1_ffn_w2"].reshape(G1, 512, D), a["L1_ffn_sw2"]], axis=0)
    arrays = {
        "x": a["x"], "ctxT": a["ctx_1024"].transpose(0, 2, 1), "ctx": a["ctx_1024"],
        "mask": a["mask_BxSxS2_bk1"], "cols": cols, "rows": rows,
        "l0_wq": a["L0_xattn_W_q"], "l0_wkT": wkv[:, :D].T, "l0_wv": wkv[:, D:],
        "l0_w1": a["L0_xattn_W1"].reshape(D, 2, 512).transpose(1, 0, 2), "l0_w2": a["L0_xattn_W2"].reshape(2, 512, D),
        "gate_wT": a["L0_ffn_gate_w"].T, "mlp1": mlp1, "mlp2": a["L0_ffn_mlp2_w"].transpose(0, 2, 1),
        "mlp2_b": a["L0_ffn_mlp2_b"], "l1_wp": l1_wp, "router_w": a["L1_ffn_router_w"], "l1_w1": l1_w1,
        "l1_w2": l1_w2, "l1_b2": np.concatenate([a["L1_ffn_b2"], a["L1_ffn_sb2"]], axis=0),
    }
    arrays = {k: np.ascontiguousarray(v) for k, v in arrays.items()}
    nc = bacc.Bacc("TRN2", target_bir_lowering=False, num_devices=1)
    args = {k: nc.dram_tensor(k, v.shape, mybir.dt.from_np(v.dtype), kind="ExternalInput").ap()
            for k, v in arrays.items()}
    args["out"] = nc.dram_tensor("out", (B, S, D), F32, kind="ExternalOutput").ap()
    build_program(nc, **args)
    r = run(nc, [arrays], core_ids=[0])
    return r.results[0]["out"]
```

```python
from contextlib import ExitStack

import concourse.bass as bass
from concourse import mybir

F32 = mybir.dt.float32
F32R = mybir.dt.float32r
U8 = mybir.dt.uint8
I32 = mybir.dt.int32
ACT = mybir.ActivationFunctionType
ALU = mybir.AluOpType
AX = mybir.AxisListType

P = 128
B, S, D = 4, 512, 256
S2 = 1601
KD = D // P
QT = S // P
NT = B * QT
S2P = S2 + 1
KT = -(-S2 // P)
KLAST = S2 - (KT - 1) * P
E0, I0 = 8, 256
E1, H1 = 64, 64
ES, HS = 2, 512
TOP1 = 8
G1 = E1 * H1 // 512
GS = ES * HS // 512
HEADS, DH = 16, 64
PAIRS = HEADS // 2
WIN = S2 // 4
W0 = S2 - WIN
LN_EPS = 1e-5
RMS_EPS = 1.1920928955078125e-07
BIG = 3.4028234663852886e38
LIMIT, ALPHA = 7.0, 1.702

COLS = {}
ROWS = {}


def _place(table, parts):
    at = 0
    for name, n in parts:
        table[name] = (at, n)
        at += n
    return at


NCOLS = _place(COLS, [("bq", KD), ("bk", KD), ("bv", KD), ("b1", 8), ("mlp1_b", 4 * E0), ("l1_b1", 4 * (G1 + GS)),
                      ("gate_b", 1), ("router_b", 1)])
NROWS = _place(ROWS, [("b2", D), ("norm_w", D), ("bo", D)])


def split_matmul(pe, out, w, x, first=True, last=True):
    pe.matmul(out, w[0], x[0], start=first, stop=False)
    pe.matmul(out, w[0], x[1], start=False, stop=False)
    return pe.matmul(out, w[1], x[0], start=False, stop=last)


def build_program(nc, x, ctxT, ctx, mask, cols, rows, l0_wq, l0_wkT, l0_wv, l0_w1, l0_w2, gate_wT,
                  mlp1, mlp2, mlp2_b, l1_wp, router_w, l1_w1, l1_w2, l1_b2, out):
    with ExitStack() as ctx_all:
        def sem(name):
            return ctx_all.enter_context(nc.semaphore(name))

        def keep(name, shape, dt=F32):
            return ctx_all.enter_context(nc.sbuf_tensor(name, shape, dt))

        def arena():
            stack = ExitStack()

            def sb(name, shape, dt=F32):
                return stack.enter_context(nc.sbuf_tensor(name, shape, dt))
            return stack, sb

        X = keep("X", [P, NT, D])
        ident = keep("ident", [P, P])
        halfneg = keep("halfneg", [P, NT])
        C = keep("C", [P, NCOLS])
        R = keep("R", [P, NROWS])
        ZT = [keep(f"ZT{h}", [P, KD, B * S], F32R) for h in range(2)]
        Z = keep("Z", [P, QT, D])
        HZ = keep("HZ", [P, QT, D])
        zz = keep("zz", [P, D])
        st = keep("st", [P, NT, 6])
        mv = keep("mv", [P, NT, 2])
        ve = keep("ve", [P, NT])
        rs = keep("rs", [P, NT])
        ms = keep("ms", [P, QT])
        ve2 = keep("ve2", [P, QT])
        rs2 = keep("rs2", [P, QT])
        flag = keep("flag", [P, 1], I32)
        fl_m = keep("fl_m", [P, QT, S2], U8)
        fl_a = keep("fl_a", [P, NT])
        fl_b = keep("fl_b", [P, NT])
        fl_s = keep("fl_s", [P, 2])
        PS = ctx_all.enter_context(nc.psum_tensor("PS", [P, 8, 512], F32))
        wscratch = nc.dram_tensor("wscratch", [(G1 + GS) * 8, B * S], F32).ap()

        def col(name, j):
            return C[:, COLS[name][0] + j:COLS[name][0] + j + 1]

        def row(name):
            return R[:, ROWS[name][0]:ROWS[name][0] + ROWS[name][1]]

        stA, sb = arena()
        a_raw = sb("a_raw", [P, 3, KD, D])
        a_w = [sb(f"a_w{h}", [P, 3, KD, D], F32R) for h in range(2)]
        a_bk = sb("a_bk", [P, KD, 2], F32R)
        a_cT = sb("a_cT", [P, KD, S2])
        a_c = [sb(f"a_c{h}", [P, KD, S2P], F32R) for h in range(2)]
        a_nat = sb("a_nat", [P, KT, D])
        a_q = [sb(f"a_q{h}", [P, KD, S], F32R) for h in range(2)]
        a_p = [sb(f"a_p{i}", [P, S2]) for i in range(2)]
        a_pt = sb("a_pt", [P, KT, P])
        a_qt = [[sb(f"a_qt{h}{i}", [P, KD, P], F32R) for h in range(2)] for i in range(2)]
        a_un = sb("a_un", [P, 2, D])
        a_u = [sb(f"a_u{h}", [P, KD, S], F32R) for h in range(2)]
        a_cs = sb("a_cs", [P, NT])
        a_mx = sb("a_mx", [P, QT])
        a_nm = sb("a_nm", [P, QT])
        a_nb = sb("a_nb", [P, QT])
        a_l = sb("a_l", [P, QT])
        a_rl = sb("a_rl", [P, QT])
        stA.close()

        def ffn_memory(tag, KTH):
            return dict(
                w1r=sb(tag + "_w1r", [P, KD, 512]), w2r=sb(tag + "_w2r", [P, KTH, D]),
                w1=[[sb(f"{tag}_w1{h}{i}", [P, KD, 512], F32R) for h in range(2)] for i in range(2)],
                w2=[[sb(f"{tag}_w2{h}{i}", [P, KTH, D], F32R) for h in range(2)] for i in range(2)],
                hf=sb(tag + "_hf", [P, 4, 512]),
                h=[[sb(f"{tag}_h{h}{i}", [P, KTH, 512], F32R) for h in range(2)] for i in range(2)],
            )

        stM, sb = arena()
        memM = ffn_memory("m", 4)
        stM.close()
        stB, sb = arena()
        memB = ffn_memory("b", 2)
        b_gs = sb("b_gs", [P, 2, 512])
        b_c1 = sb("b_c1", [P, 4 * E0])
        b_gate_raw = sb("b_gate_raw", [P, KD, E0])
        b_gate = [sb(f"b_gate{h}", [P, KD, E0], F32R) for h in range(2)]
        b_lt = sb("b_lt", [E0, 512])
        b_lg = sb("b_lg", [P, QT, 16])
        b_mr = sb("b_mr", [P, QT, 16])
        b_top = sb("b_top", [P, QT, 8])
        b_in = sb("b_in", [P, QT, 8])
        b_d = sb("b_d", [P, QT, 2])
        b_w = sb("b_w", [P, QT, 2])
        b_s1 = sb("b_s1", [P, QT, E0])
        b_s2 = sb("b_s2", [P, QT, E0])
        b_wt = sb("b_wt", [P, NT, E0])
        b_wT = sb("b_wT", [E0, 512])
        b_b2 = sb("b_b2", [E0, D])
        stB.close()
        stD, sb = arena()
        memD = ffn_memory("d", 4)
        d_wb = [sb(f"d_wb{i}", [P, 4, 512]) for i in range(2)]
        d_rw_raw = sb("d_rw_raw", [P, KD, E1])
        d_rw = [sb(f"d_rw{h}", [P, KD, E1], F32R) for h in range(2)]
        d_lt = [sb(f"d_lt{i}", [E1, 512]) for i in range(2)]
        d_pr = sb("d_pr", [P, NT, E1])
        d_mr = sb("d_mr", [P, NT, E1])
        d_top = sb("d_top", [P, NT, TOP1])
        d_nm = sb("d_nm", [P, NT])
        d_sm = sb("d_sm", [P, NT])
        d_rsm = sb("d_rsm", [P, NT])
        d_ts = sb("d_ts", [P, NT])
        d_rts = sb("d_rts", [P, NT])
        d_w = sb("d_w", [P, NT, E1])
        d_wT = [sb(f"d_wT{i}", [E1 + ES, 512]) for i in range(2)]
        d_one = sb("d_one", [GS * 8, B * S])
        d_b2 = sb("d_b2", [E1 + ES, D])
        stD.close()

        def attn_memory(tag, nk, kt, sbufs):
            nkp = nk + nk % 2
            m = dict(nk=nk, nkp=nkp, kt=kt, sbufs=sbufs,
                     tag=tag, wr=sb(tag + "wr", [P, 3 * KD + 2, P]),
                     w=[sb(f"{tag}w{h}", [P, 3 * KD + 2, P], F32R) for h in range(2)],
                     q=[sb(f"{tag}q{h}", [P, S], F32R) for h in range(2)],
                     k=[sb(f"{tag}k{h}", [P, nkp], F32R) for h in range(2)],
                     v=sb(tag + "v", [P, len(kt), P]),
                     sm=[sb(f"{tag}sm{i}", [P, nk]) for i in range(2)],
                     pr=[sb(f"{tag}pr{i}", [P, nk]) for i in range(2 * sbufs)],
                     pt=sb(tag + "pt", [P, 2 if sbufs == 2 else 1, len(kt), S]),
                     u=[sb(f"{tag}u{h}", [P, S], F32R) for h in range(2)],
                     mn=sb(tag + "mn", [P, 8]), l=sb(tag + "l", [P, 8]), rl=sb(tag + "rl", [P, 8]))
            return m

        stC, sb = arena()
        c_mw = sb("c_mw", [P, NT, WIN])
        c_mu = sb("c_mu", [P, NT, WIN], U8)
        c_cr = sb("c_cr", [P, KD, WIN])
        c_c = [sb(f"c_c{h}", [P, B, KD, WIN], F32R) for h in range(2)]
        memF = attn_memory("f_", WIN, [(WIN // 4 * j, WIN // 4) for j in range(4)], 2)
        stC.close()
        stG, sb = arena()
        g_cr = sb("g_cr", [P, KD, S2])
        g_c = [sb(f"g_c{h}", [P, KD, S2P], F32R) for h in range(2)]
        g_mu = sb("g_mu", [P, QT, S2], U8)
        memG = attn_memory("g_", S2, [(P * j, min(P, S2 - P * j)) for j in range(KT)], 1)
        stG.close()
        const_in = sem("const_in")
        x_in = sem("x_in")
        ones_ready = sem("ones_ready")
        ident_ready = sem("ident_ready")
        x_done = [sem(f"x_done{i}") for i in range(5)]
        LN = {k: sem("ln_" + k) for k in ("stats", "moments", "ve", "rstd", "z", "turned", "hi", "lo", "ms", "ve2",
                                          "rstd2", "h", "zadd")}
        flag_in = sem("flag_in")
        flag_red = sem("flag_red")
        flag_sum = sem("flag_sum")
        flag_ready = sem("flag_ready")

        def wait_past(eng, s, value):
            if isinstance(value, int) and value <= 0:
                return
            eng.wait_ge(s, value)

        def each(eng, n, steps, peel=True):
            if peel:
                steps(0)
            with eng.Fori(1 if peel else 0, n) as i:
                steps(i)

        def settle(eng):
            eng.nop(nofuse=True)

        def ln_dve(dve, s, rms=False, after=None):
            L = LN
            for n in range(NT):
                dve.bn_stats(st[:, n, :], X[:, n, :]).then_inc(L["stats"], 1)
            dve.wait_ge(L["stats"], (s + 1) * NT)
            for n in range(NT):
                dve.bn_aggr(mv[:, n, :], st[:, n, :]).then_inc(L["moments"], 1)
            dve.wait_ge(L["moments"], (s + 1) * NT)
            dve.tensor_scalar(ve[:, :], mv[:, :, 1], LN_EPS, None, ALU.add).then_inc(L["ve"], 1)
            dve.wait_ge(L["rstd"], s + 1)
            def batch(b):
                for i in range(QT):
                    if rms:
                        wait_past(dve, L["zadd"], b * QT)
                    else:
                        wait_past(dve, L["turned"], (s * B + b) * QT)
                    dve.tensor_scalar(Z[:, i, :], X[:, b * QT + i, :], mv[:, b * QT + i, 0:1], rs[:, bass.ds(b * QT + i, 1)],
                                      ALU.subtract, ALU.mult).then_inc(L["z"], 1)
                if rms:
                    for i in range(QT):
                        dve.wait_ge(L["z"], (s * B + b) * QT + i + 1)
                        dve.tensor_tensor_reduce(zz[:, :], Z[:, i, :], Z[:, i, :], 1.0, 0.0, ALU.mult, ALU.add,
                                                 ms[:, i:i + 1]).then_inc(L["ms"], 1)
                        dve.wait_ge(L["ms"], b * QT + i + 1)
                    dve.tensor_scalar(ve2[:, :], ms[:, :], 1.0 / D, RMS_EPS, ALU.mult, ALU.add).then_inc(L["ve2"], 1)
                    dve.wait_ge(L["rstd2"], b + 1)
                    dve.wait_ge(L["turned"], (s * B + b) * QT)
                    for i in range(QT):
                        dve.scalar_tensor_tensor(HZ[:, i, :], Z[:, i, :], rs2[:, i:i + 1], row("norm_w"),
                                                 ALU.mult, ALU.mult).then_inc(L["h"], 1)
                for i in range(QT):
                    dve.wait_ge(L["hi"], (s * B + b) * QT + i + 1)
                    dve.tensor_tensor(ZT[1][:, :, bass.ds(b * S + i * P, P)],
                                      PS[:, 6 + i % 2, 0:KD * P].rearrange("p (k t) -> p k t", k=KD),
                                      ZT[0][:, :, bass.ds(b * S + i * P, P)].bitcast(F32),
                                      ALU.subtract).then_inc(L["lo"], 1)
                if after:
                    after(b)
            each(dve, B, batch)

        def ln_pool(pool, s, rms=False):
            L = LN
            pool.wait_ge(L["ve"], s + 1)
            pool.tensor_tensor(rs[:, :], ve[:, :], halfneg[:, :], ALU.pow).then_inc(L["rstd"], 1)
            def batch(b):
                if rms:
                    pool.wait_ge(L["ve2"], b + 1)
                    pool.tensor_tensor(rs2[:, :], ve2[:, :], halfneg[:, 0:QT], ALU.pow).then_inc(L["rstd2"], 1)
                    pool.wait_ge(L["h"], b * QT + QT)
                    for i in range(QT):
                        pool.tensor_tensor(X[:, b * QT + i, :], X[:, b * QT + i, :], Z[:, i, :],
                                           ALU.add).then_inc(L["zadd"], 1)
            if rms:
                each(pool, B, batch)

        def ln_pe(pe, s, rms=False, after=None):
            L = LN
            src = HZ if rms else Z
            def batch(b):
                for i in range(QT):
                    pe.wait_ge(L["h"] if rms else L["z"], (b if rms else s * B + b) * QT + i + 1)
                    if i >= 2:
                        pe.wait_ge(L["lo"], (s * B + b) * QT + i - 1)
                    else:
                        wait_past(pe, L["lo"], (s * B + b) * QT)
                    for k in range(KD):
                        last = pe.transpose(PS[:, 6 + i % 2, k * P:(k + 1) * P], src[:, i, k * P:(k + 1) * P],
                                            ident[:, :])
                    last.then_inc(L["turned"], 1)
                if after:
                    after(b)
            each(pe, B, batch)

        def ln_act(act, s, after=None):
            L = LN
            def batch(b):
                for i in range(QT):
                    act.wait_ge(L["turned"], (s * B + b) * QT + i + 1)
                    settle(act)
                    act.activation(ZT[0][:, :, bass.ds(b * S + i * P, P)],
                                   PS[:, 6 + i % 2, 0:KD * P].rearrange("p (k t) -> p k t", k=KD),
                                   ACT.Copy).then_inc(L["hi"], 1)
                if after:
                    after(b)
            each(act, B, batch)

        def wait_blocks(eng, s):
            eng.wait_ge(LN["lo"], NT * (s + 1))

        A = {k: sem("a_" + k) for k in (
            "w_in", "w_hi", "w_lo", "pad", "ctxT_in", "nat_in", "ctx_hi", "ctx_lo", "q", "q_hi", "q_lo", "qp", "qp_hi",
            "qp_lo", "csum", "q_tile", "s", "own", "nb", "exp", "rl", "norm", "t", "t_out_act", "t_out_dve", "u", "ut",
            "u_hi", "u_lo", "o", "o_hi", "o_lo")}
        TG = [(0, 4), (4, 4), (8, 4), (12, 1)]
        sflat = PS[:, 0:4, :].rearrange("p a c -> p (a c)")

        def a_batches(eng, batch, last):
            batch(0, False)
            with eng.Fori(1, B - 1) as b:
                batch(b, False)
            batch(B - 1, True)
            last()

        def a_weights_sync(sp):
            for j, w in enumerate((l0_wq, l0_wkT, l0_wv)):
                sp.dma_start(a_raw[:, j, :, :], w.rearrange("(k p) n -> p k n", p=P)).then_inc(A["w_in"], 16)

        def a_sync(sp):
            def batch(b):
                wait_past(sp, A["ctx_lo"], b * KD)
                sp.dma_start(a_cT[:, :, :], ctxT[b].rearrange("(k p) s -> p k s", p=P)).then_inc(A["ctxT_in"], 16)
                wait_past(sp, A["u"], b * QT)
                settle(sp)
                sp.dma_start(a_nat[:, 0:KT - 1, :],
                             ctx[b, 0:(KT - 1) * P].rearrange("(t p) d -> p t d", p=P)).then_inc(A["nat_in"], 16)
                sp.dma_start(a_nat[0:KLAST, KT - 1, :], ctx[b, (KT - 1) * P:S2]).then_inc(A["nat_in"], 16)
                wait_past(sp, flag_red, b * QT * 2)
                settle(sp)
                sp.dma_start(fl_m[:, :, :], mask[b].rearrange("(i p) s -> p i s", p=P)).then_inc(flag_in, 16)
            each(sp, B, batch)

        def a_queries_pe(pe, b):
            pe.wait_ge(LN["lo"], b * QT + QT)
            pe.wait_ge(A["w_lo"], 2)
            zb = [z[:, :, bass.ds(b * S, S)] for z in ZT]
            for m in range(KD):
                for k in range(KD):
                    last = split_matmul(pe, PS[:, m, :], [w[:, 0, k, m * P:(m + 1) * P] for w in a_w],
                                        [z[:, k, :] for z in zb], k == 0, k == KD - 1)
                last.then_inc(A["q"], 1)
            pe.wait_ge(A["q_lo"], b * KD + KD)
            wait_past(pe, A["qp_lo"], b * KD)
            for m in range(KD):
                for k in range(KD):
                    last = split_matmul(pe, PS[:, 2 + m, :], [w[:, 1, k, m * P:(m + 1) * P] for w in a_w],
                                        [q[:, k, :] for q in a_q], k == 0, k == KD - 1)
                last.then_inc(A["qp"], 1)
            wait_past(pe, A["csum"], b)
            settle(pe)
            for i in range(QT):
                for n, (k, h) in enumerate([(k, h) for k in range(KD) for h in range(2)]):
                    last = pe.matmul(PS[:, 4, 2 * i:2 * i + 2], a_q[h][:, k, i * P:(i + 1) * P], a_bk[:, k, :],
                                     start=n == 0, stop=n == 2 * KD - 1)
            last.then_inc(A["qp"], 1)

        def a_queries_act(act, b):
            if isinstance(b, int):
                act.wait_ge(A["w_in"], 48)
                act.wait_ge(const_in, 32)
                act.activation(a_w[0][:, :, :, :], a_raw[:, :, :, :], ACT.Copy).then_inc(A["w_hi"], 1)
                act.activation(a_bk[:, :, 0], C[:, COLS["bk"][0]:COLS["bk"][0] + KD], ACT.Copy).then_inc(A["w_hi"], 1)
            for m in range(KD):
                act.wait_ge(A["q"], b * KD + m + 1)
                wait_past(act, A["qp"], b * (KD + 1))
                act.activation(a_q[0][:, m, :], PS[:, m, :], ACT.Identity, bias=col("bq", m)).then_inc(A["q_hi"], 1)
            for m in range(KD):
                act.wait_ge(A["qp"], b * (KD + 1) + m + 1)
                settle(act)
                act.activation(ZT[0][:, m, bass.ds(b * S, S)], PS[:, 2 + m, :], ACT.Copy).then_inc(A["qp_hi"], 1)

        def a_queries_dve(dve, b):
            if isinstance(b, int):
                dve.wait_ge(A["w_hi"], 2)
                dve.tensor_tensor(a_w[1][:, :, :, :].rearrange("p a k n -> p (a k n)"),
                                  a_raw[:, :, :, :].rearrange("p a k n -> p (a k n)"),
                                  a_w[0][:, :, :, :].rearrange("p a k n -> p (a k n)").bitcast(F32),
                                  ALU.subtract).then_inc(A["w_lo"], 1)
                dve.tensor_tensor(a_bk[:, :, 1], C[:, COLS["bk"][0]:COLS["bk"][0] + KD], a_bk[:, :, 0].bitcast(F32),
                                  ALU.subtract).then_inc(A["w_lo"], 1)
            for m in range(KD):
                dve.wait_ge(A["q_hi"], b * KD + m + 1)
                dve.scalar_tensor_tensor(a_q[1][:, m, :], PS[:, m, :], col("bq", m), a_q[0][:, m, :].bitcast(F32),
                                         ALU.add, ALU.subtract).then_inc(A["q_lo"], 1)
            for m in range(KD):
                dve.wait_ge(A["qp_hi"], b * KD + m + 1)
                block_b = bass.ds(b * S, S)
                dve.tensor_tensor(ZT[1][:, m, block_b], PS[:, 2 + m, :], ZT[0][:, m, block_b].bitcast(F32),
                                  ALU.subtract).then_inc(A["qp_lo"], 1)
            dve.wait_ge(A["qp"], b * (KD + 1) + KD + 1)
            settle(dve)
            dve.tensor_reduce(a_cs[:, bass.ds(b * QT, QT)], PS[:, 4, 0:2 * QT].rearrange("p (i h) -> p i h", h=2),
                              AX.X, ALU.add).then_inc(A["csum"], 1)

        def a_pe(pe):
            def attend(n, i):
                pe.wait_ge(A["t_out_dve"], n * 2 + 2)
                pe.wait_ge(A["t_out_act"], n * 2 + 2)
                wait_past(pe, A["norm"], n - 1)
                settle(pe)
                for t in range(KT):
                    w = P if t < KT - 1 else KLAST
                    last = pe.matmul(PS[:, 6, i % 2 * D:(i % 2 + 1) * D], a_pt[0:w, t, :], a_nat[0:w, t, :],
                                     start=t == 0, stop=t == KT - 1)
                last.then_inc(A["u"], 1)

            def turn_attended(n, i):
                pe.wait_ge(A["norm"], n + 1)
                wait_past(pe, A["u_lo"], n)
                settle(pe)
                for k in range(KD):
                    last = pe.transpose(PS[:, 7, k * P:(k + 1) * P], a_un[:, i % 2, k * P:(k + 1) * P], ident[:, :])
                last.then_inc(A["ut"], 1)

            def output(b):
                pe.wait_ge(A["u_lo"], b * QT + QT)
                for m in range(KD):
                    for k in range(KD):
                        last = split_matmul(pe, PS[:, 4 + m, :], [w[:, 2, k, m * P:(m + 1) * P] for w in a_w],
                                            [u[:, k, :] for u in a_u], k == 0, k == KD - 1)
                    last.then_inc(A["o"], 1)

            def batch(b, final):
                first = isinstance(b, int) and b == 0
                if first:
                    pe.wait_ge(A["qp_lo"], B * KD)
                    pe.wait_ge(A["csum"], B)
                pe.wait_ge(A["ctx_lo"], b * KD + KD)
                for i in range(QT):
                    n = b * QT + i
                    if not (first and i == 0):
                        pe.wait_ge(A["exp"], n)
                        settle(pe)
                    pe.wait_ge(A["q_tile"], n * 2 + 2)
                    settle(pe)
                    for c in range(4):
                        w = min(512, S2P - 512 * c)
                        for k in range(KD):
                            last = split_matmul(pe, sflat[:, 512 * c:512 * c + w],
                                                [q[:, k, :] for q in a_qt[i % 2]],
                                                [a[:, k, 512 * c:512 * c + w] for a in a_c], k == 0, k == KD - 1)
                    last.then_inc(A["s"], 1)
                    if i == 1 and not first:
                        pe.wait_ge(A["t_out_dve"], n * 2)
                        pe.wait_ge(A["t_out_act"], n * 2)
                        output(b - 1)
                    if i:
                        attend(n - 1, i - 1)
                    elif not first:
                        pe.wait_ge(A["nat_in"], b * 32)
                        attend(n - 1, QT - 1)
                    pe.wait_ge(A["exp"], n + 1)
                    if i == 1 and not first:
                        pe.wait_ge(A["o_lo"], b * KD)
                    for g, (t0, nt) in enumerate(TG):
                        if g >= 2:
                            pe.wait_ge(A["t_out_dve" if g % 2 == 0 else "t_out_act"], n * 2 + 1)
                        settle(pe)
                        for t in range(t0, t0 + nt):
                            w = P if t < KT - 1 else KLAST
                            last = pe.transpose(PS[0:w, 4 + g % 2, (t - t0) * P:(t - t0 + 1) * P],
                                                a_p[i % 2][:, t * P:t * P + w], ident[:, :])
                        last.then_inc(A["t"], 1)
                    if i:
                        turn_attended(n - 1, i - 1)
                    elif not first:
                        turn_attended(n - 1, QT - 1)
                    if i == 0:
                        pe.wait_ge(A["nat_in"], b * 32 + 32)

            def last():
                attend(NT - 1, QT - 1)
                turn_attended(NT - 1, QT - 1)
                output(B - 1)
            a_batches(pe, batch, last)

        def a_act(act):
            def context(b, k):
                act.wait_ge(A["ctxT_in"], b * 16 + 16)
                act.activation(a_c[0][:, k, 0:S2], a_cT[:, k, :], ACT.Copy).then_inc(A["ctx_hi"], 1)

            def attended(n, i):
                act.wait_ge(A["ut"], n + 1)
                act.activation(a_u[0][:, :, i * P:(i + 1) * P],
                               PS[:, 7, 0:KD * P].rearrange("p (k t) -> p k t", k=KD), ACT.Copy).then_inc(A["u_hi"], 1)

            def output(b):
                for m in range(KD):
                    act.wait_ge(A["o"], b * KD + m + 1)
                    settle(act)
                    act.activation(ZT[0][:, m, bass.ds(b * S, S)], PS[:, 4 + m, :], ACT.Identity,
                                   bias=col("bv", m)).then_inc(A["o_hi"], 1)

            for k in range(KD):
                context(0, k)

            def batch(b, final):
                first = isinstance(b, int) and b == 0
                for i in range(QT):
                    n = b * QT + i
                    if i == QT - 1 and not final:
                        act.wait_ge(A["s"], n + 1)
                        for k in range(KD):
                            context(b + 1, k)
                    act.wait_ge(A["nb"], n + 1)
                    if not (first and i < 2):
                        act.wait_ge(A["t"], (n - 1) * 4)
                    act.activation(a_p[i % 2][:, :], sflat[:, 0:S2], ACT.Exp,
                                   bias=a_nb[:, i:i + 1], accum_out=a_l[:, i:i + 1]).then_inc(A["exp"], 1)
                    if i == 1 and not first:
                        output(b - 1)
                    wait_past(act, A["u"], n)
                    for g in (1, 3):
                        t0, nt = TG[g]
                        w = P if t0 + nt < KT else KLAST
                        act.wait_ge(A["t"], n * 4 + g + 1)
                        act.activation(a_pt[0:w, t0:t0 + nt, :],
                                       PS[0:w, 5, 0:nt * P].rearrange("p (t q) -> p t q", t=nt),
                                       ACT.Copy).then_inc(A["t_out_act"], 1)
                    if not (first and i == 0):
                        attended(n - 1, (i - 1) % QT)

            def last():
                attended(NT - 1, QT - 1)
                output(B - 1)
            a_batches(act, batch, last)

        def a_pool(pool):
            pool.memset(a_c[0][:, :, S2:S2P].bitcast(F32), 0.0).then_inc(A["pad"], 1)
            pool.memset(a_c[1][:, :, S2:S2P].bitcast(F32), 0.0).then_inc(A["pad"], 1)
            pool.wait_ge(A["qp_lo"], B * KD)
            def batch(b, final):
                for i in range(QT):
                    wait_past(pool, A["s"], b * QT + i - 1)
                    settle(pool)
                    for h in range(2):
                        pool.tensor_copy(a_qt[i % 2][h][:, :, :],
                                         ZT[h][:, :, bass.ds(b * S + i * P, P)]).then_inc(A["q_tile"], 1)
            a_batches(pool, batch, lambda: None)

        def a_dve(dve):
            dve.wait_ge(A["pad"], 2)

            def context(b, k):
                dve.wait_ge(A["ctx_hi"], b * KD + k + 1)
                dve.tensor_tensor(a_c[1][:, k, 0:S2], a_cT[:, k, :], a_c[0][:, k, 0:S2].bitcast(F32),
                                  ALU.subtract).then_inc(A["ctx_lo"], 1)

            def normalise(n, i):
                dve.wait_ge(A["u"], n + 1)
                wait_past(dve, A["ut"], n - 1)
                dve.wait_ge(A["rl"], n + 1)
                settle(dve)
                dve.tensor_scalar(a_un[:, i % 2, :], PS[:, 6, i % 2 * D:(i % 2 + 1) * D], a_rl[:, i:i + 1], None,
                                  ALU.mult).then_inc(A["norm"], 1)

            def attended(n, i):
                dve.wait_ge(A["u_hi"], n + 1)
                dve.tensor_tensor(a_u[1][:, :, i * P:(i + 1) * P],
                                  PS[:, 7, 0:KD * P].rearrange("p (k t) -> p k t", k=KD),
                                  a_u[0][:, :, i * P:(i + 1) * P].bitcast(F32), ALU.subtract).then_inc(A["u_lo"], 1)

            def output(b):
                for m in range(KD):
                    dve.wait_ge(A["o_hi"], b * KD + m + 1)
                    dve.scalar_tensor_tensor(ZT[1][:, m, bass.ds(b * S, S)], PS[:, 4 + m, :], col("bv", m),
                                             ZT[0][:, m, bass.ds(b * S, S)].bitcast(F32), ALU.add,
                                             ALU.subtract).then_inc(A["o_lo"], 1)

            for k in range(KD):
                context(0, k)

            def batch(b, final):
                first = isinstance(b, int) and b == 0
                for i in range(QT):
                    n = b * QT + i
                    dve.wait_ge(A["s"], n + 1)
                    settle(dve)
                    dve.tensor_reduce(a_mx[:, i:i + 1], sflat[:, 0:S2], AX.X, ALU.max).then_inc(A["own"], 1)
                    dve.wait_ge(A["own"], 2 * n + 1)
                    cs = a_cs[:, bass.ds(n, 1)]
                    settle(dve)
                    dve.tensor_scalar(a_nm[:, i:i + 1], a_mx[:, i:i + 1], cs, -1.0, ALU.add,
                                      ALU.mult).then_inc(A["own"], 1)
                    dve.wait_ge(A["own"], 2 * n + 2)
                    settle(dve)
                    dve.tensor_tensor(a_nb[:, i:i + 1], a_nm[:, i:i + 1], cs, ALU.add).then_inc(A["nb"], 1)
                    if i == QT - 1 and not final:
                        for k in range(KD):
                            context(b + 1, k)
                    if i == 1 and not first:
                        output(b - 1)
                    dve.wait_ge(A["exp"], n + 1)
                    dve.reciprocal(a_rl[:, i:i + 1], a_l[:, i:i + 1]).then_inc(A["rl"], 1)
                    if not (first and i == 0):
                        normalise(n - 1, (i - 1) % QT)
                    wait_past(dve, A["u"], n)
                    for g in (0, 2):
                        t0, nt = TG[g]
                        dve.wait_ge(A["t"], n * 4 + g + 1)
                        dve.tensor_copy(a_pt[:, t0:t0 + nt, :],
                                        PS[:, 4, 0:nt * P].rearrange("p (t q) -> p t q", t=nt)).then_inc(A["t_out_dve"], 1)
                    if not (first and i == 0):
                        attended(n - 1, (i - 1) % QT)
                    dve.wait_ge(flag_in, b * 16 + 16)
                    settle(dve)
                    dve.tensor_reduce(fl_a[:, bass.ds(n, 1)], fl_m[:, i, 0:W0], AX.X, ALU.min).then_inc(flag_red, 1)
                    dve.tensor_reduce(fl_b[:, bass.ds(n, 1)], fl_m[:, i, W0:S2], AX.X, ALU.min).then_inc(flag_red, 1)

            def last():
                normalise(NT - 1, QT - 1)
                attended(NT - 1, QT - 1)
                output(B - 1)
            a_batches(dve, batch, last)

        def ffn_sems(tag, *own):
            return {k: sem(tag + "_" + k) for k in ("w_in", "w1_hi", "w2_hi", "w_lo", "h", "h_hi", "h_lo", "y", *own)}

        def sweep(eng, G, unit, split):
            def groups(g0, last):
                for n in range(2 * B):
                    g = g0 + n // B
                    unit(g, n % B, g * B + n % B)
                    if n % B == SPLIT_AT and split and not (last and n // B == 1):
                        split(g + 1, (n // B + 1) % 2)
            if split:
                split(0, 0)
            groups(0, G == 2)
            if G > 4:
                with eng.Fori(1, G // 2 - 1) as j:
                    groups(j * 2, False)
            if G > 2:
                groups(G - 2, True)
        SPLIT_AT = 1

        def ffn_sync(sp, F, mem, G, w1, w2, wb=None):
            def unit(g, b, u):
                if b == 0:
                    wait_past(sp, F["w_lo"], g * 2)
                    sp.dma_start(mem["w1r"][:, :, :], w1[g].rearrange("(k p) n -> p k n", p=P)).then_inc(F["w_in"], 16)
                    sp.dma_start(mem["w2r"][:, :, :], w2[g].rearrange("(k p) n -> p k n", p=P)).then_inc(F["w_in"], 16)
                if wb:
                    wb(g, b, u)
            sweep(sp, G, unit, None)

        def ffn_pe(pe, F, mem, G, KTH, x_sem, x_incs, h_read):
            def hidden(g, b, u, wpar):
                if b == 0:
                    pe.wait_ge(F["w_lo"], g * 2 + 2)
                for m in range(4):
                    h_read(u, m)
                    for k in range(KD):
                        last = split_matmul(pe, PS[:, m, :], [w[:, k, m * P:(m + 1) * P] for w in mem["w1"][wpar]],
                                            [z[:, k, b * S:(b + 1) * S] for z in ZT], k == 0, k == KD - 1)
                    last.then_inc(F["h"], 1)

            def second(g, b, u, wpar):
                pe.wait_ge(F["h_lo"], u * KTH + KTH)
                wait_past(pe, x_sem, (u - 1) * x_incs)
                for i in range(QT):
                    for k in range(KTH):
                        last = split_matmul(pe, PS[:, 4 + 2 * (b % 2) + i // 2, (i % 2) * D:(i % 2 + 1) * D],
                                            [h[:, k, i * P:(i + 1) * P] for h in mem["h"][b % 2]],
                                            [w[:, k, :] for w in mem["w2"][wpar]], k == 0, k == KTH - 1)
                last.then_inc(F["y"], 1)

            def groups(g0, last):
                for n in range(2 * B):
                    if n + 1 < 2 * B or not last:
                        g, b = g0 + (n + 1) // B, (n + 1) % B
                        hidden(g, b, g * B + b, ((n + 1) // B) % 2)
                    g, b = g0 + n // B, n % B
                    second(g, b, g * B + b, n // B)
            hidden(0, 0, 0, 0)
            groups(0, G == 2)
            if G > 4:
                with pe.Fori(1, G // 2 - 1) as j:
                    groups(j * 2, False)
            if G > 2:
                groups(G - 2, True)

        def split_act(act, F, mem):
            def split(g, wpar):
                act.wait_ge(F["w_in"], g * 32 + 32)
                wait_past(act, F["y"], (g - 1) * B)
                act.activation(mem["w1"][wpar][0][:, :, :], mem["w1r"][:, :, :], ACT.Copy).then_inc(F["w1_hi"], 1)
            return split

        def split_pool(pool, F, mem):
            def split(g, wpar):
                pool.wait_ge(F["w_in"], g * 32 + 32)
                wait_past(pool, F["y"], (g - 1) * B)
                settle(pool)
                pool.tensor_copy(mem["w2"][wpar][0][:, :, :], mem["w2r"][:, :, :]).then_inc(F["w2_hi"], 1)
            return split

        def split_dve(dve, F, mem):
            def split(g, wpar):
                dve.wait_ge(F["w1_hi"], g + 1)
                dve.tensor_tensor(mem["w1"][wpar][1][:, :, :], mem["w1r"][:, :, :],
                                  mem["w1"][wpar][0][:, :, :].bitcast(F32), ALU.subtract).then_inc(F["w_lo"], 1)
                dve.wait_ge(F["w2_hi"], g + 1)
                dve.tensor_tensor(mem["w2"][wpar][1][:, :, :], mem["w2r"][:, :, :],
                                  mem["w2"][wpar][0][:, :, :].bitcast(F32), ALU.subtract).then_inc(F["w_lo"], 1)
            return split

        def high_hidden(eng, F, mem, u, b, m, KTH, ready):
            eng.wait_ge(ready, u * KTH + m + 1)
            wait_past(eng, F["y"], u - 1)
            settle(eng)
            if eng is nc.scalar:
                i = eng.activation(mem["h"][b % 2][0][:, m, :], mem["hf"][:, m, :], ACT.Copy)
            else:
                i = eng.tensor_copy(mem["h"][b % 2][0][:, m, :], mem["hf"][:, m, :])
            i.then_inc(F["h_hi"], 1)

        def low_hidden(dve, F, mem, u, b, m, KTH):
            dve.wait_ge(F["h_hi"], u * KTH + m + 1)
            dve.tensor_tensor(mem["h"][b % 2][1][:, m, :], mem["hf"][:, m, :],
                              mem["h"][b % 2][0][:, m, :].bitcast(F32), ALU.subtract).then_inc(F["h_lo"], 1)

        def accumulate(dve, F, u, b, x_sem):
            dve.wait_ge(F["y"], u + 1)
            for h in range(2):
                xs = X[:, b * QT + 2 * h:b * QT + 2 * h + 2, :]
                dve.tensor_tensor(xs, PS[:, 4 + 2 * (b % 2) + h, :].rearrange("p (t d) -> p t d", t=2), xs,
                                  ALU.add).then_inc(x_sem, 1)

        M = ffn_sems("m", "act")
        bias_added = sem("m_bias_added")

        def m_act(act):
            def unit(g, b, u):
                for m in range(4):
                    act.wait_ge(M["h"], u * 4 + m + 1)
                    wait_past(act, M["h_lo"], (u - 1) * 4 + m + 1)
                    act.activation(memM["hf"][:, m, :], PS[:, m, :], ACT.Gelu, bias=col("b1", g * 4 + m)
                                   ).then_inc(M["act"], 1)
            sweep(act, 2, unit, split_act(act, M, memM))

        def m_pool(pool):
            pool.wait_ge(LN["z"], NT)
            for b in range(B):
                pool.tensor_tensor(X[:, b * QT:(b + 1) * QT, :], X[:, b * QT:(b + 1) * QT, :],
                                   row("b2").unsqueeze(1).to_broadcast([P, QT, D]), ALU.add).then_inc(bias_added, 1)

            def unit(g, b, u):
                for m in range(4):
                    high_hidden(pool, M, memM, u, b, m, 4, M["act"])
            sweep(pool, 2, unit, split_pool(pool, M, memM))

        def m_dve(dve):
            dve.wait_ge(bias_added, B)

            def unit(g, b, u):
                for m in range(4):
                    low_hidden(dve, M, memM, u, b, m, 4)
                if u > 0:
                    accumulate(dve, M, u - 1, (b - 1) % B, x_done[0])
            sweep(dve, 2, unit, split_dve(dve, M, memM))
            accumulate(dve, M, 2 * B - 1, B - 1, x_done[0])

        BM = ffn_sems("b", "glu", "lin", "sig", "gated", "mul")
        BR = {k: sem("br_" + k) for k in ("w_in", "w_hi", "w_lo", "set", "lt", "lt_out", "lg", "own", "neg",
                                           "sig", "w", "keep", "wt", "wt_out", "yb", "x")}

        def b_sync(sp):
            sp.dma_start(b_gate_raw[:, :, :], gate_wT.rearrange("(k p) e -> p k e", p=P)).then_inc(BR["w_in"], 16)
            sp.dma_start(b_b2[:, :], mlp2_b).then_inc(BR["w_in"], 16)
            ffn_sync(sp, BM, memB, E0, mlp1, mlp2)

        def b_route_pe(pe):
            wait_blocks(pe, 1)
            pe.wait_ge(BR["w_lo"], 1)
            pe.wait_ge(BR["w_in"], 32)
            def batch(b):
                for k in range(KD):
                    last = split_matmul(pe, PS[0:E0, 0, :], [w[:, k, :] for w in b_gate],
                                        [z[:, k, bass.ds(b * S, S)] for z in ZT], k == 0, k == KD - 1)
                last.then_inc(BR["lt"], 1)
                pe.wait_ge(BR["lt_out"], b + 1)
                settle(pe)
                for i in range(QT):
                    last = pe.transpose(PS[:, 1, i * E0:(i + 1) * E0], b_lt[:, i * P:(i + 1) * P], ident[0:E0, 0:E0])
                last.then_inc(BR["lg"], 1)
                pe.wait_ge(BR["w"], b + 1)
                for i in range(QT):
                    last = pe.transpose(PS[0:E0, 2, i * P:(i + 1) * P], b_s2[:, i, :], ident[:, :])
                last.then_inc(BR["wt"], 1)
                pe.wait_ge(BR["wt_out"], b + 1)
                wait_past(pe, BR["x"], b * 2)
                for i in range(QT):
                    last = pe.matmul(PS[:, 3 + i // 2, (i % 2) * D:(i % 2 + 1) * D], b_wT[:, i * P:(i + 1) * P],
                                     b_b2[:, :], start=True, stop=True)
                last.then_inc(BR["yb"], 1)
            each(pe, B, batch)
            pe.wait_ge(BR["x"], B * 2)

        def b_route_act(act):
            act.wait_ge(BR["w_in"], 32)
            act.activation(b_gate[0][:, :, :], b_gate_raw[:, :, :], ACT.Copy).then_inc(BR["w_hi"], 1)
            def batch(b):
                act.wait_ge(BR["lt"], b + 1)
                wait_past(act, BR["lg"], b)
                act.activation(b_lt[:, :], PS[0:E0, 0, :], ACT.Identity,
                               bias=col("gate_b", 0)[0:E0]).then_inc(BR["lt_out"], 1)
                act.wait_ge(BR["neg"], b + 1)
                wait_past(act, BR["w"], b)
                for i in range(QT):
                    act.activation(b_s1[:, i, :], b_lg[:, i, 0:E0], ACT.Sigmoid, bias=b_d[:, i, 0:1],
                                   scale=2.0).then_inc(BR["sig"], 1)
            each(act, B, batch)

        def b_route_pool(pool):
            pool.memset(b_lg[:, :, :], -BIG).then_inc(BR["set"], 1)
            pool.memset(b_in[:, :, :], -BIG).then_inc(BR["set"], 1)

        def b_route_dve(dve):
            dve.wait_ge(BR["w_hi"], 1)
            dve.tensor_tensor(b_gate[1][:, :, :], b_gate_raw[:, :, :], b_gate[0][:, :, :].bitcast(F32),
                              ALU.subtract).then_inc(BR["w_lo"], 1)
            dve.tensor_scalar(b_c1[:, :], C[:, COLS["mlp1_b"][0]:COLS["mlp1_b"][0] + 4 * E0], 1.0, None,
                              ALU.add).then_inc(BR["keep"], 1)
            dve.wait_ge(BR["set"], 2)
            def batch(b):
                dve.wait_ge(BR["lg"], b + 1)
                wait_past(dve, BR["sig"], b * QT)
                dve.tensor_copy(b_lg[:, :, 0:E0],
                                PS[:, 1, 0:QT * E0].rearrange("p (i e) -> p i e", e=E0)).then_inc(BR["own"], 1)
                dve.wait_ge(BR["own"], b * 10 + 1)
                settle(dve)
                for i in range(QT):
                    dve.max(b_top[:, i, :], b_lg[:, i, 0:E0]).then_inc(BR["own"], 1)
                dve.wait_ge(BR["own"], b * 10 + 5)
                dve.tensor_copy(b_in[:, :, 0:2], b_top[:, :, 0:2]).then_inc(BR["own"], 1)
                dve.scalar_tensor_tensor(b_d[:, :, 0], b_top[:, :, 0], -1.0, b_top[:, :, 1], ALU.mult,
                                         ALU.subtract).then_inc(BR["neg"], 1)
                dve.wait_ge(BR["own"], b * 10 + 6)
                settle(dve)
                for i in range(QT):
                    dve.match_replace(b_mr[:, i, :], b_in[:, i, :], b_lg[:, i, :], BIG).then_inc(BR["own"], 1)
                dve.wait_ge(BR["own"], b * 10 + 10)
                dve.wait_ge(BR["sig"], b * QT + QT)
                wait_past(dve, BR["wt"], b)
                dve.scalar_tensor_tensor(b_s2[:, :, :], b_mr[:, :, 0:E0], BIG, b_s1[:, :, :], ALU.is_equal,
                                         ALU.mult).then_inc(BR["w"], 1)
                dve.wait_ge(BR["w"], b + 1)
                dve.tensor_copy(b_wt[:, bass.ds(b * QT, QT), :], b_s2[:, :, :]).then_inc(BR["keep"], 1)
                dve.wait_ge(BR["wt"], b + 1)
                wait_past(dve, BR["yb"], b)
                dve.tensor_copy(b_wT[:, :], PS[0:E0, 2, :]).then_inc(BR["wt_out"], 1)
                dve.wait_ge(BR["yb"], b + 1)
                dve.wait_ge(LN["zadd"], NT)
                for h in range(2):
                    xs = X[:, bass.ds(b * QT + 2 * h, 2), :]
                    dve.tensor_tensor(xs, PS[:, 3 + h, :].rearrange("p (t d) -> p t d", t=2), xs,
                                      ALU.add).then_inc(BR["x"], 1)
            each(dve, B, batch)

        def b_act(act):
            def unit(g, b, u):
                for j in range(2):
                    act.wait_ge(BM["glu"], u * 2 + j + 1)
                    wait_past(act, BM["mul"], (u - 1) * 2 + j + 1)
                    act.activation(b_gs[:, j, :], memB["hf"][:, j, :], ACT.Sigmoid, scale=ALPHA).then_inc(BM["sig"], 1)
                for j in range(2):
                    high_hidden(act, BM, memB, u, b, j, 2, BM["mul"])
            sweep(act, E0, unit, split_act(act, BM, memB))

        def b_pool(pool):
            def unit(g, b, u):
                for j in range(2):
                    pool.wait_ge(BM["sig"], u * 2 + j + 1)
                    pool.tensor_tensor(b_gs[:, j, :], b_gs[:, j, :], memB["hf"][:, j, :], ALU.mult).then_inc(BM["gated"], 1)
            sweep(pool, E0, unit, split_pool(pool, BM, memB))

        def b_accumulate(dve, g, u, b):
            dve.wait_ge(BM["y"], u + 1)
            for i in range(QT):
                t = b * QT + i
                dve.scalar_tensor_tensor(X[:, t, :], PS[:, 4 + 2 * (b % 2) + i // 2, (i % 2) * D:(i % 2 + 1) * D],
                                         b_wt[:, t, bass.ds(g, 1)], X[:, t, :], ALU.mult, ALU.add
                                         ).then_inc(x_done[1], 1)

        def b_dve(dve):
            dve.wait_ge(BR["x"], B * 2)
            dve.wait_ge(BR["keep"], B + 1)
            b1 = COLS["mlp1_b"][0]

            def unit(g, b, u):
                for j in range(2):
                    dve.wait_ge(BM["h"], u * 4 + j + 1)
                    wait_past(dve, BM["h_lo"], (u - 1) * 2 + j + 1)
                    dve.tensor_scalar(memB["hf"][:, j, :], PS[:, j, :], C[:, bass.ds(b1 + g * 4 + j, 1)], LIMIT,
                                      ALU.add, ALU.min).then_inc(BM["glu"], 1)
                for j in range(2):
                    dve.wait_ge(BM["h"], u * 4 + 2 + j + 1)
                    dve.tensor_scalar(memB["hf"][:, 2 + j, :], PS[:, 2 + j, :], b_c1[:, bass.ds(g * 4 + 2 + j, 1)],
                                      LIMIT + 1.0, ALU.add, ALU.min).then_inc(BM["lin"], 1)
                for j in range(2):
                    dve.wait_ge(BM["lin"], u * 2 + j + 1)
                    dve.wait_ge(BM["gated"], u * 2 + j + 1)
                    dve.scalar_tensor_tensor(memB["hf"][:, j, :], memB["hf"][:, 2 + j, :], 1.0 - LIMIT, b_gs[:, j, :],
                                             ALU.max, ALU.mult).then_inc(BM["mul"], 1)
                for j in range(2):
                    low_hidden(dve, BM, memB, u, b, j, 2)
                if not (isinstance(u, int) and u == 0):
                    b_accumulate(dve, (g - 1) if b == 0 else g, u - 1, (b - 1) % B)
            sweep(dve, E0, unit, split_dve(dve, BM, memB))
            b_accumulate(dve, E0 - 1, E0 * B - 1, B - 1)

        DM = ffn_sems("d", "act", "mul", "wb_in0", "wb_in1")
        DR = {k: BR[k] for k in ("w_in", "w_hi", "w_lo", "lt", "lt_out", "lg", "wt", "wt_out", "yb", "x")}
        DR |= {k: sem("dr_" + k) for k in ("one", "max", "exp", "own", "sel", "w", "stored0", "stored1", "one_stored")}
        NE = (G1 + GS) * 8

        def d_sync(sp):
            sp.dma_start(d_rw_raw[:, :, :], router_w.rearrange("(k p) e -> p k e", p=P)).then_inc(DR["w_in"], 16)
            sp.dma_start(d_b2[:, :], l1_b2).then_inc(DR["w_in"], 16)
            sp.wait_ge(DR["one"], 3)
            sp.dma_start(wscratch[E1:NE, :], d_one[:, :]).then_inc(DR["one_stored"], 16)
            for b in range(B):
                sp.wait_ge(DR["wt_out"], (B + b) + 1)
                sp.dma_start(wscratch[0:E1, b * S:(b + 1) * S], d_wT[b % 2][0:E1, :]).then_inc(DR[f"stored{b % 2}"], 16)
            sp.wait_ge(DR["one_stored"], 16)
            for i in range(2):
                sp.wait_ge(DR[f"stored{i}"], 16 * (B // 2))

            def wb(g, b, u):
                wait_past(sp, DM["mul"], (u - 1) * 4)
                for s in range(2):
                    src = wscratch[bass.ds(g * 8, 8), b * S:(b + 1) * S].rearrange("(m s) t -> s m t", s=2)[s]
                    sp.dma_start(d_wb[b % 2][s * H1:(s + 1) * H1, :, :],
                                 src.unsqueeze(0).to_broadcast([H1, 4, S])).then_inc(DM[f"wb_in{b % 2}"], 16)
            ffn_sync(sp, DM, memD, G1 + GS, l1_w1, l1_w2, wb)

        def staggered(first, second):
            for b in range(B):
                first(b)
                if b:
                    second(b - 1)
            second(B - 1)

        def d_logits(b):
            return PS[:, (1, 2, 4, 5)[b], 0:QT * E1]

        def d_route_pe(pe):
            wait_blocks(pe, 3)
            pe.wait_ge(DR["w_lo"], 2)
            pe.wait_ge(DR["w_in"], 64)
            pe.wait_ge(DR["one"], 3)

            def logits(b):
                if b >= 2:
                    pe.wait_ge(DR["lt_out"], B + b - 1)
                for k in range(KD):
                    last = split_matmul(pe, PS[0:E1, b % 2 * 3, :], [w[:, k, :] for w in d_rw],
                                        [z[:, k, b * S:(b + 1) * S] for z in ZT], k == 0, k == KD - 1)
                last.then_inc(DR["lt"], 1)

            def turn_logits(b):
                pe.wait_ge(DR["lt_out"], B + b + 1)
                for i in range(QT):
                    last = pe.transpose(d_logits(b)[:, i * E1:(i + 1) * E1], d_lt[b % 2][:, i * P:(i + 1) * P],
                                        ident[0:E1, 0:E1])
                last.then_inc(DR["lg"], 1)
            staggered(logits, turn_logits)

            def turn_weights(b):
                pe.wait_ge(DR["w"], b * QT + QT)
                if b >= 2:
                    pe.wait_ge(DR["wt_out"], B + b - 1)
                for i in range(QT):
                    last = pe.transpose(PS[0:E1, b % 2 * 3, i * P:(i + 1) * P], d_w[:, b * QT + i, :], ident[:, :])
                last.then_inc(DR["wt"], 1)

            def biases(b):
                pe.wait_ge(DR["wt_out"], B + b + 1)
                if b >= 2:
                    pe.wait_ge(DR["x"], (B + b - 1) * 2)
                for i in range(QT):
                    last = pe.matmul(PS[:, 4 + b % 2 * 2 + i // 2, (i % 2) * D:(i % 2 + 1) * D],
                                     d_wT[b % 2][:, i * P:(i + 1) * P], d_b2[:, :], start=True, stop=True)
                last.then_inc(DR["yb"], 1)
            staggered(turn_weights, biases)
            pe.wait_ge(DR["x"], B * 4)

        def d_route_act(act):
            act.wait_ge(DR["w_in"], 64)
            act.activation(d_rw[0][:, :, :], d_rw_raw[:, :, :], ACT.Copy).then_inc(DR["w_hi"], 1)

            def logits_out(b):
                act.wait_ge(DR["lt"], B + b + 1)
                if b >= 2:
                    act.wait_ge(DR["lg"], B + b - 1)
                act.activation(d_lt[b % 2][:, :], PS[0:E1, b % 2 * 3, :], ACT.Identity,
                               bias=col("router_b", 0)[0:E1]).then_inc(DR["lt_out"], 1)

            def exponentials(b):
                act.wait_ge(DR["max"], b + 1)
                for i in range(QT):
                    n = b * QT + i
                    act.activation(d_pr[:, n, :], d_logits(b)[:, i * E1:(i + 1) * E1], ACT.Exp,
                                   bias=d_nm[:, n:n + 1], accum_out=d_sm[:, n:n + 1]).then_inc(DR["exp"], 1)
            staggered(logits_out, exponentials)

        def d_route_pool(pool):
            pool.memset(d_one[:, :], 1.0).then_inc(DR["one"], 1)
            for i in range(2):
                pool.memset(d_wT[i][E1:E1 + ES, :], 1.0).then_inc(DR["one"], 1)
            pool.wait_ge(DR["one"], 3)

        def d_route_dve(dve):
            dve.wait_ge(DR["w_hi"], 2)
            dve.tensor_tensor(d_rw[1][:, :, :], d_rw_raw[:, :, :], d_rw[0][:, :, :].bitcast(F32),
                              ALU.subtract).then_inc(DR["w_lo"], 1)
            for b in range(B):
                dve.wait_ge(DR["lg"], B + b + 1)
                dve.tensor_reduce(d_nm[:, b * QT:(b + 1) * QT], d_logits(b).rearrange("p (i e) -> p i e", e=E1),
                                  AX.X, ALU.max, negate=True).then_inc(DR["max"], 1)
            dve.wait_ge(DR["exp"], NT)
            dve.reciprocal(d_rsm[:, :], d_sm[:, :]).then_inc(DR["own"], 1)
            dve.wait_ge(DR["own"], 1)
            for n in range(NT):
                dve.tensor_scalar(d_pr[:, n, :], d_pr[:, n, :], d_rsm[:, n:n + 1], None,
                                  ALU.mult).then_inc(DR["own"], 1)
            dve.wait_ge(DR["own"], NT + 1)
            for n in range(NT):
                dve.max(d_top[:, n, :], d_pr[:, n, :]).then_inc(DR["own"], 1)
            dve.wait_ge(DR["own"], 2 * NT + 1)
            dve.tensor_reduce(d_ts[:, :], d_top[:, :, :], AX.X, ALU.add).then_inc(DR["own"], 1)
            for n in range(NT):
                dve.match_replace(d_mr[:, n, :], d_top[:, n, :], d_pr[:, n, :], -1.0).then_inc(DR["own"], 1)
            dve.wait_ge(DR["own"], 2 * NT + 2)
            dve.reciprocal(d_rts[:, :], d_ts[:, :]).then_inc(DR["own"], 1)
            dve.wait_ge(DR["own"], 3 * NT + 3)
            dve.scalar_tensor_tensor(d_w[:, :, :], d_mr[:, :, :], -1.0, d_pr[:, :, :], ALU.is_equal,
                                     ALU.mult).then_inc(DR["sel"], 1)
            dve.wait_ge(DR["sel"], 1)
            for n in range(NT):
                dve.tensor_scalar(d_w[:, n, :], d_w[:, n, :], d_rts[:, n:n + 1], None, ALU.mult).then_inc(DR["w"], 1)

            def weights_out(b):
                dve.wait_ge(DR["wt"], B + b + 1)
                if b >= 2:
                    dve.wait_ge(DR["yb"], B + b - 1)
                    dve.wait_ge(DR[f"stored{b % 2}"], b // 2 * 16)
                dve.tensor_copy(d_wT[b % 2][0:E1, :], PS[0:E1, b % 2 * 3, :]).then_inc(DR["wt_out"], 1)

            def add_biases(b):
                dve.wait_ge(DR["yb"], B + b + 1)
                for h in range(2):
                    xs = X[:, b * QT + 2 * h:b * QT + 2 * h + 2, :]
                    dve.tensor_tensor(xs, PS[:, 4 + b % 2 * 2 + h, :].rearrange("p (t d) -> p t d", t=2), xs,
                                      ALU.add).then_inc(DR["x"], 1)
            staggered(weights_out, add_biases)

        def d_act(act):
            b1 = COLS["l1_b1"][0]

            def unit(g, b, u):
                for m in range(4):
                    act.wait_ge(DM["h"], u * 4 + m + 1)
                    wait_past(act, DM["h_lo"], (u - 1) * 4 + m + 1)
                    settle(act)
                    act.activation(memD["hf"][:, m, :], PS[:, m, :], ACT.Silu, bias=C[:, bass.ds(b1 + g * 4 + m, 1)]
                                   ).then_inc(DM["act"], 1)
            sweep(act, G1 + GS, unit, split_act(act, DM, memD))

        def d_pool(pool):
            def unit(g, b, u):
                for m in range(4):
                    high_hidden(pool, DM, memD, u, b, m, 4, DM["mul"])
            sweep(pool, G1 + GS, unit, split_pool(pool, DM, memD))

        def d_dve(dve):
            dve.wait_ge(DR["x"], B * 4)

            def unit(g, b, u):
                dve.wait_ge(DM[f"wb_in{b % 2}"], (u // 2) * 32 + 32 if isinstance(u, int) else (g * 2 + b // 2) * 32 + 32)
                for m in range(4):
                    dve.wait_ge(DM["act"], u * 4 + m + 1)
                    dve.tensor_tensor(memD["hf"][:, m, :], memD["hf"][:, m, :], d_wb[b % 2][:, m, :],
                                      ALU.mult).then_inc(DM["mul"], 1)
                for m in range(4):
                    low_hidden(dve, DM, memD, u, b, m, 4)
                if not (isinstance(u, int) and u == 0):
                    accumulate(dve, DM, u - 1, (b - 1) % B, x_done[3])
            sweep(dve, G1 + GS, unit, split_dve(dve, DM, memD))
            accumulate(dve, DM, (G1 + GS) * B - 1, B - 1, x_done[3])

        def attn_sems(tag):
            return {k: sem("c" + tag + k) for k in (
                "w_in", "w_hi", "w_lo", "q", "q_hi", "q_lo", "k", "k_hi", "k_lo", "v", "v_out", "s", "min", "exp", "rl",
                "norm", "t", "t_out_act", "t_out_dve", "u", "u_hi", "u_lo", "y", "x", "ctx_in", "ctx_hi", "ctx_lo",
                "mask_in", "mask", "pad")}

        CF = CG = attn_sems("_")
        bo_added = sem("c_bo_added")
        attn_done = sem("attn_done")
        WQ, WK, WV, WO = 0, KD, 2 * KD, 3 * KD

        def chunks(m):
            return [(c, min(512, m["nkp"] - c)) for c in range(0, m["nkp"], 512)]

        def tile_groups(m):
            n = len(m["kt"])
            return [(t, min(4, n - t)) for t in range(0, n, 4)]

        def v_groups(m):
            return tile_groups(m)

        def c_sync(sp, m, F):
            def head_pair(pair):
                wait_past(sp, F["w_lo"], pair)
                sp.dma_start(m["wr"][:, :, :], l1_wp[pair]).then_inc(F["w_in"], 16)
                def batch(b):
                    it = pair * B + b
                    wait_past(sp, F["ctx_lo"], it)
                    settle(sp)
                    wait_past(sp, F["min"], it * 8)
                    sp.dma_start(g_cr[:, :, :], ctxT[b].rearrange("(k p) s -> p k s", p=P)).then_inc(F["ctx_in"], 16)
                    sp.dma_start(g_mu[:, :, :], mask[b].rearrange("(i p) s -> p i s", p=P)).then_inc(F["mask_in"], 16)
                each(sp, B, batch, isinstance(pair, int))
            each(sp, PAIRS, head_pair)

        def over_units(eng, start, unit):
            def head_pair(pair):
                start(pair)
                def batch(b):
                    unit(pair * B + b, b)
                each(eng, B, batch, isinstance(pair, int))
            each(eng, PAIRS, head_pair)

        def c_pe(pe, m, F):
            TB = 6
            tg, ngr = tile_groups(m), len(tile_groups(m))
            sall = PS[:, 0:4, :].rearrange("p a c -> p (a c)")
            wait_blocks(pe, 2)

            def start(pair):
                pe.wait_ge(F["w_lo"], pair + 1)
                settle(pe)

            def unit(it, b):
                zb = [z[:, :, bass.ds(b * S, S)] for z in ZT]
                cc = g_c
                pe.wait_ge(F["ctx_lo"], it + 1)
                wait_past(pe, F["x"], it * 2)
                for k in range(KD):
                    last = split_matmul(pe, PS[:, 4, :], [w[:, WQ + k, :] for w in m["w"]], [z[:, k, :] for z in zb],
                                        k == 0, k == KD - 1)
                last.then_inc(F["q"], 1)
                nch = len(chunks(m))
                for n, (c0, cw) in enumerate(chunks(m)):
                    if n:
                        pe.wait_ge(F["k_lo"], it * nch + n)
                    for k in range(KD):
                        last = split_matmul(pe, PS[:, 5, 0:cw], [w[:, WK + k, :] for w in m["w"]],
                                            [c[:, k, c0:c0 + cw] for c in cc], k == 0, k == KD - 1)
                    last.then_inc(F["k"], 1)
                wait_past(pe, F["t_out_dve"], it * 8 * ngr)
                for n, (t0, nt) in enumerate(v_groups(m)):
                    if n:
                        pe.wait_ge(F["v_out"], it * len(v_groups(m)) + n)
                    for t in range(t0, t0 + nt):
                        k0, kw = m["kt"][t]
                        for k in range(KD):
                            last = split_matmul(pe, PS[0:kw, 6, (t - t0) * P:(t - t0 + 1) * P],
                                                [c[:, k, k0:k0 + kw] for c in cc], [w[:, WV + k, :] for w in m["w"]],
                                                k == 0, k == KD - 1)
                    last.then_inc(F["v"], 1)

                def scores(n):
                    h, i = n // QT, n % QT
                    wait_past(pe, F["min"], it * 8 + n)
                    if n == 0:
                        pe.wait_ge(F["q_lo"], it + 1)
                        pe.wait_ge(F["k_lo"], it * nch + nch)
                    for c0, cw in chunks(m):
                        o = sall[:, c0:c0 + cw]
                        last = split_matmul(pe, o, [q[h * DH:(h + 1) * DH, i * P:(i + 1) * P] for q in m["q"]],
                                            [k[h * DH:(h + 1) * DH, c0:c0 + cw] for k in m["k"]])
                    last.then_inc(F["s"], 1)

                def turn(n):
                    pe.wait_ge(F["norm"], it * 8 + n + 1)
                    for g, (t0, nt) in enumerate(tg):
                        wait_past(pe, F["t_out_dve"], (it * 8 + n) * ngr + g)
                        if n == 0 and g == 0:
                            pe.wait_ge(F["v_out"], it * ngr + ngr)
                        for t in range(t0, t0 + nt):
                            k0, kw = m["kt"][t]
                            last = pe.transpose(PS[0:kw, TB, (t - t0) * P:(t - t0 + 1) * P],
                                                m["pr"][n % len(m["pr"])][:, k0:k0 + kw], ident[:, :])
                        last.then_inc(F["t"], 1)

                def attend(heads):
                    pe.wait_ge(F["t_out_dve"], (it * 8 + 4 * heads[0] + 4) * ngr)
                    pe.wait_ge(F["v_out"], it * ngr + ngr)
                    wait_past(pe, F["u_lo"], it)
                    for t, (k0, kw) in enumerate(m["kt"]):
                        for h in heads:
                            last = pe.matmul(PS[h * DH:(h + 1) * DH, 7, :], m["v"][0:kw, t, h * DH:(h + 1) * DH],
                                             m["pt"][0:kw, 0, t, :], start=t == 0,
                                             stop=t == len(m["kt"]) - 1, skip_group_check=True)
                    last.then_inc(F["u"], 1)

                for h in range(2):
                    for n in range(4 * h, 4 * h + 4):
                        scores(n)
                        turn(n)
                    attend([h])
                pe.wait_ge(F["u_lo"], it + 1)
                for i in range(QT):
                    wo = [w[:, WO:WO + 2, :].rearrange("p a n -> p (a n)") for w in m["w"]]
                    last = split_matmul(pe, PS[:, 4 + i // 2, (i % 2) * D:(i % 2 + 1) * D],
                                        [u[:, i * P:(i + 1) * P] for u in m["u"]], wo)
                last.then_inc(F["y"], 1)
            over_units(pe, start, unit)

        def c_act(act, m, F):
            def start(pair):
                act.wait_ge(F["w_in"], pair * 16 + 16)
                wait_past(act, F["y"], pair * B)
                act.activation(m["w"][0][:, :, :], m["wr"][:, :, :], ACT.Copy).then_inc(F["w_hi"], 1)

            def unit(it, b):
                nch = len(chunks(m))
                act.wait_ge(F["ctx_in"], it * 16 + 16)
                wait_past(act, F["y"], it)
                act.activation(g_c[0][:, :, 0:S2], g_cr[:, :, :], ACT.Copy).then_inc(F["ctx_hi"], 1)
                act.wait_ge(F["q"], it + 1)
                wait_past(act, F["s"], it * 8)
                act.activation(m["q"][0][:, :], PS[:, 4, :], ACT.Copy, scale=-DH ** -0.5).then_inc(F["q_hi"], 1)
                for n, (c0, cw) in enumerate(chunks(m)):
                    act.wait_ge(F["k"], it * nch + n + 1)
                    act.activation(m["k"][0][:, c0:c0 + cw], PS[:, 5, 0:cw], ACT.Copy).then_inc(F["k_hi"], 1)

                def attended(h, count):
                    hs = slice(h * DH, (h + 1) * DH)
                    act.wait_ge(F["u"], count)
                    wait_past(act, F["y"], it)
                    act.activation(m["u"][0][hs, :], PS[hs, 7, :], ACT.Copy).then_inc(F["u_hi"], 1)

                ngr = len(tile_groups(m))
                for n in range(8):
                    act.wait_ge(F["min"], it * 8 + n + 1)
                    np_ = len(m["pr"])
                    if n >= np_:
                        act.wait_ge(F["t"], (it * 8 + n - np_ + 1) * ngr)
                    else:
                        wait_past(act, F["t"], it * 8 * ngr)
                    act.activation(m["pr"][n % np_][:, :], m["sm"][n % 2][:, :], ACT.Exp, bias=m["mn"][:, n:n + 1],
                                   scale=-1.0, accum_out=m["l"][:, n:n + 1]).then_inc(F["exp"], 1)
                    if n % QT == QT - 1:
                        attended(n // QT, it * 2 + n // QT + 1)
            over_units(act, start, unit)

        def c_pool(pool, m, F):
            pool.memset(g_c[0][:, :, S2:S2P].bitcast(F32), 0.0).then_inc(F["pad"], 1)
            pool.memset(g_c[1][:, :, S2:S2P].bitcast(F32), 0.0).then_inc(F["pad"], 1)

            def unit(it, b):
                for n in range(8):
                    pool.wait_ge(F["rl"], it * 8 + n + 1)
                    settle(pool)
                    p = m["pr"][n % len(m["pr"])]
                    pool.tensor_scalar(p[:, :], p[:, :], m["rl"][:, n:n + 1], None, ALU.mult).then_inc(F["norm"], 1)
            over_units(pool, lambda pair: None, unit)

        def c_dve(dve, m, F):
            dve.wait_ge(bo_added, B)

            def start(pair):
                dve.wait_ge(F["w_hi"], pair + 1)
                dve.tensor_tensor(m["w"][1][:, :, :], m["wr"][:, :, :], m["w"][0][:, :, :].bitcast(F32),
                                  ALU.subtract).then_inc(F["w_lo"], 1)

            def unit(it, b):
                nch, ngr = len(chunks(m)), len(tile_groups(m))
                dve.wait_ge(F["pad"], 2)
                dve.wait_ge(F["ctx_hi"], it + 1)
                dve.tensor_tensor(g_c[1][:, :, 0:S2], g_cr[:, :, :], g_c[0][:, :, 0:S2].bitcast(F32),
                                  ALU.subtract).then_inc(F["ctx_lo"], 1)
                dve.wait_ge(F["q_hi"], it + 1)
                dve.scalar_tensor_tensor(m["q"][1][:, :], PS[:, 4, :], -DH ** -0.5, m["q"][0][:, :].bitcast(F32),
                                         ALU.mult, ALU.subtract).then_inc(F["q_lo"], 1)
                for n, (c0, cw) in enumerate(chunks(m)):
                    dve.wait_ge(F["k_hi"], it * nch + n + 1)
                    dve.tensor_tensor(m["k"][1][:, c0:c0 + cw], PS[:, 5, 0:cw], m["k"][0][:, c0:c0 + cw].bitcast(F32),
                                      ALU.subtract).then_inc(F["k_lo"], 1)
                for n, (t0, nt) in enumerate(v_groups(m)):
                    kw = m["kt"][t0 + nt - 1][1]
                    dve.wait_ge(F["v"], it * ngr + n + 1)
                    if n == 0:
                        wait_past(dve, F["u"], it * 2)
                    dve.tensor_copy(m["v"][0:kw, t0:t0 + nt, :],
                                    PS[0:kw, 6, 0:nt * P].rearrange("p (t n) -> p t n", t=nt)).then_inc(F["v_out"], 1)

                def masked(n):
                    i = n % QT
                    dve.wait_ge(F["s"], it * 8 + n + 1)
                    wait_past(dve, F["exp"], it * 8 + n - 1 if n >= 2 else it * 8)
                    sc = PS[:, 0:4, :].rearrange("p a c -> p (a c)")[:, 0:m["nk"]]
                    dve.wait_ge(F["mask_in"], it * 16 + 16)
                    dve.tensor_scalar(m["sm"][n % 2][:, :], g_mu[:, i, :], BIG, None, ALU.mult).then_inc(F["mask"], 1)
                    dve.wait_ge(F["mask"], it * 8 + n + 1)
                    mw = m["sm"][n % 2][:, :]
                    settle(dve)
                    dve.tensor_tensor_reduce(m["sm"][n % 2][:, :], sc, mw, 1.0, BIG, ALU.add, ALU.min,
                                             m["mn"][:, n:n + 1]).then_inc(F["min"], 1)

                def recip(n):
                    dve.wait_ge(F["exp"], it * 8 + n + 1)
                    dve.reciprocal(m["rl"][:, n:n + 1], m["l"][:, n:n + 1]).then_inc(F["rl"], 1)

                def turned(n):
                    for g, (t0, nt) in enumerate(tile_groups(m)):
                        kw = m["kt"][t0 + nt - 1][1]
                        dve.wait_ge(F["t"], (it * 8 + n) * ngr + g + 1)
                        wait_past(dve, F["u"], it * 2 + n // QT)
                        dve.tensor_copy(m["pt"][0:kw, 0, t0:t0 + nt, (n % QT) * P:(n % QT + 1) * P],
                                        PS[0:kw, 6, 0:nt * P].rearrange("p (t q) -> p t q", q=P)
                                        ).then_inc(F["t_out_dve"], 1)

                for n in range(8):
                    masked(n)
                    recip(n)
                    turned(n)
                    if n % QT == QT - 1:
                        h = n // QT
                        dve.wait_ge(F["u_hi"], it * 2 + h + 1)
                        hs = slice(h * DH, (h + 1) * DH)
                        u_lo = dve.tensor_tensor(m["u"][1][hs, :], PS[hs, 7, :], m["u"][0][hs, :].bitcast(F32),
                                                 ALU.subtract)
                        if h == 1:
                            u_lo.then_inc(F["u_lo"], 1)
                dve.wait_ge(F["y"], it + 1)
                for h in range(2):
                    xs = X[:, bass.ds(b * QT + 2 * h, 2), :]
                    dve.tensor_tensor(xs, PS[:, 4 + h, :].rearrange("p (t d) -> p t d", t=2), xs,
                                      ALU.add).then_inc(F["x"], 1)
            over_units(dve, start, unit)
            dve.wait_ge(F["x"], PAIRS * B * 2)
            dve.memset(fl_s[:, 0:1], 0.0).then_inc(attn_done, 1)

        NS = 2 * QT
        UNITS = PAIRS * B
        AHEAD = 3

        def window_units(eng, steps, before):
            def head_pair(pair, final):
                for b in range(B):
                    steps(pair, b, pair if b < B - 1 else pair + 1, (b + 1) % B, final and b == B - 1)
            before()
            head_pair(0, False)
            with eng.Fori(1, PAIRS - 1) as pair:
                head_pair(pair, False)
            head_pair(PAIRS - 1, True)

        def w_sync(sp, m, F):
            for b in range(B):
                sp.dma_start(c_mu[:, b * QT:(b + 1) * QT, :],
                             mask[b, :, W0:S2].rearrange("(i p) s -> p i s", p=P)).then_inc(F["mask_in"], 16)
            sp.dma_start(m["wr"][:, :, :], l1_wp[0]).then_inc(F["w_in"], 16)
            for b in range(B):
                wait_past(sp, F["ctx_lo"], b)
                sp.dma_start(c_cr[:, :, :], ctxT[b, :, W0:S2].rearrange("(k p) s -> p k s", p=P)
                             ).then_inc(F["ctx_in"], 16)
            with sp.Fori(1, PAIRS) as pair:
                sp.wait_ge(F["w_lo"], pair * 2)
                sp.dma_start(m["wr"][:, :, :], l1_wp[pair]).then_inc(F["w_in"], 16)

        def w_pe(pe, m, F):
            def queries_and_keys(pair, b):
                u = pair * B + b
                if b == 0:
                    pe.wait_ge(F["w_lo"], pair * 2 + 1)
                if isinstance(u, int) and u < B:
                    pe.wait_ge(F["ctx_lo"], u + 1)
                wait_past(pe, F["x"], (u - 1) * 2)
                for k in range(KD):
                    last = split_matmul(pe, PS[:, 4, :], [w[:, WQ + k, :] for w in m["w"]],
                                        [z[:, k, b * S:(b + 1) * S] for z in ZT], k == 0, k == KD - 1)
                last.then_inc(F["q"], 1)
                for k in range(KD):
                    last = split_matmul(pe, PS[:, 5, 0:WIN], [w[:, WK + k, :] for w in m["w"]],
                                        [c[:, b, k, :] for c in c_c], k == 0, k == KD - 1)
                last.then_inc(F["k"], 1)

            def values(pair, b):
                u = pair * B + b
                wait_past(pe, F["v_out"], u)
                for t, (k0, kw) in enumerate(m["kt"]):
                    for k in range(KD):
                        last = split_matmul(pe, PS[0:kw, 6, t * P:(t + 1) * P], [c[:, b, k, k0:k0 + kw] for c in c_c],
                                            [w[:, WV + k, :] for w in m["w"]], k == 0, k == KD - 1)
                last.then_inc(F["v"], 1)

            def scores(u, n):
                h, i = n // QT, n % QT
                wait_past(pe, F["min"], u * NS + n - 1)
                if n == 0:
                    pe.wait_ge(F["q_lo"], u + 1)
                    pe.wait_ge(F["k_lo"], u + 1)
                split_matmul(pe, PS[:, n % 2, 0:WIN], [q[h * DH:(h + 1) * DH, i * P:(i + 1) * P] for q in m["q"]],
                             [k[h * DH:(h + 1) * DH, :] for k in m["k"]]).then_inc(F["s"], 1)

            def turn(u, n):
                pe.wait_ge(F["norm"], u * NS + n + 1)
                wait_past(pe, F["t_out_act"], u * NS + n - 1)
                for t, (k0, kw) in enumerate(m["kt"]):
                    last = pe.transpose(PS[0:kw, 2 + n % 2, t * P:(t + 1) * P], m["pr"][n % 4][:, k0:k0 + kw], ident[:, :])
                last.then_inc(F["t"], 1)

            def attend(u):
                pe.wait_ge(F["t_out_act"], u * NS + NS)
                pe.wait_ge(F["v_out"], u + 1)
                wait_past(pe, F["u_lo"], u)
                for t, (k0, kw) in enumerate(m["kt"]):
                    for h in range(2):
                        last = pe.matmul(PS[h * DH:(h + 1) * DH, 7, :], m["v"][0:kw, t, h * DH:(h + 1) * DH],
                                         m["pt"][0:kw, h, t, :], start=t == 0, stop=t == len(m["kt"]) - 1,
                                         skip_group_check=True)
                last.then_inc(F["u"], 1)

            def project(u):
                pe.wait_ge(F["u_lo"], u + 1)
                wo = [w[:, WO:WO + 2, :].rearrange("p a n -> p (a n)") for w in m["w"]]
                for i in range(QT):
                    last = split_matmul(pe, PS[:, 4 + i // 2, (i % 2) * D:(i % 2 + 1) * D],
                                        [a[:, i * P:(i + 1) * P] for a in m["u"]], wo)
                last.then_inc(F["y"], 1)

            def before():
                wait_blocks(pe, 2)
                queries_and_keys(0, 0)
                values(0, 0)
                for n in range(AHEAD):
                    scores(0, n)

            def steps(pair, b, pair2, b2, final):
                u = pair * B + b
                for n in range(NS):
                    if n + AHEAD < NS:
                        scores(u, n + AHEAD)
                    turn(u, n)
                    if n + AHEAD == NS - 1 and not final:
                        queries_and_keys(pair2, b2)
                if not final:
                    for n in range(AHEAD):
                        scores(u + 1, n)
                attend(u)
                if not final:
                    values(pair2, b2)
                if b == 0:
                    pe.wait_ge(F["w_lo"], pair * 2 + 2)
                project(u)
            window_units(pe, steps, before)

        def w_act(act, m, F):
            def high_weights(pair):
                act.wait_ge(F["w_in"], pair * 16 + 16)
                wait_past(act, F["v"], pair * B)
                act.activation(m["w"][0][:, 0:WO, :], m["wr"][:, 0:WO, :], ACT.Copy).then_inc(F["w_hi"], 1)

            def high_output(pair):
                wait_past(act, F["y"], pair * B)
                act.activation(m["w"][0][:, WO:, :], m["wr"][:, WO:, :], ACT.Copy).then_inc(F["w_hi"], 1)

            def high_queries_and_keys(u):
                act.wait_ge(F["q"], u + 1)
                wait_past(act, F["s"], u * NS)
                act.activation(m["q"][0][:, :], PS[:, 4, :], ACT.Copy, scale=-DH ** -0.5).then_inc(F["q_hi"], 1)
                act.wait_ge(F["k"], u + 1)
                act.activation(m["k"][0][:, :], PS[:, 5, 0:WIN], ACT.Copy).then_inc(F["k_hi"], 1)

            def exponentials(u, n):
                act.wait_ge(F["min"], u * NS + n + 1)
                wait_past(act, F["t"], u * NS + n - 3)
                act.activation(m["pr"][n % 4][:, :], m["sm"][n % 2][:, :], ACT.Exp, bias=m["mn"][:, n:n + 1],
                               scale=-1.0, accum_out=m["l"][:, n:n + 1]).then_inc(F["exp"], 1)

            def turned(u, n):
                act.wait_ge(F["t"], u * NS + n + 1)
                if n == 0:
                    wait_past(act, F["u"], u)
                act.activation(m["pt"][0:WIN // 4, n // QT, :, (n % QT) * P:(n % QT + 1) * P],
                               PS[0:WIN // 4, 2 + n % 2, :].rearrange("p (t q) -> p t q", q=P), ACT.Copy
                               ).then_inc(F["t_out_act"], 1)

            def before():
                high_weights(0)
                high_output(0)
                for b in range(B):
                    act.wait_ge(F["ctx_in"], 16 * b + 16)
                    act.activation(c_c[0][:, b, :, :], c_cr[:, :, :], ACT.Copy).then_inc(F["ctx_hi"], 1)
                    if b == 0:
                        high_queries_and_keys(0)
                for n in range(AHEAD):
                    exponentials(0, n)

            def steps(pair, b, pair2, b2, final):
                u = pair * B + b
                if b == 0 and not (isinstance(pair, int) and pair == 0):
                    high_output(pair)
                for n in range(AHEAD, NS):
                    exponentials(u, n)
                    turned(u, n - AHEAD)
                    if n == NS - 2 and b == B - 1 and not final:
                        high_weights(pair2)
                if not final:
                    high_queries_and_keys(u + 1)
                for n in range(NS - AHEAD, NS):
                    turned(u, n)
                if not final:
                    for n in range(AHEAD):
                        exponentials(u + 1, n)
                act.wait_ge(F["u"], u + 1)
                wait_past(act, F["y"], u)
                act.activation(m["u"][0][:, :], PS[:, 7, :], ACT.Copy).then_inc(F["u_hi"], 1)
            window_units(act, steps, before)

        def w_pool(pool, m, F):
            for b in range(B):
                pool.wait_ge(F["mask_in"], B * 16)
                pool.tensor_scalar(c_mw[:, b * QT:(b + 1) * QT, :], c_mu[:, b * QT:(b + 1) * QT, :], BIG, None,
                                   ALU.mult).then_inc(F["mask"], 1)

        def w_dve(dve, m, F):
            def low_weights(pair):
                dve.wait_ge(F["w_hi"], pair * 2 + 1)
                dve.tensor_tensor(m["w"][1][:, 0:WO, :], m["wr"][:, 0:WO, :], m["w"][0][:, 0:WO, :].bitcast(F32),
                                  ALU.subtract).then_inc(F["w_lo"], 1)

            def low_output(pair):
                dve.wait_ge(F["w_hi"], pair * 2 + 2)
                dve.tensor_tensor(m["w"][1][:, WO:, :], m["wr"][:, WO:, :], m["w"][0][:, WO:, :].bitcast(F32),
                                  ALU.subtract).then_inc(F["w_lo"], 1)

            def low_queries_and_keys(u):
                dve.wait_ge(F["q_hi"], u + 1)
                dve.scalar_tensor_tensor(m["q"][1][:, :], PS[:, 4, :], -DH ** -0.5, m["q"][0][:, :].bitcast(F32),
                                         ALU.mult, ALU.subtract).then_inc(F["q_lo"], 1)
                dve.wait_ge(F["k_hi"], u + 1)
                dve.tensor_tensor(m["k"][1][:, :], PS[:, 5, 0:WIN], m["k"][0][:, :].bitcast(F32),
                                  ALU.subtract).then_inc(F["k_lo"], 1)

            def values_out(u):
                dve.wait_ge(F["v"], u + 1)
                wait_past(dve, F["u"], u)
                dve.tensor_copy(m["v"][0:WIN // 4, :, :],
                                PS[0:WIN // 4, 6, :].rearrange("p (t n) -> p t n", n=P)).then_inc(F["v_out"], 1)

            def masked(u, b, n):
                dve.wait_ge(F["s"], u * NS + n + 1)
                wait_past(dve, F["exp"], u * NS + n - 1)
                settle(dve)
                dve.tensor_tensor_reduce(m["sm"][n % 2][:, :], PS[:, n % 2, 0:WIN], c_mw[:, b * QT + n % QT, :], 1.0,
                                         BIG, ALU.add, ALU.min, m["mn"][:, n:n + 1]).then_inc(F["min"], 1)

            def normalised(u, n):
                dve.wait_ge(F["exp"], u * NS + n + 1)
                dve.reciprocal(m["rl"][:, n:n + 1], m["l"][:, n:n + 1]).then_inc(F["rl"], 1)
                dve.wait_ge(F["rl"], u * NS + n + 1)
                p = m["pr"][n % 4]
                dve.tensor_scalar(p[:, :], p[:, :], m["rl"][:, n:n + 1], None, ALU.mult).then_inc(F["norm"], 1)

            def first_probabilities(u, b):
                masked(u, b, 0)
                for n in range(AHEAD):
                    if n + 1 < AHEAD:
                        masked(u, b, n + 1)
                    normalised(u, n)

            def before():
                low_weights(0)
                low_output(0)
                for b in range(B):
                    dve.wait_ge(F["ctx_hi"], b + 1)
                    dve.tensor_tensor(c_c[1][:, b, :, :], c_cr[:, :, :], c_c[0][:, b, :, :].bitcast(F32),
                                      ALU.subtract).then_inc(F["ctx_lo"], 1)
                    if b == 0:
                        low_queries_and_keys(0)
                values_out(0)
                dve.wait_ge(F["mask"], B)
                dve.wait_ge(bo_added, B)
                first_probabilities(0, 0)

            def steps(pair, b, pair2, b2, final):
                u = pair * B + b
                if b == 0 and not (isinstance(pair, int) and pair == 0):
                    low_output(pair)
                masked(u, b, AHEAD)
                for n in range(AHEAD, NS):
                    if n + 1 < NS:
                        masked(u, b, n + 1)
                    normalised(u, n)
                    if n == NS - 1 and b == B - 1 and not final:
                        low_weights(pair2)
                if not final:
                    low_queries_and_keys(u + 1)
                    first_probabilities(u + 1, b2)
                dve.wait_ge(F["u_hi"], u + 1)
                dve.tensor_tensor(m["u"][1][:, :], PS[:, 7, :], m["u"][0][:, :].bitcast(F32),
                                  ALU.subtract).then_inc(F["u_lo"], 1)
                if not final:
                    values_out(u + 1)
                dve.wait_ge(F["y"], u + 1)
                for h in range(2):
                    xs = X[:, b * QT + 2 * h:b * QT + 2 * h + 2, :]
                    dve.tensor_tensor(xs, PS[:, 4 + h, :].rearrange("p (t d) -> p t d", t=2), xs,
                                      ALU.add).then_inc(F["x"], 1)
            window_units(dve, steps, before)
            dve.wait_ge(F["x"], UNITS * 2)
            dve.memset(fl_s[:, 0:1], 0.0).then_inc(attn_done, 1)

        def both_paths(eng, window, general):
            eng.wait_ge(flag_ready, 1)
            path = eng.value_load(flag[0:1, 0:1], min_val=0, max_val=1)
            with eng.If(path == 0):
                window(eng, memF, CF)
            with eng.Else():
                general(eng, memG, CG)

        block = ctx_all.enter_context(nc.Block())

        @block.sync
        def _(sp):
            for b in range(B):
                sp.dma_start(X[:, b * QT:(b + 1) * QT, :], x[b].rearrange("(i p) d -> p i d", p=P)).then_inc(x_in, 16)
            sp.dma_start(C[:, :], cols).then_inc(const_in, 16)
            sp.dma_start(R[:, :], rows.partition_broadcast(P)).then_inc(const_in, 16)
            a_weights_sync(sp)
            a_sync(sp)
            sp.wait_ge(A["o_lo"], B * KD)
            ffn_sync(sp, M, memM, 2, l0_w1, l0_w2)
            sp.wait_ge(x_done[0], 2 * B * 2)
            b_sync(sp)
            sp.wait_ge(x_done[1], E0 * B * QT)
            both_paths(sp, w_sync, c_sync)
            sp.wait_ge(attn_done, 1)
            d_sync(sp)
            sp.wait_ge(x_done[3], (G1 + GS) * B * 2)
            for b in range(B):
                sp.dma_start(out[b].rearrange("(i p) d -> p i d", p=P), X[:, b * QT:(b + 1) * QT, :]).then_inc(x_in, 16)
            sp.wait_ge(x_in, 2 * B * 16)

        @block.gpsimd
        def _(pool):
            pool.memset(halfneg[:, :], -0.5).then_inc(ident_ready, 1)
            pool.memset(ident[:, :], 0.0).then_inc(ident_ready, 1)
            pool.wait_ge(ident_ready, 2)
            pool.affine_select(out=ident[:, :], in_=ident[:, :], compare_op=ALU.not_equal, fill=1.0, base=0,
                               pattern=[[-1, P]], channel_multiplier=1).then_inc(ident_ready, 1)
            ln_pool(pool, 0)
            a_pool(pool)
            pool.wait_ge(A["o_lo"], B * KD)
            pool.wait_ge(const_in, 32)
            m_pool(pool)
            pool.wait_ge(x_done[0], 2 * B * 2)
            b_route_pool(pool)
            ln_pool(pool, 1, rms=True)
            b_pool(pool)
            pool.wait_ge(x_done[1], E0 * B * QT)
            ln_pool(pool, 2)
            pool.wait_ge(LN["z"], NT * 3)
            for b in range(B):
                pool.tensor_tensor(X[:, b * QT:(b + 1) * QT, :], X[:, b * QT:(b + 1) * QT, :],
                                   row("bo").unsqueeze(1).to_broadcast([P, QT, D]), ALU.add).then_inc(bo_added, 1)
            both_paths(pool, w_pool, c_pool)
            pool.wait_ge(attn_done, 1)
            d_route_pool(pool)
            ln_pool(pool, 3)
            d_pool(pool)

        @block.scalar
        def _(act):
            ln_act(act, 0, after=lambda b: a_queries_act(act, b))
            a_act(act)
            act.wait_ge(A["o_lo"], B * KD)
            m_act(act)
            act.wait_ge(x_done[0], 2 * B * 2)
            ln_act(act, 1)
            b_route_act(act)
            b_act(act)
            act.wait_ge(x_done[1], E0 * B * QT)
            ln_act(act, 2)
            both_paths(act, w_act, c_act)
            act.wait_ge(attn_done, 1)
            ln_act(act, 3)
            d_route_act(act)
            d_act(act)

        @block.vector
        def _(dve):
            dve.wait_ge(x_in, B * 16)
            ln_dve(dve, 0, after=lambda b: a_queries_dve(dve, b))
            a_dve(dve)
            dve.wait_ge(flag_red, 2 * NT)
            dve.tensor_reduce(fl_s[:, 0:1], fl_a[:, :], AX.X, ALU.min).then_inc(flag_sum, 1)
            dve.tensor_reduce(fl_s[:, 1:2], fl_b[:, :], AX.X, ALU.max).then_inc(flag_sum, 1)
            dve.wait_ge(flag_sum, 2)
            dve.tensor_tensor(fl_a[:, 0:1], fl_s[:, 1:2], fl_s[:, 0:1], ALU.subtract).then_inc(flag_sum, 1)
            dve.wait_ge(flag_sum, 3)
            dve.tensor_scalar(fl_b[:, 0:1], fl_a[:, 0:1], 1.0, None, ALU.add).then_inc(flag_sum, 1)
            dve.memset(fl_b[:, 1:2], 1.0).then_inc(flag_sum, 1)
            dve.wait_ge(flag_sum, 6)
            dve.tensor_scalar(flag[0:1, :], PS[0:1, 3, 0:1], 1.0, None, ALU.min).then_inc(flag_ready, 1)
            m_dve(dve)
            dve.wait_ge(x_done[0], 2 * B * 2)
            ln_dve(dve, 1, rms=True)
            b_route_dve(dve)
            b_dve(dve)
            dve.wait_ge(x_done[1], E0 * B * QT)
            ln_dve(dve, 2)
            both_paths(dve, w_dve, c_dve)
            ln_dve(dve, 3)
            d_route_dve(dve)
            d_dve(dve)

        @block.tensor
        def _(pe):
            pe.wait_ge(ident_ready, 3)
            ln_pe(pe, 0, after=lambda b: a_queries_pe(pe, b))
            a_pe(pe)
            pe.wait_ge(flag_sum, 5)
            pe.matmul(PS[0:1, 3, 0:1], fl_b[:, 0:1], fl_b[:, 1:2], start=True, stop=True).then_inc(flag_sum, 1)
            pe.wait_ge(flag_ready, 1)
            pe.wait_ge(A["o_lo"], B * KD)
            ffn_pe(pe, M, memM, 2, 4, x_done[0], 2,
                   lambda u, m: wait_past(pe, M["act"], (u - 1) * 4 + m + 1))
            pe.wait_ge(x_done[0], 2 * B * 2)
            ln_pe(pe, 1, rms=True)
            b_route_pe(pe)
            ffn_pe(pe, BM, memB, E0, 2, x_done[1], QT,
                   lambda u, m: wait_past(pe, BM["glu" if m < 2 else "lin"], (u - 1) * 2 + m % 2 + 1))
            pe.wait_ge(x_done[1], E0 * B * QT)
            ln_pe(pe, 2)
            both_paths(pe, w_pe, c_pe)
            pe.wait_ge(attn_done, 1)
            ln_pe(pe, 3)
            d_route_pe(pe)
            ffn_pe(pe, DM, memD, G1 + GS, 4, x_done[3], 2,
                   lambda u, m: wait_past(pe, DM["act"], (u - 1) * 4 + m + 1))


def kernel(**inp):
    import numpy as np
    import concourse.bacc as bacc
    from concourse.bass_utils import run_bass_kernel_spmd as run

    a = {k: np.asarray(v) for k, v in inp.items()}

    def tall(v):
        return v.reshape(-1, P).T

    def one_column(v):
        c = np.zeros((P, 1), v.dtype)
        c[:len(v), 0] = v
        return c

    wkv, bkv = a["L0_xattn_W_kv"], a["L0_xattn_b_kv"]
    mlp1 = np.concatenate([a["L0_ffn_mlp1_w"][:, 0::2], a["L0_ffn_mlp1_w"][:, 1::2]], axis=1).transpose(0, 2, 1)
    mlp1_b = np.concatenate([a["L0_ffn_mlp1_b"][:, 0::2], a["L0_ffn_mlp1_b"][:, 1::2]], axis=1)
    l1_b1 = np.concatenate([a["L1_ffn_b1"].reshape(-1), a["L1_ffn_sb1"].reshape(-1)])
    cols = np.concatenate([tall(a["L0_xattn_b_q"]), tall(bkv[:D]), tall(bkv[D:]), tall(a["L0_xattn_b1"]),
                           tall(mlp1_b.reshape(-1)), tall(l1_b1), one_column(a["L0_ffn_gate_b"]),
                           one_column(a["L1_ffn_router_b"])], axis=1)
    rows = np.concatenate([a["L0_xattn_b2"], a["L0_ffn_norm_w"], a["L1_xattn_bo"]])

    def pair_cols(w):
        return w.reshape(KD, P, PAIRS, P).transpose(2, 1, 0, 3)

    l1_wp = np.concatenate([pair_cols(a["L1_xattn_Wq"]), pair_cols(a["L1_xattn_Wk"]), pair_cols(a["L1_xattn_Wv"]),
                            a["L1_xattn_Wo"].reshape(PAIRS, P, 2, P)], axis=2)
    l1_w1 = np.concatenate([a["L1_ffn_w1"].reshape(G1, 8, D, H1).transpose(0, 2, 1, 3).reshape(G1, D, 512),
                            a["L1_ffn_sw1"]], axis=0)
    l1_w2 = np.concatenate([a["L1_ffn_w2"].reshape(G1, 512, D), a["L1_ffn_sw2"]], axis=0)
    arrays = {
        "x": a["x"], "ctxT": a["ctx_1024"].transpose(0, 2, 1), "ctx": a["ctx_1024"],
        "mask": a["mask_BxSxS2_bk1"], "cols": cols, "rows": rows,
        "l0_wq": a["L0_xattn_W_q"], "l0_wkT": wkv[:, :D].T, "l0_wv": wkv[:, D:],
        "l0_w1": a["L0_xattn_W1"].reshape(D, 2, 512).transpose(1, 0, 2), "l0_w2": a["L0_xattn_W2"].reshape(2, 512, D),
        "gate_wT": a["L0_ffn_gate_w"].T, "mlp1": mlp1, "mlp2": a["L0_ffn_mlp2_w"].transpose(0, 2, 1),
        "mlp2_b": a["L0_ffn_mlp2_b"], "l1_wp": l1_wp, "router_w": a["L1_ffn_router_w"], "l1_w1": l1_w1,
        "l1_w2": l1_w2, "l1_b2": np.concatenate([a["L1_ffn_b2"], a["L1_ffn_sb2"]], axis=0),
    }
    arrays = {k: np.ascontiguousarray(v) for k, v in arrays.items()}
    nc = bacc.Bacc("TRN2", target_bir_lowering=False, num_devices=1)
    args = {k: nc.dram_tensor(k, v.shape, mybir.dt.from_np(v.dtype), kind="ExternalInput").ap()
            for k, v in arrays.items()}
    args["out"] = nc.dram_tensor("out", (B, S, D), F32, kind="ExternalOutput").ap()
    build_program(nc, **args)
    r = run(nc, [arrays], core_ids=[0])
    return r.results[0]["out"]
```
